# Optimizing a Trainium2 kernel written in Bass

```python
import numpy as np
import jax
import jax.numpy as jnp

def _softmax(x, axis=-1):
    return jax.nn.softmax(x, axis=axis)

def _gelu(x):
    return jax.nn.gelu(x, approximate=True)

def _silu(x):
    return jax.nn.silu(x)

def _sigmoid(x):
    return jax.nn.sigmoid(x)

def _layernorm(x, axis=-1, eps=1e-05):
    m = jnp.mean(x, axis=axis, keepdims=True)
    v = jnp.var(x, axis=axis, keepdims=True)
    return (x - m) / jnp.sqrt(v + eps)

def _scatter_add(tgt, idx, src, axis=0):
    return tgt.at[idx].add(src)

def _segment_sum(src, seg, n):
    return jax.ops.segment_sum(src, seg, n)
kernel_name = 'mk_gnn_ffn_d2_gnn_r32_28da9c'

def setup_inputs(seed: int=0):
    np.random.seed(seed)
    _w = jnp.asarray

    def _rec_inputs():
        import jax
        import jax.numpy as jnp
        _gk = jax.random.key(seed)
        x = -0.0002928 + 1 * jax.random.normal(jax.random.fold_in(_gk, 1), (256, 512), jnp.float32)
        _s = jax.random.randint(jax.random.fold_in(_gk, 2), (2048,), 0, 256, jnp.int32)
        _d = jax.random.randint(jax.random.fold_in(_gk, 3), (2048,), 0, 256, jnp.int32)
        _loop = jnp.arange(256, dtype=jnp.int32)
        src = jnp.concatenate([_s, _d, _loop])
        dst = jnp.concatenate([_d, _s, _loop])
        _o = jnp.argsort(dst, stable=True)
        src = src[_o]
        dst = dst[_o]
        edge_attr_128 = 0.000283511 + 1.00007 * jax.random.normal(jax.random.fold_in(_gk, 11), (4352, 128), jnp.float32)
        return (x, src, dst, edge_attr_128)
    x, src, dst, edge_attr_128 = _rec_inputs()

    def _L0_gnn_setup():
        import jax, jax.numpy as jnp
        import numpy as np
        N = 256
        D = 512
        E = 8192
        STEPS = 3
        key = jax.random.key(seed)
        k1, k2, k3 = jax.random.split(key, 3)
        x = jax.random.normal(k1, (N, D), dtype=jnp.float32)
        edge_index = jax.random.randint(k2, (2, E), 0, N, dtype=jnp.int32)
        W = jax.random.normal(k3, (D, D), dtype=jnp.float32) / np.sqrt(D)
        b = jnp.zeros((D,), dtype=jnp.float32)
        diffusion_weights = jnp.ones((STEPS + 1,), dtype=jnp.float32) / (STEPS + 1)
        return {'x': x, 'edge_index': edge_index, 'W': W, 'b': b, 'diffusion_weights': diffusion_weights}
    _L0_gnn_all = _L0_gnn_setup()
    _L0_gnn_in = {k: v for k, v in _L0_gnn_all.items() if k in ('W', 'b', 'diffusion_weights')}
    del _L0_gnn_all

    def _L0_ffn_setup():
        import jax, jax.numpy as jnp
        import numpy as np
        E = 8
        TOP_K = 2
        D = 512
        H = 1024
        B, S = (16, 128)
        key = jax.random.key(seed)
        ks = jax.random.split(key, 10)
        sd = lambda fan_in: 1.0 / np.sqrt(fan_in)
        x = jax.random.normal(ks[0], (B, S, D), dtype=jnp.float32)
        gw1 = jax.random.uniform(ks[1], (D, D // 2), jnp.float32, -sd(D), sd(D))
        gb1 = jnp.zeros((D // 2,), jnp.float32)
        gw2 = jax.random.uniform(ks[2], (D // 2, E), jnp.float32, -sd(D // 2), sd(D // 2))
        gb2 = jnp.zeros((E,), jnp.float32)
        we1 = jax.random.uniform(ks[3], (E, D, H), jnp.float32, -sd(D), sd(D))
        be1 = jnp.zeros((E, H), jnp.float32)
        we2 = jax.random.uniform(ks[4], (E, H, D), jnp.float32, -sd(H), sd(H))
        be2 = jnp.zeros((E, D), jnp.float32)
        return {'x': x, 'gw1': gw1, 'gb1': gb1, 'gw2': gw2, 'gb2': gb2, 'we1': we1, 'be1': be1, 'we2': we2, 'be2': be2}
    _L0_ffn_all = _L0_ffn_setup()
    _L0_ffn_in = {k: v for k, v in _L0_ffn_all.items() if k in ('gw1', 'gb1', 'gw2', 'gb2', 'we1', 'be1', 'we2', 'be2')}
    del _L0_ffn_all

    def _L1_gnn_setup():
        import jax, jax.numpy as jnp
        import numpy as np
        N, E = (10000, 150000)
        HD, ED = (512, 128)
        BN_EPS = 1e-05
        key = jax.random.key(seed)
        ks = jax.random.split(key, 16)
        s = 0.02
        return {'h': jax.random.normal(ks[0], (N, HD), jnp.float32), 'edge_index': jax.random.randint(ks[1], (2, E), 0, N, jnp.int32), 'edge_attr': jax.random.normal(ks[2], (E, ED), jnp.float32), 'W1': jax.random.normal(ks[3], (HD, HD + ED), jnp.float32) * s, 'b1': jnp.zeros((HD,), jnp.float32), 'W2': jax.random.normal(ks[4], (HD, HD), jnp.float32) * s, 'b2': jnp.zeros((HD,), jnp.float32), 'W_ih': jax.random.normal(ks[5], (3 * HD, HD), jnp.float32) * s, 'W_hh': jax.random.normal(ks[6], (3 * HD, HD), jnp.float32) * s, 'b_ih': jnp.zeros((3 * HD,), jnp.float32), 'b_hh': jnp.zeros((3 * HD,), jnp.float32), 'gamma': jnp.ones((HD,), jnp.float32), 'beta': jnp.zeros((HD,), jnp.float32), 'run_mean': jnp.zeros((HD,), jnp.float32), 'run_var': jnp.ones((HD,), jnp.float32)}
    _L1_gnn_all = _L1_gnn_setup()
    _L1_gnn_in = {k: v for k, v in _L1_gnn_all.items() if k in ('W1', 'b1', 'W2', 'b2', 'W_ih', 'W_hh', 'b_ih', 'b_hh', 'gamma', 'beta', 'run_mean', 'run_var')}
    del _L1_gnn_all

    def _L1_ffn_setup():
        import jax, jax.numpy as jnp
        import numpy as np
        S, B, I, O, H, E, K = (128, 32, 512, 512, 512, 8, 2)

        def _expert(x_seq, Wi, Wh, b, Wo, bo):
            Bsz = x_seq.shape[1]
            Hd = Wh.shape[0]

            def step(carry, xt):
                h, c = carry
                gates = xt @ Wi + h @ Wh + b
                i_, f_, g_, o_ = jnp.split(gates, 4, axis=-1)
                c = jax.nn.sigmoid(f_) * c + jax.nn.sigmoid(i_) * jnp.tanh(g_)
                h = jax.nn.sigmoid(o_) * jnp.tanh(c)
                return ((h, c), h @ Wo + bo)
            init = (jnp.zeros((Bsz, Hd), x_seq.dtype), jnp.zeros((Bsz, Hd), x_seq.dtype))
            _, ys = jax.lax.scan(step, init, x_seq)
            return ys
        key = jax.random.key(seed)
        ks = jax.random.split(key, 6)
        s = 0.02
        return {'x': jax.random.normal(ks[0], (S, B, I), dtype=jnp.float32), 'router_w': jax.random.normal(ks[1], (I, E), dtype=jnp.float32) * s, 'router_b': jnp.zeros((E,), dtype=jnp.float32), 'Wi': jax.random.normal(ks[2], (E, I, 4 * H), dtype=jnp.float32) * s, 'Wh': jax.random.normal(ks[3], (E, H, 4 * H), dtype=jnp.float32) * s, 'b': jnp.zeros((E, 4 * H), dtype=jnp.float32), 'Wo': jax.random.normal(ks[4], (E, H, O), dtype=jnp.float32) * s, 'bo': jnp.zeros((E, O), dtype=jnp.float32)}
    _L1_ffn_all = _L1_ffn_setup()
    _L1_ffn_in = {k: v for k, v in _L1_ffn_all.items() if k in ('router_w', 'router_b', 'Wi', 'Wh', 'b', 'Wo', 'bo')}
    del _L1_ffn_all
    return {'x': x, 'src': src, 'dst': dst, 'edge_attr_128': edge_attr_128, 'L0_gnn_W': _L0_gnn_in['W'], 'L0_gnn_b': _L0_gnn_in['b'], 'L0_gnn_diffusion_weights': _L0_gnn_in['diffusion_weights'], 'L0_ffn_gw1': _L0_ffn_in['gw1'], 'L0_ffn_gb1': _L0_ffn_in['gb1'], 'L0_ffn_gw2': _L0_ffn_in['gw2'], 'L0_ffn_gb2': _L0_ffn_in['gb2'], 'L0_ffn_we1': _L0_ffn_in['we1'], 'L0_ffn_be1': _L0_ffn_in['be1'], 'L0_ffn_we2': _L0_ffn_in['we2'], 'L0_ffn_be2': _L0_ffn_in['be2'], 'L1_gnn_W1': _L1_gnn_in['W1'], 'L1_gnn_b1': _L1_gnn_in['b1'], 'L1_gnn_W2': _L1_gnn_in['W2'], 'L1_gnn_b2': _L1_gnn_in['b2'], 'L1_gnn_W_ih': _L1_gnn_in['W_ih'], 'L1_gnn_W_hh': _L1_gnn_in['W_hh'], 'L1_gnn_b_ih': _L1_gnn_in['b_ih'], 'L1_gnn_b_hh': _L1_gnn_in['b_hh'], 'L1_gnn_gamma': _L1_gnn_in['gamma'], 'L1_gnn_beta': _L1_gnn_in['beta'], 'L1_gnn_run_mean': _L1_gnn_in['run_mean'], 'L1_gnn_run_var': _L1_gnn_in['run_var'], 'L1_ffn_router_w': _L1_ffn_in['router_w'], 'L1_ffn_router_b': _L1_ffn_in['router_b'], 'L1_ffn_Wi': _L1_ffn_in['Wi'], 'L1_ffn_Wh': _L1_ffn_in['Wh'], 'L1_ffn_b': _L1_ffn_in['b'], 'L1_ffn_Wo': _L1_ffn_in['Wo'], 'L1_ffn_bo': _L1_ffn_in['bo']}

def reference(x, src, dst, edge_attr_128, L0_gnn_W, L0_gnn_b, L0_gnn_diffusion_weights, L0_ffn_gw1, L0_ffn_gb1, L0_ffn_gw2, L0_ffn_gb2, L0_ffn_we1, L0_ffn_be1, L0_ffn_we2, L0_ffn_be2, L1_gnn_W1, L1_gnn_b1, L1_gnn_W2, L1_gnn_b2, L1_gnn_W_ih, L1_gnn_W_hh, L1_gnn_b_ih, L1_gnn_b_hh, L1_gnn_gamma, L1_gnn_beta, L1_gnn_run_mean, L1_gnn_run_var, L1_ffn_router_w, L1_ffn_router_b, L1_ffn_Wi, L1_ffn_Wh, L1_ffn_b, L1_ffn_Wo, L1_ffn_bo):
    import jax
    import jax.numpy as jnp

    def _L0_gnn_ref(x, edge_index, W, b, diffusion_weights):
        import jax, jax.numpy as jnp
        import numpy as np
        N = 256
        D = 512
        E = 8192
        STEPS = 3
        h = x @ W + b
        row, col = (edge_index[0], edge_index[1])
        adj = jnp.zeros((N, N), dtype=h.dtype)
        adj = adj.at[row, col].set(1.0)
        adj = adj.at[col, row].set(1.0)
        adj = adj + jnp.eye(N, dtype=h.dtype)
        row_sum = adj.sum(axis=1, keepdims=True)
        adj = adj / jnp.maximum(row_sum, 1.0)
        out = diffusion_weights[0] * h
        cur = h
        for i in range(STEPS):
            cur = adj @ cur
            out = out + diffusion_weights[i + 1] * cur
        return jax.nn.relu(out)

    def _L0_ffn_ref(x, gw1, gb1, gw2, gb2, we1, be1, we2, be2):
        import jax, jax.numpy as jnp
        import numpy as np
        E = 8
        TOP_K = 2
        D = 512
        H = 1024
        B, S = (16, 128)
        b, s, d = x.shape
        xf = x.reshape(-1, d)
        T = xf.shape[0]
        gate_logits = jax.nn.relu(xf @ gw1 + gb1) @ gw2 + gb2
        gate_weights = jax.nn.softmax(gate_logits, axis=-1)
        top_w, top_idx = jax.lax.top_k(gate_weights, TOP_K)
        top_w = jax.nn.softmax(top_w, axis=-1)
        combine = jnp.zeros((T, E), dtype=xf.dtype)
        combine = combine.at[jnp.arange(T)[:, None], top_idx].add(top_w)
        out = jnp.zeros_like(xf)
        for e in range(E):
            h = jax.nn.gelu(xf @ we1[e] + be1[e], approximate=False)
            y = h @ we2[e] + be2[e]
            out = out + combine[:, e:e + 1] * y
        return out.reshape(b, s, d)

    def _L1_gnn_ref(h, edge_index, edge_attr, W1, b1, W2, b2, W_ih, W_hh, b_ih, b_hh, gamma, beta, run_mean, run_var):
        import jax, jax.numpy as jnp
        import numpy as np
        N, E = (10000, 150000)
        HD, ED = (512, 128)
        BN_EPS = 1e-05
        src, dst = (edge_index[0], edge_index[1])
        m_in = jnp.concatenate([h[src], edge_attr], axis=1)
        m = jax.nn.relu(m_in @ W1.T + b1) @ W2.T + b2
        agg = jax.ops.segment_sum(m, dst, num_segments=h.shape[0])
        gi = agg @ W_ih.T + b_ih
        gh = h @ W_hh.T + b_hh
        i_r, i_z, i_n = jnp.split(gi, 3, axis=1)
        h_r, h_z, h_n = jnp.split(gh, 3, axis=1)
        r = jax.nn.sigmoid(i_r + h_r)
        z = jax.nn.sigmoid(i_z + h_z)
        n = jnp.tanh(i_n + r * h_n)
        h_new = (1.0 - z) * n + z * h
        bn = gamma * (h_new - run_mean) * jax.lax.rsqrt(run_var + BN_EPS) + beta
        return h + bn

    def _L1_ffn_ref(x, router_w, router_b, Wi, Wh, b, Wo, bo):
        import jax, jax.numpy as jnp
        import numpy as np
        S, B, I, O, H, E, K = (128, 32, 512, 512, 512, 8, 2)

        def _expert(x_seq, Wi, Wh, b, Wo, bo):
            Bsz = x_seq.shape[1]
            Hd = Wh.shape[0]

            def step(carry, xt):
                h, c = carry
                gates = xt @ Wi + h @ Wh + b
                i_, f_, g_, o_ = jnp.split(gates, 4, axis=-1)
                c = jax.nn.sigmoid(f_) * c + jax.nn.sigmoid(i_) * jnp.tanh(g_)
                h = jax.nn.sigmoid(o_) * jnp.tanh(c)
                return ((h, c), h @ Wo + bo)
            init = (jnp.zeros((Bsz, Hd), x_seq.dtype), jnp.zeros((Bsz, Hd), x_seq.dtype))
            _, ys = jax.lax.scan(step, init, x_seq)
            return ys
        S_, B_, I_ = x.shape
        N = S_ * B_
        flat_x = x.reshape(N, I_)
        logits = flat_x @ router_w + router_b
        top_vals, top_idx = jax.lax.top_k(logits, K)
        rw = jax.nn.softmax(top_vals, axis=1)
        mask = (top_idx.T[:, None, :] == jnp.arange(E)[None, :, None]).astype(x.dtype)
        expert_x = (mask[..., None] * flat_x[None, None]).reshape(K, E, S_, B_, I_)
        run_e = jax.vmap(_expert, in_axes=(0, 0, 0, 0, 0, 0))
        run_ke = jax.vmap(run_e, in_axes=(0, None, None, None, None, None))
        out = run_ke(expert_x, Wi, Wh, b, Wo, bo)
        out = out.reshape(K, E, N, -1)
        y = jnp.einsum('ken,nk,keno->no', mask, rw, out)
        return y.reshape(S_, B_, -1)
    edge_index = jnp.stack([src, dst])
    x = x + _L0_gnn_ref(_layernorm(x, axis=-1), edge_index, L0_gnn_W, L0_gnn_b, L0_gnn_diffusion_weights)
    x = x + _L0_ffn_ref(_layernorm(x, axis=-1)[None], L0_ffn_gw1, L0_ffn_gb1, L0_ffn_gw2, L0_ffn_gb2, L0_ffn_we1, L0_ffn_be1, L0_ffn_we2, L0_ffn_be2)[0]
    x = x + _L1_gnn_ref(_layernorm(x, axis=-1), edge_index, edge_attr_128, L1_gnn_W1, L1_gnn_b1, L1_gnn_W2, L1_gnn_b2, L1_gnn_W_ih, L1_gnn_W_hh, L1_gnn_b_ih, L1_gnn_b_hh, L1_gnn_gamma, L1_gnn_beta, L1_gnn_run_mean, L1_gnn_run_var)
    x = x + _L1_ffn_ref(_layernorm(x, axis=-1)[None], L1_ffn_router_w, L1_ffn_router_b, L1_ffn_Wi, L1_ffn_Wh, L1_ffn_b, L1_ffn_Wo, L1_ffn_bo)[0]
    return x

_drawn_inputs = setup_inputs


def setup_inputs(seed=0):
    import zlib

    import numpy as np

    out = dict(_drawn_inputs(seed))
    spreads = {'L0_gnn_b': (0.0, 0.1),
     'L0_gnn_diffusion_weights': (0.25, 0.6),
     'L0_ffn_gb1': (0.0, 0.1),
     'L0_ffn_gb2': (0.0, 0.1),
     'L0_ffn_be1': (0.0, 0.328),
     'L0_ffn_be2': (0.0, 0.1),
     'L1_gnn_b1': (0.0, 0.1),
     'L1_gnn_b2': (0.0, 0.1),
     'L1_gnn_b_ih': (0.0, 0.448),
     'L1_gnn_b_hh': (0.0, 0.606),
     'L1_gnn_gamma': (1.0, 0.2),
     'L1_gnn_beta': (0.0, 0.1),
     'L1_gnn_run_mean': (0.0, 0.1),
     'L1_gnn_run_var': (1.0, 0.57),
     'L1_ffn_router_b': (0.0, 0.542),
     'L1_ffn_b': (0.0, 0.8),
     'L1_ffn_bo': (0.0, 0.29)}
    factors = {'L1_ffn_Wi': 4.658, 'L1_ffn_Wo': 4.539}
    for name, (base, spread) in spreads.items():
        noise = np.random.default_rng([zlib.crc32(name.encode()), seed]).standard_normal(out[name].shape)
        drawn = base * np.exp(spread * noise) if base else spread * noise
        out[name] = jnp.asarray(drawn.astype(out[name].dtype))
    for name, factor in factors.items():
        out[name] = (out[name] * factor).astype(out[name].dtype)
    return out
```

```python
import numpy as np
import concourse.bass as bass
from concourse import mybir
from contextlib import ExitStack

P = 128
T = 256
NT = T // P
D = 512
KB = D // P
E = 8
MORE = 2 * T // (P + 1)
EDGES = 4352
ET = EDGES // P
C = 512
EPS = 1e-5
RAW = 4
SPL = 4
GRP = 4
NG = -(-ET // GRP)

FFN_IN, FFN_OUT = 2, 2
LSTM_IN, LSTM_OUT = 3, 1


def moe_order(layer, n_in, n_out):
    order = []
    for step in range(E + 1):
        if step < E:
            order += [(layer, "in", step, c) for c in range(n_in)]
        if step >= 1:
            order += [(layer, "out", step - 1, c) for c in range(n_out)]
    return order


FFN_ORDER = moe_order("ffn", FFN_IN, FFN_OUT)
LSTM_ORDER = moe_order("lstm", LSTM_IN, LSTM_OUT)
EC = FFN_IN + FFN_OUT
GNN_ORDER = [("gnn", "W1")] + [("gnn", "Whh", g) for g in range(3)] + [("gnn", "W2")] \
    + [("gnn", "Wih", g) for g in range(3)]
ORDER = [("L0", "W")] + FFN_ORDER + GNN_ORDER + LSTM_ORDER
CHUNK = {key: n for n, key in enumerate(ORDER)}


def moe_store(layer, n_in):
    return [(layer, "in", e, c) if c < n_in else (layer, "out", e, c - n_in)
            for e in range(E) for c in range(EC)]


STORE = [("L0", "W")] + moe_store("ffn", FFN_IN) + GNN_ORDER + moe_store("lstm", LSTM_IN)
PLACE = {key: n for n, key in enumerate(STORE)}


def build(nc, A, out, node_rows):
    f32, f32r, bf16, i32, u32 = (mybir.dt.float32, mybir.dt.float32r, mybir.dt.bfloat16,
                                 mybir.dt.int32, mybir.dt.uint32)
    ALU = mybir.AluOpType
    ACT = mybir.ActivationFunctionType
    AX = mybir.AxisListType.X

    ctx = ExitStack()
    with ctx:
        def sb(name, shape, dt=f32, stack=ctx):
            return stack.enter_context(nc.sbuf_tensor(name, shape, dt))

        def sem(name):
            return ctx.enter_context(nc.semaphore(name))

        raw = [sb(f"raw{i}", [P, KB, C]) for i in range(RAW)]
        whi = [sb(f"whi{i}", [P, KB, C], f32r) for i in range(SPL)]
        wlo = [sb(f"wlo{i}", [P, KB, C], f32r) for i in range(SPL)]
        x = sb("x", [P, NT, D])
        xn = sb("xn", [P, NT, D])
        xnT = sb("xnT", [P, NT, KB, P])
        iota_t = sb("iota_t", [P, T])
        node_id = sb("node_id", [P, NT])
        eye2 = sb("eye2", [P, NT, T])
        ident = eye2[:, 0, 0:P]
        src_i = sb("src_i", [P, ET], i32)
        dst_i = sb("dst_i", [P, ET], i32)
        dst_f = sb("dst_f", [P, ET])
        deg = sb("deg", [P, NT])
        stats = sb("stats", [P, NT, 6])
        mv = sb("mv", [P, NT, 2])
        rstd = sb("rstd", [P, NT])
        var_eps = sb("var_eps", [P, NT])
        minus_half = sb("minus_half", [P, NT])
        iota_b = sb("iota_b", [P, T], bf16)
        more_i = [sb(f"more_i{i}", [P, 1 + MORE], i32) for i in range(2)]
        rw = sb("rw", [P, KB, E])
        gb = sb("gb", [P, 2, E])

        with ExitStack() as st:
            g0_src_f = sb("g0_src_f", [P, ET], f32, st)
            g0_S = sb("g0_S", [P, 4, T], bf16, st)
            g0_D = sb("g0_D", [P, 4, T], bf16, st)
            g0_cnt = sb("g0_cnt", [P, NT, T], f32, st)
            g0_sum = sb("g0_sum", [P, NT, T], f32, st)
            g0_adj = sb("g0_adj", [P, NT, T], f32r, st)
            g0_rs = sb("g0_rs", [P, NT], f32, st)
            g0_rinv = sb("g0_rinv", [P, NT], f32, st)
            g0_xT_hi = sb("g0_xT_hi", [P, NT, KB, P], f32r, st)
            g0_xT_lo = sb("g0_xT_lo", [P, NT, KB, P], f32r, st)
            g0_h = sb("g0_h", [P, NT, D], f32, st)
            g0_cur = sb("g0_cur", [P, NT, D], f32, st)
            g0_wh = sb("g0_wh", [P, 3, NT, D], f32, st)
            g0_hi = sb("g0_hi", [P, NT, D], f32r, st)
            g0_lo = sb("g0_lo", [P, NT, D], f32r, st)
            g0_b = sb("g0_b", [P, D], f32, st)
            g0_w = sb("g0_w", [P, 4], f32, st)
        with ExitStack() as st:
            xn_hi = sb("xn_hi", [P, NT, D], f32r, st)
            xn_lo = sb("xn_lo", [P, NT, D], f32r, st)
            xe_hi = sb("xe_hi", [P, KB, P], f32r, st)
            xe_lo = sb("xe_lo", [P, KB, P], f32r, st)
            act3 = sb("act3", [P, 3, C], f32, st)
            hT_hi = sb("hT_hi", [P, 2 * KB, P], f32r, st)
            hT_lo = sb("hT_lo", [P, 2 * KB, P], f32r, st)
            y_hi = sb("y_hi", [P, D], f32r, st)
            y_lo = sb("y_lo", [P, D], f32r, st)
            G = sb("G", [P, 2, NT, P], f32r, st)
            GT = sb("GT", [P, 3, T], f32r, st)
            wslot = sb("wslot", [P, 3], f32, st)
            sel_v = sb("sel_v", [2 * E, E, P], f32, st)
            sel_a = sb("sel_a", [2 * E, E, P], f32, st)
            sel = sb("sel", [2 * E, E, P], f32r, st)
            b_hi = sb("b_hi", [2 * E, 3 * C], f32r, st)
            b_rows = sb("b_rows", [2 * E, 3 * C], f32r, st)
            alpha = sb("alpha", [2 * E, 1], f32, st)
            hid = sb("hid", [P, 2, T], f32, st)
            lg = sb("lg", [P, NT, E], f32, st)
            pr = sb("pr", [P, NT, E], f32, st)
            red = sb("red", [P, NT], f32, st)
            red2 = sb("red2", [P, NT], f32, st)
            top = sb("top", [P, NT, 8], f32, st)
            topi = sb("topi", [P, NT, 8], u32, st)
            topf = sb("topf", [P, NT, 8], f32, st)
            tw = sb("tw", [P, NT, 4], f32, st)
            oh = sb("oh", [P, NT, 2, E], f32, st)
            mask = sb("mask", [P, NT, E], f32, st)
            comb = sb("comb", [P, NT, E], f32, st)
            combT = sb("combT", [E, T], f32, st)
            posm = sb("posm", [P, NT, E], f32, st)
            penal = sb("penal", [P, NT, E], f32, st)
            tri = sb("tri", [P, T], f32, st)
            over = sb("over", [P, E], f32, st)
            rank = sb("rank", [P, E], f32, st)
            picked = sb("picked", [P, MORE, E], f32, st)
            prod = sb("prod", [P, 2 * NT, E], f32, st)
            ids = sb("ids", [P, 1 + MORE], f32, st)
            more_pc = sb("more_pc", [P, MORE, 2 * NT], f32, st)
            sel_m = sb("sel_m", [2 * E, 2, P], f32, st)
            sel_more = sb("sel_more", [2 * E, P], f32r, st)
            b_raw = sb("b_raw", [2 * E, 3 * C], f32, st)
            b_out = sb("b_out", [E, D], f32, st)
            gw1 = sb("gw1", [P, KB, 256], f32, st)
            gb1 = sb("gb1", [P, 2], f32, st)
            gw2 = sb("gw2", [P, 2, E], f32, st)
        with ExitStack() as st:
            g1_xT_hi = sb("g1_xT_hi", [P, NT, KB, P], f32r, st)
            g1_xT_lo = sb("g1_xT_lo", [P, NT, KB, P], f32r, st)
            A_sb = sb("A_sb", [P, NT, D], f32, st)
            gh = sb("gh", [P, NT, 3, D], f32, st)
            w1e_hi = sb("w1e_hi", [P, D], f32r, st)
            w1e_lo = sb("w1e_lo", [P, D], f32r, st)
            onehot = sb("onehot", [P, 4, T], f32r, st)
            gb_rows = sb("gb_rows", [4, 3 * D], f32r, st)
            gsel = sb("gsel", [4, 3, P], f32r, st)
            galpha = sb("galpha", [4, 1], f32, st)
            g1_it = sb("g1_it", [4, 3, P], f32, st)
            g1_t = sb("g1_t", [4, 3, P], f32, st)
            with ExitStack() as st2:
                ea = sb("ea", [P, 3, GRP * P], f32, st2)
                ea_hi = sb("ea_hi", [P, 2, GRP * P], f32r, st2)
                ea_lo = sb("ea_lo", [P, 2, GRP * P], f32r, st2)
                gath = sb("gath", [P, 4, D], f32, st2)
                mp = sb("mp", [P, 2, D], f32, st2)
                m_hi = sb("m_hi", [P, 2, D], f32r, st2)
                m_lo = sb("m_lo", [P, 2, D], f32r, st2)
            with ExitStack() as st2:
                pad = sb("pad0", [P, 7, GRP * P], f32, st2)
                gb_raw = sb("gb_raw", [4, 3 * D], f32, st2)
            with ExitStack() as st2:
                S1 = sb("S1", [P, NT, D], f32, st2)
                agg = sb("agg", [P, NT, D], f32, st2)
                aT_hi = sb("aT_hi", [P, NT, KB, P], f32r, st2)
                aT_lo = sb("aT_lo", [P, NT, KB, P], f32r, st2)
                rz = sb("rz", [P, NT, 3, D], f32, st2)
            edge_space = sb("edge_space", [P, 38 * 256], f32, st)
            w1e = sb("w1e", [P, D], f32, st)
            g2s = sb("g2s", [P, D], f32, st)
            g2b = sb("g2b", [P, D], f32, st)
            g2m = sb("g2m", [P, D], f32, st)
            g2v = sb("g2v", [P, D], f32, st)
            b1 = sb("b1", [P, D], f32, st)
            b2 = sb("b2", [P, D], f32, st)

        B = [ctx.enter_context(nc.psum_tensor(f"bank{i}", [P, C], f32)) for i in range(8)]

        def quarters(bank):
            return bank[:, :].rearrange("p (k t) -> p k t", k=KB)

        raw_in = [sem(f"raw_in{i}") for i in range(RAW)]
        hi_cut = sem("hi_cut")
        lo_cut = sem("lo_cut")
        chunk_used = sem("chunk_used")
        layer_done = sem("layer_done")
        x_in, idx_in, par0, par1, par2, par3 = (sem(n) for n in (
            "x_in", "idx_in", "par0", "par1", "par2", "par3"))
        PAR1 = (16 * 9, 16 * 12)
        iota_ok = sem("iota_ok")
        half_ok = sem("half_ok")
        var_ok = sem("var_ok")
        rstd_ok = sem("rstd_ok")
        consts_ok = sem("consts_ok")
        xn_ok = sem("xn_ok")
        xt_ps = sem("xt_ps")
        xt_sb = sem("xt_sb")
        dve_chain = sem("dve_chain")
        act_chain = sem("act_chain")

        class Chain:

            def __init__(self, eng, s):
                self.eng, self.s, self.n = eng, s, 0

            def __call__(self, ins):
                self.n += 1
                ins.then_inc(self.s, 1)
                self.eng.wait_ge(self.s, self.n)

        def both_tiles(eng, n, first_tile, value, chunk):
            if n == 0:
                eng.wait_ge(first_tile, value)
            else:
                eng.wait_ge(chunk_used, chunk + 1)

        class Run:
            def __init__(self, name, layer, window):
                self.layer, self.window = layer, window
                self.n_in, self.n_out = (FFN_IN, FFN_OUT) if layer == 0 else (LSTM_IN, LSTM_OUT)
                self.order = FFN_ORDER if layer == 0 else LSTM_ORDER
                self.at = {key: n for n, key in enumerate(self.order)}
                self.tag = "ffn" if layer == 0 else "lstm"
                self.g_built = sem(f"{name}_g_built")
                self.gather_ps = sem(f"{name}_gather_ps")
                self.turn_ps = sem(f"{name}_turn_ps")
                self.xe_cut = sem(f"{name}_xe_cut")
                self.gt_sb = sem(f"{name}_gt_sb")
                self.gates = sem(f"{name}_gates")
                self.h_ok = sem(f"{name}_h_ok")
                self.hT_ps = sem(f"{name}_hT_ps")
                self.hT_hi = sem(f"{name}_hT_hi")
                self.hT_lo = sem(f"{name}_hT_lo")
                self.y_cut = sem(f"{name}_y_cut")
                self.sum_ps = sem(f"{name}_sum_ps")
                self.sel_ok = sem(f"{name}_sel_ok") if window else None
                self.banks_h = 2 if layer == 0 else 1
                if window == 0:
                    self.jobs = E
                    self.base = CHUNK[self.order[0]]
                    self.raw_in, self.hi_cut, self.lo_cut, self.used = raw_in, hi_cut, lo_cut, chunk_used
                else:
                    self.jobs = MORE
                    self.base = 0
                    self.raw_in = [sem(f"{name}_raw_in{i}") for i in range(RAW)]
                    self.hi_cut, self.lo_cut, self.used = (sem(f"{name}_{n}") for n in (
                        "hi_cut", "lo_cut", "used"))

            def chunk(self, kind, e, c):
                if self.window:
                    return EC * e + (c if kind == "in" else self.n_in + c)
                return self.base + self.at[(self.tag, kind, e, c)]

            def last_in(self, e):
                return self.chunk("in", e, self.n_in - 1)

            def last_out(self, e):
                return self.chunk("out", e, self.n_out - 1)

        ffn, ffn_more, lstm, lstm_more = (Run("ffn", 0, 0), Run("ffn2", 0, 1),
                                          Run("lstm", 1, 0), Run("lstm2", 1, 1))
        gate = {n: sem(f"gate_{n}") for n in (
            "hid_ps", "hid_sb", "lg_ps", "shift", "exp", "d", "dexp", "mask", "pos_ps", "route",
            "combT", "more", "xn_cut", "par")}

        g0 = {n: sem(f"g0_{n}") for n in ("hot", "used", "cnt", "turn_ps", "adj", "h_ps",
                                          "cur", "cut", "lo", "ps", "xT_hi", "wh")}
        more_chain = [sem("ffn2_chain"), sem("lstm2_chain")]
        g1 = {n: sem(f"g1_{n}") for n in (
            "a_ps", "a_sb", "a_out", "gh_ps", "gh_sb", "w1e_hi", "w1e_lo", "ea_hi", "ea_lo", "e_ps",
            "mp", "m_hi", "m_lo", "hot_even", "hot_odd", "sum_ps", "s1", "s1T_ps", "aT", "agg_ps", "agg", "aggT_ps",
            "gi_ps", "rz_in", "rz", "n_in", "n", "rows", "bn", "gsel")}
        ea_in = [sem(f"g1_ea_in{i}") for i in range(3)]
        gath_in = [sem(f"g1_gath_in{i}") for i in range(4)]
        out_done = sem("out_done")

        block = ctx.enter_context(nc.Block())

        weights = A["weights"]

        @block.sync
        def _(sp):
            sp.dma_start(x[:, :, :], A["x"].rearrange("(n p) d -> p n d", p=P)).then_inc(x_in, 16)
            sp.dma_start(src_i[:, :], A["src"]).then_inc(idx_in, 16)
            sp.dma_start(dst_i[:, :], A["dst"]).then_inc(idx_in, 16)

            def load(run_raw_in, run_hi, run_lo, n, source):
                if n >= RAW:
                    sp.wait_ge(run_hi, n - RAW + 1)
                    sp.wait_ge(run_lo, n - RAW + 1)
                sp.dma_start(raw[n % RAW][:, :, :], source).then_inc(run_raw_in[n % RAW], 16)

            def more(run):
                sp.wait_ge(gate["more"], run.layer + 1)
                table = more_i[run.layer]
                number = sp.value_load(table[0:1, 0:1], min_val=0, max_val=MORE)
                for job in range(MORE):
                    with sp.If(number > job):
                        expert = sp.value_load(table[0:1, 1 + job:2 + job], min_val=0, max_val=E - 1)
                        sp.wait_ge(lo_cut, CHUNK[run.order[-1]] + 1)
                        for c in range(EC):
                            first = PLACE[(run.tag, "in", 0, 0)] + c
                            load(run.raw_in, run.hi_cut, run.lo_cut, EC * job + c,
                                 weights[bass.ds(expert * EC + first, 1), :, :, :]
                                 .rearrange("a p k c -> (a p) k c"))
                        sp.wait_ge(run.lo_cut, EC * (job + 1))

            def main(keys):
                for key in keys:
                    load(raw_in, hi_cut, lo_cut, CHUNK[key], weights[PLACE[key], :, :, :])

            def edge_attr(g):
                if g >= 3:
                    sp.wait_ge(g1["ea_hi"], g - 2)
                    sp.wait_ge(g1["ea_lo"], g - 2)
                n = min(GRP, ET - g * GRP) * P
                sp.dma_start(ea[:, g % 3, 0:n], A["ea"][:, g * GRP * P:g * GRP * P + n]).then_inc(ea_in[g % 3], 16)

            main([("L0", "W")] + FFN_ORDER)
            more(ffn_more)
            main(GNN_ORDER[0:4])
            sp.wait_ge(layer_done, 2)
            for g in range(3):
                edge_attr(g)
            main(GNN_ORDER[4:8])
            for g in range(3, NG):
                edge_attr(g)
            main(LSTM_ORDER)
            more(lstm_more)
            sp.wait_ge(layer_done, 4)
            sp.dma_start(out.rearrange("(n p) d -> p n d", p=P), x[:, :, :]).then_inc(out_done, 16)
            sp.wait_ge(out_done, 16)

        @block.gpsimd
        def _(pool):
            pool.iota(iota_t[:, :], [[1, T]], base=0, channel_multiplier=0,
                      allow_small_or_imprecise_dtypes=True).then_inc(iota_ok, 1)
            pool.iota(node_id[:, :], [[P, NT]], base=0, channel_multiplier=1,
                      allow_small_or_imprecise_dtypes=True).then_inc(iota_ok, 1)
            pool.dma_start(g0_b[:, :], A["L0_gnn_b"].partition_broadcast(P)).then_inc(par0, 16)
            pool.dma_start(g0_w[:, :], A["L0_gnn_diffusion_weights"].partition_broadcast(P)).then_inc(par0, 16)

            pool.memset(minus_half[:, :], -0.5).then_inc(half_ok, 1)
            pool.wait_ge(half_ok, 1)

            def root(layer):
                pool.wait_ge(var_ok, layer + 1)
                pool.tensor_tensor(rstd[:, :], var_eps[:, :], minus_half[:, :], ALU.pow).then_inc(rstd_ok, 1)

            root(0)

            def moe_params(b_in, b_o):
                n = b_in.shape[1]
                pool.dma_start(b_raw[0:E, 0:n], b_in).then_inc(par1, 16)
                pool.dma_start(b_raw[E:2 * E, 0:n], b_in).then_inc(par1, 16)
                pool.dma_start(b_out[:, :], b_o).then_inc(par1, 16)

            for nth, name in enumerate(("L0_ffn_gb2", "L1_ffn_router_b")):
                pool.dma_start(gb[:, nth, :], A[name].partition_broadcast(P)).then_inc(par1, 16)
            pool.dma_start(rw[:, :, :], A["L1_ffn_router_w"].rearrange("(k p) n -> p k n", p=P)).then_inc(par1, 16)
            pool.dma_start(gw1[:, :, :], A["L0_ffn_gw1"].rearrange("(k p) n -> p k n", p=P)).then_inc(par1, 16)
            pool.dma_start(gb1[:, :], A["L0_ffn_gb1"]).then_inc(par1, 16)
            pool.dma_start(gw2[:, :, :], A["L0_ffn_gw2"].rearrange("(k p) n -> p k n", p=P)).then_inc(par1, 16)
            moe_params(A["L0_ffn_be1"], A["L0_ffn_be2"])
            root(1)
            pool.wait_ge(layer_done, 1)
            pool.iota(sel_v[:, :, :], [[-1, E], [0, P]], base=0, channel_multiplier=1,
                      allow_small_or_imprecise_dtypes=True).then_inc(gate["par"], 1)

            pool.dma_start(w1e[:, :], A["w1e"]).then_inc(par2, 16)
            for dst, name in ((b1, "b1"), (g2v, "run_var"), (b2, "b2"), (g2s, "gamma"),
                              (g2b, "beta"), (g2m, "run_mean")):
                pool.dma_start(dst[:, :], A["L1_gnn_" + name].partition_broadcast(P)).then_inc(par2, 16)
            root(2)
            for r in range(4):
                pool.dma_start(gb_raw[r:r + 1, :], A["L1_gnn_b_ih" if r % 2 == 0 else "L1_gnn_b_hh"]).then_inc(par3, 16)
            pool.iota(g1_it[:, :, :], [[0, 3], [0, P]], base=0, channel_multiplier=1,
                      allow_small_or_imprecise_dtypes=True).then_inc(gate["par"], 1)

            pool.wait_ge(g1["a_sb"], NT)
            for n in range(NT):
                pool.dma_start(node_rows[n * P:(n + 1) * P, :], A_sb[:, n, :]).then_inc(g1["a_out"], 16)

            def hot(t):
                if t >= 4:
                    pool.wait_ge(g1["sum_ps"], t - 3)
                pool.tensor_scalar(onehot[:, t % 4, :], iota_t[:, :], dst_f[:, t:t + 1], None,
                                   ALU.is_equal).then_inc(g1["hot_even"], 1)

            pool.wait_ge(g1["a_out"], 16 * NT)
            for t in range(ET):
                if t >= 4:
                    pool.wait_ge(g1["mp"], t - 3)
                pool.indirect_dma_start(
                    out=gath[:, t % 4, :], out_offset=None, in_=node_rows[:, :],
                    in_offset=bass.IndirectOffsetOnAxis(ap=src_i[:, t:t + 1], axis=0)).then_inc(gath_in[t % 4], 16)
                if t >= 3 and t % 2:
                    hot(t - 3)
            for t in range(ET - 2, ET, 2):
                hot(t)

            pool.wait_ge(layer_done, 3)
            moe_params(A["lstm_b"], A["L1_ffn_bo"])
            root(3)
            pool.iota(sel_v[:, :, :], [[-1, E], [0, P]], base=0, channel_multiplier=1,
                      allow_small_or_imprecise_dtypes=True).then_inc(gate["par"], 1)

        @block.scalar
        def _(act):
            def cut_hi(run_raw_in, run_hi, run_used, n):
                act.wait_ge(run_raw_in[n % RAW], 16 * (n // RAW + 1))
                if n >= SPL:
                    act.wait_ge(run_used, n - SPL + 1)
                act.activation(whi[n % SPL][:, :, :], raw[n % RAW][:, :, :], ACT.Copy).then_inc(run_hi, 1)

            done = [0]

            def cut_to(n):
                while done[0] < n:
                    cut_hi(raw_in, hi_cut, chunk_used, done[0])
                    done[0] += 1

            def xT_copy(layer, dst):
                for n in range(NT):
                    act.wait_ge(xt_ps, NT * layer + n + 1)
                    act.activation(dst[:, n, :, :], quarters(B[5 - n]), ACT.Copy).then_inc(xt_sb, 1)

            def experts(run):
                def cuts(upto):
                    cut_to(min(upto, run.base + len(run.order)))

                def xe(e):
                    act.wait_ge(run.gather_ps, e + 1)
                    act.activation(xe_hi[:, :, :], quarters(B[6]), ACT.Copy).then_inc(run.xe_cut, 1)

                def outputs(e):
                    act.wait_ge(run.used, run.last_out(e) + 1)
                    act.wait_ge(run.gt_sb, e + 1)
                    act.activation(y_hi[:, :], B[7][:, :], ACT.Copy,
                                   scale=wslot[:, e % 3:e % 3 + 1]).then_inc(run.y_cut, 1)

                def turned(e):
                    for b in range(run.banks_h):
                        act.wait_ge(run.hT_ps, run.banks_h * e + b + 1)
                        act.activation(hT_hi[:, KB * b:KB * b + KB, :], quarters(B[5 - b]),
                                       ACT.Copy).then_inc(run.hT_hi, 1)

                def results(e):
                    if run.layer == 0:
                        for c in range(2):
                            act.wait_ge(run.used, run.chunk("in", e, c) + 1)
                            act.activation(act3[:, c, :], B[2 + c][:, :], ACT.Gelu).then_inc(run.h_ok, 1)
                        return
                    for c, f in ((0, ACT.Sigmoid), (1, ACT.Tanh), (2, ACT.Sigmoid)):
                        act.wait_ge(run.used, run.chunk("in", e, c) + 1)
                        act.activation(act3[:, c, :], B[2 + c][:, :], f).then_inc(run.gates, 1)
                    act.wait_ge(run.h_ok, 2 * e + 1)
                    act.activation(act3[:, 1, :], act3[:, 0, :], ACT.Tanh).then_inc(run.gates, 1)

                if run.window == 0:
                    cuts(run.base + SPL)
                    xe(0)
                    for step in range(E + 2):
                        if step >= 2:
                            outputs(step - 2)
                        if 1 <= step <= E:
                            turned(step - 1)
                        if step >= 2:
                            cuts(run.last_out(step - 2) + SPL + 1)
                        if step < E:
                            results(step)
                        if step + 1 < E:
                            xe(step + 1)
                        if step < E:
                            cuts(run.last_in(step) + SPL + 1)
                    return
                act.wait_ge(gate["more"], run.layer + 1)
                number = act.value_load(more_i[run.layer][0:1, 0:1], min_val=0, max_val=MORE)
                for job in range(MORE):
                    with act.If(number > job):
                        if job == 0:
                            act.wait_ge(chunk_used, CHUNK[run.order[-1]] + 1)
                        for c in range(EC):
                            cut_hi(run.raw_in, run.hi_cut, run.used, EC * job + c)
                        xe(job)
                        results(job)
                        turned(job)
                        outputs(job)

            cut_to(1)
            for n in range(NT):
                act.wait_ge(xt_ps, n + 1)
                act.activation(g0_xT_hi[:, n, :, :], quarters(B[5 - n]), ACT.Copy).then_inc(g0["xT_hi"], 1)
            for n in range(NT):
                act.wait_ge(g0["cur"], n + 1)
                for i in range(3):
                    act.activation(g0_wh[:, i, n, :], g0_h[:, n, :], ACT.Copy,
                                   scale=g0_w[:, 2 - i:3 - i]).then_inc(g0["wh"], 1)
            for i in range(3):
                for n in range(NT):
                    act.wait_ge(g0["cur"], NT * i + n + 1)
                    if n == 0 and i:
                        act.wait_ge(g0["ps"], NT * i)
                    act.activation(g0_hi[:, n, :], g0_cur[:, n, :], ACT.Copy).then_inc(g0["cut"], 1)
                cut_to(2 + i)

            def gating(nth):
                act.wait_ge(xn_ok, NT * (2 * nth - 1) + NT)
                act.activation(xn_hi[:, :, :], xn[:, :, :], ACT.Copy).then_inc(gate["xn_cut"], 1)
                xT_copy(2 * nth - 1, xnT)
                act.wait_ge(par1, PAR1[nth - 1])
                n = 2 * C if nth == 1 else 3 * C
                act.activation(b_hi[:, 0:n], b_raw[:, 0:n], ACT.Copy).then_inc(gate["xn_cut"], 1)
                if nth == 1:
                    for b in range(2):
                        act.wait_ge(gate["hid_ps"], b + 1)
                        act.activation(hid[:, b, :], B[2 + b][:, 0:T],
                                       ACT.Relu, bias=gb1[:, b:b + 1]).then_inc(gate["hid_sb"], 1)
                    act.wait_ge(gate["shift"], NT)
                    act.activation(pr[:, :, :], lg[:, :, :], ACT.Exp).then_inc(gate["exp"], 1)
                act.wait_ge(gate["d"], nth)
                act.activation(tw[:, :, 1], tw[:, :, 0], ACT.Exp).then_inc(gate["dexp"], 1)

            gating(1)
            experts(ffn)
            experts(ffn_more)

            first = CHUNK[("gnn", "W1")]
            cut_to(first + SPL)
            for n in range(NT):
                act.wait_ge(xt_ps, 2 * NT + n + 1)
                act.activation(g1_xT_hi[:, n, :, :], quarters(B[5 - n]), ACT.Copy).then_inc(xt_sb, 1)
            act.wait_ge(par2, 16 * 7)
            act.activation(w1e_hi[:, :], w1e[:, :], ACT.Copy).then_inc(g1["w1e_hi"], 1)
            act.wait_ge(par3, 16 * 4)
            act.activation(gb_rows[:, :], gb_raw[:, :], ACT.Copy).then_inc(g1["rows"], 1)

            def ea_cut(g):
                n = min(GRP, ET - g * GRP) * P
                act.wait_ge(ea_in[g % 3], 16 * (g // 3 + 1))
                if g >= 2:
                    act.wait_ge(g1["e_ps"], GRP * (g - 1))
                act.activation(ea_hi[:, g % 2, 0:n], ea[:, g % 3, 0:n], ACT.Copy).then_inc(g1["ea_hi"], 1)

            ea_cut(0)
            ea_cut(1)
            act.wait_ge(g1["bn"], 1)
            act.activation(g2v[:, :], g2v[:, :], ACT.Sqrt).then_inc(g1["bn"], 1)
            for n in range(SPL):
                cut_to(first + SPL + n + 1)
            for t in range(ET):
                act.wait_ge(g1["mp"], t + 1)
                if t >= 2:
                    act.wait_ge(g1["sum_ps"], t - 1)
                act.activation(m_hi[:, t % 2, :], mp[:, t % 2, :], ACT.Relu).then_inc(g1["m_hi"], 1)
                if t % GRP == 1 and t // GRP + 1 < NG and t >= GRP:
                    ea_cut(t // GRP + 1)
            for n in range(NT):
                act.wait_ge(g1["s1T_ps"], n + 1)
                act.activation(aT_hi[:, n, :, :], quarters(B[6 + n]), ACT.Copy).then_inc(g1["aT"], 1)
            for n in range(NT):
                act.wait_ge(g1["aggT_ps"], n + 1)
                act.activation(aT_hi[:, n, :, :], quarters(B[6 + n]), ACT.Copy).then_inc(g1["aT"], 1)
            for g in range(2):
                for n in range(NT):
                    act.wait_ge(g1["rz_in"], NT * g + n + 1)
                    act.activation(rz[:, n, g, :], rz[:, n, g, :], ACT.Sigmoid).then_inc(g1["rz"], 1)
            for n in range(NT):
                act.wait_ge(g1["n_in"], n + 1)
                act.activation(rz[:, n, 2, :], rz[:, n, 2, :], ACT.Tanh).then_inc(g1["n"], 1)

            cut_to(CHUNK[LSTM_ORDER[0]] + SPL)
            gating(2)
            experts(lstm)
            experts(lstm_more)

        @block.vector
        def _(dve):
            link = Chain(dve, dve_chain)

            def cut_lo(run_hi, run_lo, n):
                dve.wait_ge(run_hi, n + 1)
                dve.tensor_tensor(wlo[n % SPL][:, :, :], raw[n % RAW][:, :, :],
                                  whi[n % SPL][:, :, :].bitcast(f32), ALU.subtract).then_inc(run_lo, 1)

            done = [0]

            def cut_to(n):
                while done[0] < n:
                    cut_lo(hi_cut, lo_cut, done[0])
                    done[0] += 1

            def layernorm(layer):
                for n in range(NT):
                    link(dve.bn_stats(stats[:, n, :], x[:, n, :]))
                for n in range(NT):
                    link(dve.bn_aggr(mv[:, n, :], stats[:, n, :]))
                dve.tensor_scalar(var_eps[:, :], mv[:, :, 1], EPS, None, ALU.add).then_inc(var_ok, 1)
                dve.wait_ge(rstd_ok, layer + 1)
                for n in range(NT):
                    dve.tensor_scalar(xn[:, n, :], x[:, n, :], mv[:, n, 0:1], rstd[:, n:n + 1],
                                      ALU.subtract, ALU.mult).then_inc(xn_ok, 1)

            dve.wait_ge(x_in, 16)
            layernorm(0)
            dve.wait_ge(iota_ok, 2)
            for n in range(NT):
                link(dve.tensor_scalar(eye2[:, n, :], iota_t[:, :], node_id[:, n:n + 1], None, ALU.is_equal))
            link(dve.tensor_copy(iota_b[:, :], iota_t[:, :]))
            dve.wait_ge(idx_in, 32)
            dve.tensor_copy(g0_src_f[:, :], src_i[:, :]).then_inc(consts_ok, 1)
            dve.tensor_copy(dst_f[:, :], dst_i[:, :]).then_inc(consts_ok, 1)
            dve.wait_ge(consts_ok, 2)
            for n in range(NT):
                dve.wait_ge(g0["xT_hi"], n + 1)
                dve.tensor_tensor(g0_xT_lo[:, n, :, :], quarters(B[5 - n]),
                                  g0_xT_hi[:, n, :, :].bitcast(f32), ALU.subtract).then_inc(xt_sb, 1)
            cut_to(1)
            for t in range(ET):
                if t >= 4:
                    dve.wait_ge(g0["used"], t - 3)
                dve.tensor_scalar(g0_S[:, t % 4, :], iota_b[:, :], g0_src_f[:, t:t + 1], None, ALU.is_equal)
                dve.tensor_scalar(g0_D[:, t % 4, :], iota_b[:, :], dst_f[:, t:t + 1], None,
                                  ALU.is_equal).then_inc(g0["hot"], 1)
            dve.wait_ge(par0, 32)
            for n in range(NT):
                both_tiles(dve, n, g0["h_ps"], 1, 0)
                link(dve.tensor_tensor(g0_h[:, n, :], B[2 + n][:, :], g0_b[:, :], ALU.add))
                dve.tensor_scalar(g0_cur[:, n, :], g0_h[:, n, :], g0_w[:, 3:4], None,
                                  ALU.mult).then_inc(g0["cur"], 1)
            dve.wait_ge(g0["used"], ET)
            for n in range(NT):
                dve.tensor_copy(g0_cnt[:, n, :], B[n][:, 0:T]).then_inc(g0["cnt"], 1)
            dve.wait_ge(g0["turn_ps"], 1)
            dve.wait_ge(g0["cnt"], NT)
            for n in range(NT):
                turned = B[6][:, n * T:(n + 1) * T]
                dve.tensor_reduce(deg[:, n:n + 1], turned, AX, ALU.add)
                link(dve.tensor_tensor(g0_sum[:, n, :], turned, g0_cnt[:, n, :], ALU.add))
                link(dve.scalar_tensor_tensor(out=g0_adj[:, n, :], in0=g0_sum[:, n, :], scalar=1.0,
                                              in1=eye2[:, n, :], op0=ALU.min, op1=ALU.add))
            link(dve.tensor_reduce(g0_rs[:, :], g0_adj[:, :, :].bitcast(f32), AX, ALU.add))
            link(dve.tensor_scalar(g0_rs[:, :], g0_rs[:, :], 1.0, None, ALU.max))
            ins = dve.reciprocal(g0_rinv[:, :], g0_rs[:, :])
            ins.then_inc(g0["adj"], 1)
            dve.wait_ge(g0["adj"], 1)
            for i in range(3):
                for n in range(NT):
                    dve.wait_ge(g0["cut"], NT * i + n + 1)
                    dve.tensor_tensor(g0_lo[:, n, :], g0_cur[:, n, :], g0_hi[:, n, :].bitcast(f32),
                                      ALU.subtract).then_inc(g0["lo"], 1)
                dve.wait_ge(g0["wh"], 3 * NT)
                for n in range(NT):
                    dve.wait_ge(g0["ps"], NT * i + n + 1)
                    dve.scalar_tensor_tensor(out=g0_cur[:, n, :], in0=B[2 + n][:, :],
                                             scalar=g0_rinv[:, n:n + 1], in1=g0_wh[:, i, n, :],
                                             op0=ALU.mult, op1=ALU.add).then_inc(g0["cur"], 1)
            dve.wait_ge(g0["cur"], NT * 4)
            for n in range(NT):
                ins = dve.scalar_tensor_tensor(out=x[:, n, :], in0=g0_cur[:, n, :], scalar=0.0,
                                               in1=x[:, n, :], op0=ALU.max, op1=ALU.add)
                link(ins)
            dve.drain().then_inc(layer_done, 1)

            def gating(nth):
                layernorm(2 * nth - 1)
                dve.tensor_scalar(tri[:, 0:P], iota_t[:, 0:P], node_id[:, 0:1], None, ALU.is_gt)
                dve.memset(tri[:, P:T], 1.0)
                dve.wait_ge(gate["par"], 1 if nth == 1 else 3)
                link(dve.tensor_scalar(sel_a[:, :, :], sel_v[:, :, :], 0.0, None, ALU.is_equal))
                link(dve.scalar_tensor_tensor(out=sel[:, :, :], in0=sel_v[:, :, :], scalar=float(E),
                                              in1=sel_a[:, :, :], op0=ALU.is_equal, op1=ALU.max))
                link(dve.tensor_scalar(alpha[:, :], node_id[0:2 * E, 0:1], float(E), -1.0, ALU.is_ge, ALU.mult))
                n = (2 if nth == 1 else 3) * C
                dve.wait_ge(gate["xn_cut"], 2 * nth)
                dve.tensor_tensor(xn_lo[:, :, :], xn[:, :, :], xn_hi[:, :, :].bitcast(f32), ALU.subtract)
                link(dve.scalar_tensor_tensor(out=b_rows[:, 0:n], in0=b_hi[:, 0:n].bitcast(f32),
                                              scalar=alpha[:, 0:1], in1=b_raw[:, 0:n],
                                              op0=ALU.mult, op1=ALU.add))
                dve.wait_ge(par1, PAR1[0])
                dve.wait_ge(gate["lg_ps"], nth)
                ps = B[6][:, 0:NT * E].rearrange("p (n e) -> p n e", n=NT)
                dst = lg if nth == 1 else pr
                for m in range(NT):
                    link(dve.tensor_tensor(dst[:, m, :], ps[:, m, :], gb[:, nth - 1, :], ALU.add))
                if nth == 1:
                    link(dve.tensor_reduce(red[:, :], lg[:, :, :], AX, ALU.max))
                    for m in range(NT):
                        dve.tensor_scalar(lg[:, m, :], lg[:, m, :], red[:, m:m + 1], None, ALU.subtract)\
                           .then_inc(gate["shift"], 1)
                    dve.wait_ge(gate["exp"], 1)
                    link(dve.tensor_reduce(red2[:, :], pr[:, :, :], AX, ALU.add))
                    link(dve.reciprocal(red[:, :], red2[:, :]))
                    for m in range(NT):
                        link(dve.tensor_scalar(pr[:, m, :], pr[:, m, :], red[:, m:m + 1], None, ALU.mult))
                for m in range(NT):
                    link(dve.max(top[:, m, :], pr[:, m, :]))
                    link(dve.max_index(topi[:, m, :], top[:, m, :], pr[:, m, :]))
                link(dve.tensor_copy(topf[:, :, :], topi[:, :, :]))
                dve.tensor_tensor(tw[:, :, 0], top[:, :, 1], top[:, :, 0], ALU.subtract).then_inc(gate["d"], 1)
                for m in range(NT):
                    for k in range(2):
                        link(dve.tensor_scalar(oh[:, m, k, :], iota_t[:, 0:E], topf[:, m, k:k + 1], None,
                                               ALU.is_equal))
                dve.tensor_tensor(mask[:, :, :], oh[:, :, 0, :], oh[:, :, 1, :], ALU.add)\
                   .then_inc(gate["mask"], 1)
                dve.wait_ge(gate["mask"], nth)
                link(dve.tensor_scalar(penal[:, :, :], mask[:, :, :], -1000.0, 1000.0, ALU.mult, ALU.add))
                dve.wait_ge(gate["dexp"], nth)
                link(dve.tensor_scalar(tw[:, :, 2], tw[:, :, 1], 1.0, None, ALU.add))
                link(dve.reciprocal(tw[:, :, 3], tw[:, :, 2]))
                link(dve.tensor_tensor(tw[:, :, 2], tw[:, :, 1], tw[:, :, 3], ALU.mult))
                for m in range(NT):
                    link(dve.tensor_scalar(comb[:, m, :], oh[:, m, 0, :], tw[:, m, 3:4], None, ALU.mult))
                    link(dve.scalar_tensor_tensor(out=comb[:, m, :], in0=oh[:, m, 1, :],
                                                  scalar=tw[:, m, 2:3], in1=comb[:, m, :],
                                                  op0=ALU.mult, op1=ALU.add))
                dve.wait_ge(gate["pos_ps"], nth)
                ps = B[6][:, 32:32 + NT * E].rearrange("p (n e) -> p n e", n=NT)
                link(dve.tensor_tensor(posm[:, :, :], ps, penal[:, :, :], ALU.add))
                dve.tensor_scalar(over[:, :], B[6][:, 64:64 + E], float(P), None, ALU.is_gt).then_inc(gate["route"], 1)

            def more_experts(nth):
                dve.wait_ge(gate["route"], nth)
                link(dve.tensor_tensor_scan(rank[:, :], tri[:, P:P + E], over[:, :], 0.0, ALU.mult, ALU.add))
                for job in range(MORE):
                    link(dve.scalar_tensor_tensor(out=picked[:, job, :], in0=rank[:, :], scalar=job + 1.0,
                                                  in1=over[:, :], op0=ALU.is_equal, op1=ALU.mult))
                    link(dve.tensor_tensor(prod[:, 0, :], picked[:, job, :], iota_t[:, 0:E], ALU.mult))
                    link(dve.tensor_reduce(ids[:, 1 + job:2 + job], prod[:, 0, :], AX, ALU.add))
                link(dve.tensor_copy(ids[:, 0:1], rank[:, E - 1:E]))
                dve.tensor_copy(more_i[nth - 1][:, :], ids[:, :]).then_inc(gate["more"], 1)

            def experts(run, link):
                def cuts(upto):
                    cut_to(min(upto, run.base + len(run.order)))

                def build_g(e):
                    if e >= 2:
                        dve.wait_ge(run.turn_ps, e - 1)
                    for n in range(NT):
                        slot = posm[:, n, e:e + 1] if run.window == 0 else more_pc[:, e, n:n + 1]
                        ins = dve.tensor_scalar(G[:, e % 2, n, :], iota_t[:, run.window * P:(run.window + 1) * P],
                                                slot, None, ALU.is_equal)
                    ins.then_inc(run.g_built, 1)

                def xe(e):
                    dve.wait_ge(run.xe_cut, 2 * e + 1)
                    dve.tensor_tensor(xe_lo[:, :, :], quarters(B[6]), xe_hi[:, :, :].bitcast(f32),
                                      ALU.subtract).then_inc(run.xe_cut, 1)
                    dve.wait_ge(run.turn_ps, e + 1)
                    dve.tensor_copy(GT[:, e % 3, :], B[5][:, 0:T])
                    dve.tensor_copy(wslot[:, e % 3:e % 3 + 1], B[5][:, T:T + 1]).then_inc(run.gt_sb, 1)

                def outputs(e):
                    dve.wait_ge(run.y_cut, 2 * e + 1)
                    dve.wait_ge(run.gt_sb, e + 1)
                    dve.scalar_tensor_tensor(out=y_lo[:, :], in0=B[7][:, :], scalar=wslot[:, e % 3:e % 3 + 1],
                                             in1=y_hi[:, :].bitcast(f32), op0=ALU.mult,
                                             op1=ALU.subtract).then_inc(run.y_cut, 1)

                def turned(e):
                    for b in range(run.banks_h):
                        dve.wait_ge(run.hT_hi, run.banks_h * e + b + 1)
                        dve.tensor_tensor(hT_lo[:, KB * b:KB * b + KB, :], quarters(B[5 - b]),
                                          hT_hi[:, KB * b:KB * b + KB, :].bitcast(f32),
                                          ALU.subtract).then_inc(run.hT_lo, 1)

                def results(e):
                    if run.layer == 1:
                        dve.wait_ge(run.gates, 4 * e + 2)
                        dve.tensor_tensor(act3[:, 0, :], act3[:, 0, :], act3[:, 1, :], ALU.mult)\
                           .then_inc(run.h_ok, 1)
                        dve.wait_ge(run.gates, 4 * e + 4)
                        dve.tensor_tensor(act3[:, 2, :], act3[:, 2, :], act3[:, 1, :], ALU.mult)\
                           .then_inc(run.h_ok, 1)

                def add_to_x(sums):
                    dve.wait_ge(run.sum_ps, sums)
                    for n in range(NT):
                        link(dve.tensor_tensor(x[:, n, :], x[:, n, :], B[n][:, :], ALU.add))

                if run.window == 0:
                    build_g(0)
                    build_g(1)
                    cuts(run.base + SPL)
                    xe(0)
                    more_experts(run.layer + 1)
                    for step in range(E + 2):
                        if step >= 2:
                            outputs(step - 2)
                        if 1 <= step <= E:
                            turned(step - 1)
                        if step >= 2:
                            cuts(run.last_out(step - 2) + SPL + 1)
                        if step < E:
                            results(step)
                        if step + 1 < E:
                            xe(step + 1)
                        if step + 2 < E:
                            build_g(step + 2)
                        if step == 0:
                            comb_turned(run.layer + 1)
                        if step < E:
                            cuts(run.last_in(step) + SPL + 1)
                    add_to_x(E)
                    return
                dve.wait_ge(gate["more"], run.layer + 1)
                number = dve.value_load(more_i[run.layer][0:1, 0:1], min_val=0, max_val=MORE)
                for job in range(MORE):
                    with dve.If(number > job):
                        for n in range(NT):
                            for i, table in enumerate((posm, comb)):
                                link(dve.tensor_tensor(prod[:, NT * i + n, :], table[:, n, :],
                                                       picked[:, job, :], ALU.mult))
                        link(dve.tensor_reduce(more_pc[:, job, :], prod[:, :, :], AX, ALU.add))
                        build_g(job)
                        link(dve.tensor_scalar(sel_m[:, 0, :], sel_v[:, 0, :], ids[0:2 * E, 1 + job:2 + job],
                                               None, ALU.is_equal))
                        link(dve.tensor_scalar(sel_m[:, 1, :], sel_v[:, 0, :], float(E),
                                               ids[0:2 * E, 1 + job:2 + job], ALU.subtract, ALU.is_equal))
                        dve.tensor_tensor(sel_more[:, :], sel_m[:, 0, :], sel_m[:, 1, :], ALU.max)\
                           .then_inc(run.sel_ok, 1)
                        xe(job)
                        for c in range(EC):
                            cut_lo(run.hi_cut, run.lo_cut, EC * job + c)
                        results(job)
                        turned(job)
                        outputs(job)
                        add_to_x(job + 1)

            def comb_turned(nth):
                dve.wait_ge(gate["combT"], 2 * nth - 1)
                dve.tensor_copy(combT[:, :], B[7][0:E, 0:T]).then_inc(gate["combT"], 1)

            gating(1)
            experts(ffn, link)
            experts(ffn_more, Chain(dve, more_chain[0]))
            dve.drain().then_inc(layer_done, 1)

            layernorm(2)
            first = CHUNK[("gnn", "W1")]
            dve.wait_ge(xt_sb, 3 * NT)
            for n in range(NT):
                dve.tensor_tensor(g1_xT_lo[:, n, :, :], quarters(B[5 - n]),
                                  g1_xT_hi[:, n, :, :].bitcast(f32), ALU.subtract).then_inc(xt_sb, 1)
            cut_to(first + SPL)
            dve.wait_ge(par2, 16 * 7)
            dve.wait_ge(g1["w1e_hi"], 1)
            dve.tensor_tensor(w1e_lo[:, :], w1e[:, :], w1e_hi[:, :].bitcast(f32), ALU.subtract)\
               .then_inc(g1["w1e_lo"], 1)
            dve.wait_ge(gate["par"], 2)
            link(dve.tensor_scalar(galpha[:, :], node_id[0:4, 0:1], 2.0, -1.0, ALU.is_ge, ALU.mult))
            dve.wait_ge(g1["rows"], 1)
            dve.scalar_tensor_tensor(out=gb_rows[:, :], in0=gb_rows[:, :].bitcast(f32),
                                     scalar=galpha[:, 0:1], in1=gb_raw[:, :],
                                     op0=ALU.mult, op1=ALU.add).then_inc(g1["rows"], 1)
            for i, row in ((2, 0.0), (1, 1.0)):
                link(dve.tensor_scalar(g1_t[:, i, :], g1_it[:, i, :], row, None, ALU.is_equal))
                link(dve.scalar_tensor_tensor(out=gsel[:, i, :], in0=g1_it[:, i, :], scalar=row + 2.0,
                                              in1=g1_t[:, i, :], op0=ALU.is_equal, op1=ALU.max))
            dve.tensor_scalar(gsel[:, 0, :], g1_it[:, 0, :], 0.0, None, ALU.is_ge).then_inc(g1["gsel"], 1)
            dve.tensor_scalar(g2v[:, :], g2v[:, :], EPS, None, ALU.add).then_inc(g1["bn"], 1)
            for n in range(NT):
                both_tiles(dve, n, g1["a_ps"], 1, CHUNK[("gnn", "W1")])
                dve.tensor_tensor(A_sb[:, n, :], B[2 + n][:, :], b1[:, :], ALU.add).then_inc(g1["a_sb"], 1)

            def ea_cut(g):
                n = min(GRP, ET - g * GRP) * P
                dve.wait_ge(g1["ea_hi"], g + 1)
                dve.tensor_tensor(ea_lo[:, g % 2, 0:n], ea[:, g % 3, 0:n],
                                  ea_hi[:, g % 2, 0:n].bitcast(f32), ALU.subtract).then_inc(g1["ea_lo"], 1)

            ea_cut(0)
            ea_cut(1)
            for g in range(3):
                for n in range(NT):
                    both_tiles(dve, n, g1["gh_ps"], g + 1, CHUNK[("gnn", "Whh", g)])
                    dve.tensor_copy(gh[:, n, g, :], B[(6, 2, 6)[g] + n][:, :]).then_inc(g1["gh_sb"], 1)
                cut_to(first + SPL + 1 + g)
            cut_to(first + 2 * SPL)

            def m_cut(t):
                dve.wait_ge(g1["m_hi"], t + 1)
                dve.scalar_tensor_tensor(out=m_lo[:, t % 2, :], in0=mp[:, t % 2, :], scalar=0.0,
                                         in1=m_hi[:, t % 2, :].bitcast(f32), op0=ALU.max,
                                         op1=ALU.subtract).then_inc(g1["m_lo"], 1)

            def hot(t):
                if t >= 4:
                    dve.wait_ge(g1["sum_ps"], t - 3)
                dve.tensor_scalar(onehot[:, t % 4, :], iota_t[:, :], dst_f[:, t:t + 1], None,
                                  ALU.is_equal).then_inc(g1["hot_odd"], 1)

            hot(1)
            for t in range(ET):
                if t % 2 == 0 and 2 <= t < ET - 1:
                    hot(t + 1)
                dve.wait_ge(g1["e_ps"], t + 1)
                dve.wait_ge(gath_in[t % 4], 16 * (t // 4 + 1))
                if t >= 2:
                    dve.wait_ge(g1["m_lo"], t - 1)
                dve.tensor_tensor(mp[:, t % 2, :], B[2 + t % 3][:, :], gath[:, t % 4, :], ALU.add)\
                   .then_inc(g1["mp"], 1)
                if t >= 1:
                    m_cut(t - 1)
                if t % GRP == 1 and t // GRP + 1 < NG and t >= GRP:
                    ea_cut(t // GRP + 1)
            m_cut(ET - 1)
            dve.wait_ge(g1["sum_ps"], ET)
            for n in range(NT):
                dve.tensor_copy(S1[:, n, :], B[n][:, :]).then_inc(g1["s1"], 1)
            for n in range(NT):
                dve.wait_ge(g1["aT"], NT)
                dve.tensor_tensor(aT_lo[:, n, :, :], quarters(B[6 + n]),
                                  aT_hi[:, n, :, :].bitcast(f32), ALU.subtract).then_inc(g1["aT"], 1)
            for n in range(NT):
                both_tiles(dve, n, g1["agg_ps"], 1, CHUNK[("gnn", "W2")])
                dve.scalar_tensor_tensor(out=agg[:, n, :], in0=b2[:, :], scalar=deg[:, n:n + 1],
                                         in1=B[2 + n][:, :], op0=ALU.mult, op1=ALU.add)\
                   .then_inc(g1["agg"], 1)
            for n in range(NT):
                dve.wait_ge(g1["aT"], 3 * NT)
                dve.tensor_tensor(aT_lo[:, n, :, :], quarters(B[6 + n]),
                                  aT_hi[:, n, :, :].bitcast(f32), ALU.subtract).then_inc(g1["aT"], 1)
            for g in range(2):
                for n in range(NT):
                    both_tiles(dve, n, g1["gi_ps"], g + 1, CHUNK[("gnn", "Wih", g)])
                    dve.tensor_tensor(rz[:, n, g, :], B[2 * g + n][:, :], gh[:, n, g, :], ALU.add)\
                       .then_inc(g1["rz_in"], 1)
            for n in range(NT):
                dve.wait_ge(g1["rz"], n + 1)
                link(dve.tensor_tensor(rz[:, n, 2, :], rz[:, n, 0, :], gh[:, n, 2, :], ALU.mult))
                both_tiles(dve, n, g1["gi_ps"], 3, CHUNK[("gnn", "Wih", 2)])
                dve.tensor_tensor(rz[:, n, 2, :], rz[:, n, 2, :], B[4 + n][:, :], ALU.add)\
                   .then_inc(g1["n_in"], 1)
            dve.wait_ge(g1["bn"], 2)
            link(dve.reciprocal(g2v[:, :], g2v[:, :]))
            link(dve.tensor_tensor(g2s[:, :], g2s[:, :], g2v[:, :], ALU.mult))
            for n in range(NT):
                dve.wait_ge(g1["n"], n + 1)
                dve.wait_ge(g1["rz"], NT + n + 1)
                link(dve.tensor_tensor(rz[:, n, 0, :], xn[:, n, :], rz[:, n, 2, :], ALU.subtract))
                link(dve.tensor_tensor(rz[:, n, 0, :], rz[:, n, 0, :], rz[:, n, 1, :], ALU.mult))
                link(dve.tensor_tensor(rz[:, n, 0, :], rz[:, n, 0, :], rz[:, n, 2, :], ALU.add))
                link(dve.tensor_tensor(rz[:, n, 0, :], rz[:, n, 0, :], g2m[:, :], ALU.subtract))
                link(dve.tensor_tensor(rz[:, n, 0, :], rz[:, n, 0, :], g2s[:, :], ALU.mult))
                link(dve.tensor_tensor(rz[:, n, 0, :], rz[:, n, 0, :], g2b[:, :], ALU.add))
                link(dve.tensor_tensor(rz[:, n, 0, :], rz[:, n, 0, :], xn[:, n, :], ALU.add))
                link(dve.tensor_tensor(x[:, n, :], x[:, n, :], rz[:, n, 0, :], ALU.add))
            dve.drain().then_inc(layer_done, 1)

            cut_to(CHUNK[LSTM_ORDER[0]] + SPL)
            gating(2)
            experts(lstm, link)
            experts(lstm_more, Chain(dve, more_chain[1]))
            dve.drain().then_inc(layer_done, 1)

        @block.tensor
        def _(pe):
            def mm3(ps, xh, xl, wh, wl, first, last):
                pe.matmul(ps, xh, wh, start=first, stop=False)
                pe.matmul(ps, xh, wl, start=False, stop=False)
                return pe.matmul(ps, xl, wh, start=False, stop=last)

            def has_chunk(run_lo, n):
                pe.wait_ge(run_lo, n + 1)

            def turn_x(layer):
                for n in range(NT):
                    pe.wait_ge(xn_ok, NT * layer + n + 1)
                    for k in range(KB):
                        ins = pe.transpose(quarters(B[5 - n])[:, k, :], xn[:, n, k * P:(k + 1) * P], ident)
                    ins.then_inc(xt_ps, 1)

            pe.wait_ge(consts_ok, 1)
            turn_x(0)
            pe.wait_ge(xt_sb, NT)
            has_chunk(lo_cut, 0)
            for n in range(NT):
                for k in range(KB):
                    ins = mm3(B[2 + n][:, :], g0_xT_hi[:, n, k, :], g0_xT_lo[:, n, k, :],
                              whi[0][:, k, :], wlo[0][:, k, :], k == 0, k == KB - 1)
                ins.then_inc(g0["h_ps"] if n == 0 else chunk_used, 1)
            for t in range(ET):
                pe.wait_ge(g0["hot"], t + 1)
                for n in range(NT):
                    ins = pe.matmul(B[n][:, 0:T], g0_S[:, t % 4, n * P:(n + 1) * P], g0_D[:, t % 4, :],
                                    start=t == 0, stop=t == ET - 1)
                ins.then_inc(g0["used"], 1)
            pe.wait_ge(g0["cnt"], NT)
            for a in range(NT):
                for b in range(NT):
                    ins = pe.transpose(B[6][:, b * T + a * P:b * T + (a + 1) * P],
                                       g0_cnt[:, a, b * P:(b + 1) * P], ident)
            ins.then_inc(g0["turn_ps"], 1)
            pe.wait_ge(g0["adj"], 1)
            for i in range(3):
                pe.wait_ge(g0["lo"], NT * (i + 1))
                for n in range(NT):
                    for m in range(NT):
                        lhs = g0_adj[:, m, n * P:(n + 1) * P]
                        pe.matmul(B[2 + n][:, :], lhs, g0_hi[:, m, :], start=m == 0, stop=False)
                        ins = pe.matmul(B[2 + n][:, :], lhs, g0_lo[:, m, :], start=False, stop=m == NT - 1)
                    ins.then_inc(g0["ps"], 1)

            def gating(nth):
                turn_x(2 * nth - 1)
                pe.wait_ge(par1, PAR1[0])
                pe.wait_ge(xt_sb, NT * 2 if nth == 1 else 5 * NT)
                if nth == 1:
                    for b in range(2):
                        for k in range(KB):
                            ins = pe.matmul(B[2 + b][:, 0:T].rearrange("p (n t) -> p n t", n=NT),
                                            gw1[:, k, b * P:(b + 1) * P], xnT[:, :, k, :],
                                            start=k == 0, stop=k == KB - 1)
                        ins.then_inc(gate["hid_ps"], 1)
                    pe.wait_ge(gate["hid_sb"], 2)
                for n in range(NT):
                    for k in range(2 if nth == 1 else KB):
                        lhs = hid[:, k, n * P:(n + 1) * P] if nth == 1 else xnT[:, n, k, :]
                        rhs = gw2[:, k, :] if nth == 1 else rw[:, k, :]
                        ins = pe.matmul(B[6][:, n * E:(n + 1) * E], lhs, rhs, start=k == 0,
                                        stop=k == (2 if nth == 1 else KB) - 1)
                ins.then_inc(gate["lg_ps"], 1)
                pe.wait_ge(gate["mask"], nth)
                pe.matmul(B[6][:, 32:32 + E], tri[:, 0:P], mask[:, 0, :], start=True, stop=True)
                pe.matmul(B[6][:, 32 + E:32 + 2 * E], tri[:, P:T], mask[:, 0, :], start=True, stop=False)
                pe.matmul(B[6][:, 32 + E:32 + 2 * E], tri[:, 0:P], mask[:, 1, :], start=False, stop=True)
                pe.matmul(B[6][:, 64:64 + E], tri[:, P:T], mask[:, 0, :], start=True, stop=False)
                pe.matmul(B[6][:, 64:64 + E], tri[:, P:T], mask[:, 1, :], start=False, stop=True)\
                  .then_inc(gate["pos_ps"], 1)

            def biases(nth):
                pe.wait_ge(gate["route"], nth)
                for n in range(NT):
                    ins = pe.matmul(B[7][0:E, n * P:(n + 1) * P], comb[:, n, :], ident, start=True, stop=True)
                ins.then_inc(gate["combT"], 1)
                pe.wait_ge(gate["combT"], 2 * nth)
                for n in range(NT):
                    pe.matmul(B[n][:, :], combT[:, n * P:(n + 1) * P], b_out[:, :], start=True, stop=False,
                              skip_group_check=True)

            def experts(run):
                def gather(e):
                    pe.wait_ge(run.g_built, e + 1)
                    if e >= 1:
                        pe.wait_ge(run.xe_cut, 2 * e)
                        pe.wait_ge(run.gt_sb, e)
                        if run.window == 0 and e >= 2:
                            pe.wait_ge(run.hT_lo, run.banks_h * (e - 1))
                    for k in range(KB):
                        for n in range(NT):
                            pe.matmul(quarters(B[6])[:, k, :], xn_hi[:, n, k * P:(k + 1) * P],
                                      G[:, e % 2, n, :], start=n == 0, stop=False)
                            ins = pe.matmul(quarters(B[6])[:, k, :], xn_lo[:, n, k * P:(k + 1) * P],
                                            G[:, e % 2, n, :], start=False, stop=n == NT - 1)
                    ins.then_inc(run.gather_ps, 1)
                    for n in range(NT):
                        pe.transpose(B[5][:, n * P:(n + 1) * P], G[:, e % 2, n, :].bitcast(f32), ident)
                    for n in range(NT):
                        weight = comb[:, n, e:e + 1] if run.window == 0 else more_pc[:, e, NT + n:NT + n + 1]
                        ins = pe.matmul(B[5][:, T:T + 1], G[:, e % 2, n, :].bitcast(f32),
                                        weight, start=n == 0, stop=n == NT - 1)
                    ins.then_inc(run.turn_ps, 1)

                def first_product(e):
                    pe.wait_ge(run.xe_cut, 2 * e + 2)
                    if run.window:
                        pe.wait_ge(run.sel_ok, e + 1)
                    for c in range(run.n_in):
                        if e >= 1 and c == 0:
                            pe.wait_ge(run.h_ok, 2 * e)
                        q = run.chunk("in", e, c)
                        has_chunk(run.lo_cut, q)
                        rows = sel[:, e, :] if run.window == 0 else sel_more[:, :]
                        pe.matmul(B[2 + c][:, :], rows, b_rows[:, c * C:(c + 1) * C],
                                  start=True, stop=False)
                        for k in range(KB):
                            ins = mm3(B[2 + c][:, :], xe_hi[:, k, :], xe_lo[:, k, :],
                                      whi[q % SPL][:, k, :], wlo[q % SPL][:, k, :], False, k == KB - 1)
                        ins.then_inc(run.used, 1)

                def weighted_sum(e):
                    pe.wait_ge(run.y_cut, 2 * e + 2)
                    pe.wait_ge(run.gt_sb, e + 1)
                    for n in range(NT):
                        lhs = GT[:, e % 3, n * P:(n + 1) * P]
                        pe.matmul(B[n][:, :], lhs, y_hi[:, :], start=run.window == 1,
                                  stop=False, skip_group_check=True)
                        ins = pe.matmul(B[n][:, :], lhs, y_lo[:, :], start=False,
                                        stop=run.window == 1 or e == E - 1, skip_group_check=True)
                    ins.then_inc(run.sum_ps, 1)

                def second_product(e):
                    pe.wait_ge(run.hT_lo, run.banks_h * (e + 1))
                    if e >= 1:
                        pe.wait_ge(run.y_cut, 2 * e)
                    for c in range(run.n_out):
                        q = run.chunk("out", e, c)
                        has_chunk(run.lo_cut, q)
                        for k in range(KB):
                            ins = mm3(B[7][:, :], hT_hi[:, c * KB + k, :], hT_lo[:, c * KB + k, :],
                                      whi[q % SPL][:, k, :], wlo[q % SPL][:, k, :],
                                      c == 0 and k == 0, c == run.n_out - 1 and k == KB - 1)
                        ins.then_inc(run.used, 1)

                def turn_h(e):
                    pe.wait_ge(run.h_ok, 2 * (e + 1))
                    pe.wait_ge(run.gt_sb, min(e + 2, E) if run.window == 0 else e + 1)
                    for b in range(run.banks_h):
                        for k in range(KB):
                            h = act3[:, b if run.layer == 0 else 2, k * P:(k + 1) * P]
                            ins = pe.transpose(quarters(B[5 - b])[:, k, :], h, ident)
                        ins.then_inc(run.hT_ps, 1)

                if run.window == 0:
                    gather(0)
                    for step in range(E + 2):
                        if step < E:
                            first_product(step)
                        if step >= 2:
                            weighted_sum(step - 2)
                        if step + 1 < E:
                            gather(step + 1)
                        if 1 <= step <= E:
                            second_product(step - 1)
                        if step < E:
                            turn_h(step)
                        if step == 0:
                            biases(run.layer + 1)
                    return
                pe.wait_ge(gate["more"], run.layer + 1)
                number = pe.value_load(more_i[run.layer][0:1, 0:1], min_val=0, max_val=MORE)
                for job in range(MORE):
                    with pe.If(number > job):
                        gather(job)
                        first_product(job)
                        turn_h(job)
                        second_product(job)
                        weighted_sum(job)

            pe.wait_ge(layer_done, 1)
            gating(1)
            experts(ffn)
            experts(ffn_more)

            pe.wait_ge(layer_done, 2)
            turn_x(2)
            q = CHUNK[("gnn", "W1")]
            pe.wait_ge(xt_sb, 4 * NT)
            has_chunk(lo_cut, q)
            for n in range(NT):
                for k in range(KB):
                    ins = mm3(B[2 + n][:, :], g1_xT_hi[:, n, k, :], g1_xT_lo[:, n, k, :],
                              whi[q % SPL][:, k, :], wlo[q % SPL][:, k, :], k == 0, k == KB - 1)
                ins.then_inc(g1["a_ps"] if n == 0 else chunk_used, 1)
            pe.wait_ge(g1["rows"], 2)
            pe.wait_ge(g1["gsel"], 1)
            for g in range(3):
                q = CHUNK[("gnn", "Whh", g)]
                has_chunk(lo_cut, q)
                for n in range(NT):
                    ps = B[(6, 2, 6)[g] + n]
                    if g == 1:
                        pe.wait_ge(g1["a_sb"], n + 1)
                    if g == 2:
                        pe.wait_ge(g1["gh_sb"], n + 1)
                    pe.matmul(ps[:, :], gsel[:, 0 if g < 2 else 1, :], gb_rows[:, g * D:(g + 1) * D],
                              start=True, stop=False)
                    for k in range(KB):
                        ins = mm3(ps[:, :], g1_xT_hi[:, n, k, :], g1_xT_lo[:, n, k, :],
                                  whi[q % SPL][:, k, :], wlo[q % SPL][:, k, :], False, k == KB - 1)
                    ins.then_inc(g1["gh_ps"] if n == 0 else chunk_used, 1)

            pe.wait_ge(g1["w1e_lo"], 1)

            def edge_product(t):
                g, j = t // GRP, t % GRP
                if j == 0:
                    pe.wait_ge(g1["ea_lo"], g + 1)
                if t >= 3:
                    pe.wait_ge(g1["mp"], t - 2)
                elif t == 0:
                    pe.wait_ge(g1["gh_sb"], 2 * NT)
                mm3(B[2 + t % 3][:, :], ea_hi[:, g % 2, j * P:(j + 1) * P],
                    ea_lo[:, g % 2, j * P:(j + 1) * P], w1e_hi[:, :], w1e_lo[:, :], True, True)\
                    .then_inc(g1["e_ps"], 1)

            def edge_sum(t):
                pe.wait_ge(g1["m_lo"], t + 1)
                pe.wait_ge(g1["hot_odd"] if t % 2 else g1["hot_even"], t // 2 + 1)
                for n in range(NT):
                    lhs = onehot[:, t % 4, n * P:(n + 1) * P]
                    pe.matmul(B[n][:, :], lhs, m_hi[:, t % 2, :], start=t == 0, stop=False)
                    ins = pe.matmul(B[n][:, :], lhs, m_lo[:, t % 2, :], start=False, stop=t == ET - 1)
                ins.then_inc(g1["sum_ps"], 1)

            for t in range(ET):
                edge_product(t)
                if t >= 2:
                    edge_sum(t - 2)
            edge_sum(ET - 2)
            edge_sum(ET - 1)
            for n in range(NT):
                pe.wait_ge(g1["s1"], n + 1)
                for k in range(KB):
                    ins = pe.transpose(quarters(B[6 + n])[:, k, :], S1[:, n, k * P:(k + 1) * P], ident)
                ins.then_inc(g1["s1T_ps"], 1)
            pe.wait_ge(g1["aT"], 2 * NT)
            q = CHUNK[("gnn", "W2")]
            has_chunk(lo_cut, q)
            for n in range(NT):
                for k in range(KB):
                    ins = mm3(B[2 + n][:, :], aT_hi[:, n, k, :], aT_lo[:, n, k, :],
                              whi[q % SPL][:, k, :], wlo[q % SPL][:, k, :], k == 0, k == KB - 1)
                ins.then_inc(g1["agg_ps"] if n == 0 else chunk_used, 1)
            for n in range(NT):
                pe.wait_ge(g1["agg"], n + 1)
                for k in range(KB):
                    ins = pe.transpose(quarters(B[6 + n])[:, k, :], agg[:, n, k * P:(k + 1) * P], ident)
                ins.then_inc(g1["aggT_ps"], 1)
            pe.wait_ge(g1["aT"], 4 * NT)
            for g in range(3):
                q = CHUNK[("gnn", "Wih", g)]
                has_chunk(lo_cut, q)
                for n in range(NT):
                    ps = B[2 * g + n]
                    if g == 2:
                        pe.matmul(ps[:, :], gsel[:, 2, :], gb_rows[:, g * D:(g + 1) * D], start=True, stop=False)
                    for k in range(KB):
                        ins = mm3(ps[:, :], aT_hi[:, n, k, :], aT_lo[:, n, k, :],
                                  whi[q % SPL][:, k, :], wlo[q % SPL][:, k, :], g < 2 and k == 0, k == KB - 1)
                    ins.then_inc(g1["gi_ps"] if n == 0 else chunk_used, 1)

            pe.wait_ge(layer_done, 3)
            gating(2)
            experts(lstm)
            experts(lstm_more)


def kernel(**inputs):
    import numpy as _np
    import concourse.bacc as _bacc
    from concourse import mybir as _mybir
    from concourse.bass_utils import run_bass_kernel_spmd as _run

    a = {k: _np.asarray(v) for k, v in inputs.items()}

    W1T, W2T, WihT, WhhT = (a["L1_gnn_" + n].T for n in ("W1", "W2", "W_ih", "W_hh"))

    def block(w, r, c):
        return w[r * C:(r + 1) * C, c * C:(c + 1) * C]

    def matrix(key):
        kind = key[0]
        if kind == "L0":
            return a["L0_gnn_W"]
        if kind == "ffn":
            return block(a["L0_ffn_we1"][key[2]], 0, key[3]) if key[1] == "in" else \
                block(a["L0_ffn_we2"][key[2]], key[3], 0)
        if kind == "lstm":
            return block(a["L1_ffn_Wi"][key[2]], 0, (0, 2, 3)[key[3]]) if key[1] == "in" else \
                a["L1_ffn_Wo"][key[2]]
        if key[1] == "W1":
            return W1T[0:D, :]
        if key[1] == "W2":
            return W2T
        return block(WhhT if key[1] == "Whh" else WihT, 0, key[2])

    b = a["L1_ffn_b"]
    arrays = {
        "x": a["x"],
        "src": a["src"].reshape(ET, P).T,
        "dst": a["dst"].reshape(ET, P).T,
        "ea": a["edge_attr_128"].T,
        "w1e": W1T[D:, :],
        "weights": _np.stack([matrix(k).reshape(KB, P, C).transpose(1, 0, 2) for k in STORE]),
        "L0_ffn_gb1": a["L0_ffn_gb1"].reshape(2, P).T,
        "lstm_b": _np.concatenate([b[:, 0:D], b[:, 2 * D:3 * D], b[:, 3 * D:4 * D]], axis=1),
        "L1_gnn_b_ih": a["L1_gnn_b_ih"].reshape(1, 3 * D),
        "L1_gnn_b_hh": a["L1_gnn_b_hh"].reshape(1, 3 * D),
    }
    for n in ("L0_gnn_b", "L0_gnn_diffusion_weights", "L0_ffn_gw1", "L0_ffn_gw2", "L0_ffn_gb2",
              "L0_ffn_be1", "L0_ffn_be2", "L1_gnn_b1", "L1_gnn_b2", "L1_gnn_gamma", "L1_gnn_beta",
              "L1_gnn_run_mean", "L1_gnn_run_var", "L1_ffn_router_w", "L1_ffn_router_b", "L1_ffn_bo"):
        arrays[n] = a[n]
    arrays = {f"in_{n}_dram": _np.ascontiguousarray(v) for n, v in arrays.items()}

    nc = _bacc.Bacc("TRN2", target_bir_lowering=False, num_devices=1)
    aps = {n[3:-5]: nc.dram_tensor(n, v.shape, _mybir.dt.from_np(v.dtype), kind="ExternalInput").ap()
           for n, v in arrays.items()}
    out = nc.dram_tensor("out_0_dram", (T, D), _mybir.dt.float32, kind="ExternalOutput").ap()
    node_rows = nc.dram_tensor("node_rows", (T, D), _mybir.dt.float32).ap()
    build(nc, aps, out, node_rows)
    r = _run(nc, [arrays], core_ids=[0])
    return r.results[0]["out_0_dram"]
```

```python
import numpy as np
import concourse.bass as bass
from concourse import mybir
from contextlib import ExitStack

P = 128
T = 256
NT = T // P
D = 512
KB = D // P
E = 8
MORE = 2 * T // (P + 1)
EDGES = 4352
ET = EDGES // P
C = 512
EPS = 1e-5
RAW = 4
SPL = 4
HOT0 = 16
GRP = 4
NG = -(-ET // GRP)
HOT1 = 5
GATH = 5
SUMS = 2
MSG = 3
EAHEAD = 4
EBANKS = 6

FFN_IN, FFN_OUT = 2, 2
LSTM_IN, LSTM_OUT = 3, 1


def moe_order(layer, n_in, n_out):
    order = []
    for step in range(E + 1):
        if step < E:
            order += [(layer, "in", step, c) for c in range(n_in)]
        if step >= 1:
            order += [(layer, "out", step - 1, c) for c in range(n_out)]
    return order


FFN_ORDER = moe_order("ffn", FFN_IN, FFN_OUT)
LSTM_ORDER = moe_order("lstm", LSTM_IN, LSTM_OUT)
EC = FFN_IN + FFN_OUT
GNN_ORDER = [("gnn", "W1")] + [("gnn", "Whh", g) for g in range(3)] + [("gnn", "W2")] \
    + [("gnn", "Wih", g) for g in range(3)]
ORDER = [("L0", "W")] + FFN_ORDER + GNN_ORDER + LSTM_ORDER
CHUNK = {key: n for n, key in enumerate(ORDER)}


def moe_store(layer, n_in):
    return [(layer, "in", e, c) if c < n_in else (layer, "out", e, c - n_in)
            for e in range(E) for c in range(EC)]


STORE = [("L0", "W")] + moe_store("ffn", FFN_IN) + GNN_ORDER + moe_store("lstm", LSTM_IN)
PLACE = {key: n for n, key in enumerate(STORE)}


def build(nc, A, out, node_rows):
    f32, f32r, bf16, i32, u32 = (mybir.dt.float32, mybir.dt.float32r, mybir.dt.bfloat16,
                                 mybir.dt.int32, mybir.dt.uint32)
    ALU = mybir.AluOpType
    ACT = mybir.ActivationFunctionType
    AX = mybir.AxisListType.X

    ctx = ExitStack()
    with ctx:
        def sb(name, shape, dt=f32, stack=ctx):
            return stack.enter_context(nc.sbuf_tensor(name, shape, dt))

        def sem(name):
            return ctx.enter_context(nc.semaphore(name))

        raw = [sb(f"raw{i}", [P, KB, C]) for i in range(RAW)]
        whi = [sb(f"whi{i}", [P, KB, C], f32r) for i in range(SPL)]
        wlo = [sb(f"wlo{i}", [P, KB, C], f32r) for i in range(SPL)]
        x = sb("x", [P, NT, D])
        xn = sb("xn", [P, NT, D])
        xnT = sb("xnT", [P, NT, KB, P])
        iota_t = sb("iota_t", [P, T])
        node_id = sb("node_id", [P, NT])
        eye2 = sb("eye2", [P, NT, T])
        ident = eye2[:, 0, 0:P]
        src_i = sb("src_i", [P, ET], i32)
        dst_i = sb("dst_i", [P, ET], i32)
        dst_f = sb("dst_f", [P, ET])
        deg = sb("deg", [P, NT])
        stats = sb("stats", [P, NT, 6])
        mv = sb("mv", [P, NT, 2])
        rstd = sb("rstd", [P, NT])
        var_eps = sb("var_eps", [P, NT])
        minus_half = sb("minus_half", [P, NT])
        iota_b = sb("iota_b", [P, T], bf16)
        more_i = [sb(f"more_i{i}", [P, 1 + MORE], i32) for i in range(2)]
        rw = sb("rw", [P, KB, E])
        gb = sb("gb", [P, 2, E])

        with ExitStack() as st:
            g0_src_f = sb("g0_src_f", [P, ET], f32, st)
            g0_S = sb("g0_S", [P, HOT0, T], bf16, st)
            g0_D = sb("g0_D", [P, HOT0, T], bf16, st)
            g0_cnt = sb("g0_cnt", [P, NT, T], f32, st)
            g0_sum = sb("g0_sum", [P, NT, T], f32, st)
            g0_adj = sb("g0_adj", [P, NT, T], f32r, st)
            g0_rs = sb("g0_rs", [P, NT], f32, st)
            g0_rinv = sb("g0_rinv", [P, NT], f32, st)
            g0_xT_hi = sb("g0_xT_hi", [P, NT, KB, P], f32r, st)
            g0_xT_lo = sb("g0_xT_lo", [P, NT, KB, P], f32r, st)
            g0_h = sb("g0_h", [P, NT, D], f32, st)
            g0_cur = sb("g0_cur", [P, NT, D], f32, st)
            g0_wh = sb("g0_wh", [P, 3, NT, D], f32, st)
            g0_hi = sb("g0_hi", [P, NT, D], f32r, st)
            g0_lo = sb("g0_lo", [P, NT, D], f32r, st)
            g0_b = sb("g0_b", [P, D], f32, st)
            g0_w = sb("g0_w", [P, 4], f32, st)
        with ExitStack() as st:
            xn_hi = sb("xn_hi", [P, NT, D], f32r, st)
            xn_lo = sb("xn_lo", [P, NT, D], f32r, st)
            xe_hi = sb("xe_hi", [P, KB, P], f32r, st)
            xe_lo = sb("xe_lo", [P, KB, P], f32r, st)
            act3 = sb("act3", [P, 3, C], f32, st)
            hT_hi = sb("hT_hi", [P, 2 * KB, P], f32r, st)
            hT_lo = sb("hT_lo", [P, 2 * KB, P], f32r, st)
            y_hi = sb("y_hi", [P, D], f32r, st)
            y_lo = sb("y_lo", [P, D], f32r, st)
            G = sb("G", [P, 2, NT, P], f32r, st)
            GT = sb("GT", [P, 3, T], f32r, st)
            wslot = sb("wslot", [P, 3], f32, st)
            sel_v = sb("sel_v", [2 * E, E, P], f32, st)
            sel_a = sb("sel_a", [2 * E, E, P], f32, st)
            sel = sb("sel", [2 * E, E, P], f32r, st)
            b_hi = sb("b_hi", [2 * E, 3 * C], f32r, st)
            b_rows = sb("b_rows", [2 * E, 3 * C], f32r, st)
            alpha = sb("alpha", [2 * E, 1], f32, st)
            hid = sb("hid", [P, 2, T], f32, st)
            lg = sb("lg", [P, NT, E], f32, st)
            pr = sb("pr", [P, NT, E], f32, st)
            red = sb("red", [P, NT], f32, st)
            red2 = sb("red2", [P, NT], f32, st)
            top = sb("top", [P, NT, 8], f32, st)
            topi = sb("topi", [P, NT, 8], u32, st)
            topf = sb("topf", [P, NT, 8], f32, st)
            tw = sb("tw", [P, NT, 4], f32, st)
            oh = sb("oh", [P, NT, 2, E], f32, st)
            mask = sb("mask", [P, NT, E], f32, st)
            comb = sb("comb", [P, NT, E], f32, st)
            combT = sb("combT", [E, T], f32, st)
            posm = sb("posm", [P, NT, E], f32, st)
            penal = sb("penal", [P, NT, E], f32, st)
            tri = sb("tri", [P, T], f32, st)
            over = sb("over", [P, E], f32, st)
            rank = sb("rank", [P, E], f32, st)
            picked = sb("picked", [P, MORE, E], f32, st)
            prod = sb("prod", [P, 2 * NT, E], f32, st)
            ids = sb("ids", [P, 1 + MORE], f32, st)
            more_pc = sb("more_pc", [P, MORE, 2 * NT], f32, st)
            sel_m = sb("sel_m", [2 * E, 2, P], f32, st)
            sel_more = sb("sel_more", [2 * E, MORE, P], f32r, st)
            b_raw = sb("b_raw", [2 * E, 3 * C], f32, st)
            b_out = sb("b_out", [E, D], f32, st)
            gw1 = sb("gw1", [P, KB, 256], f32, st)
            gb1 = sb("gb1", [P, 2], f32, st)
            gw2 = sb("gw2", [P, 2, E], f32, st)
        with ExitStack() as st:
            g1_xT_hi = sb("g1_xT_hi", [P, NT, KB, P], f32r, st)
            g1_xT_lo = sb("g1_xT_lo", [P, NT, KB, P], f32r, st)
            A_sb = sb("A_sb", [P, NT, D], f32, st)
            gh = sb("gh", [P, NT, 3, D], f32, st)
            w1e_hi = sb("w1e_hi", [P, D], f32r, st)
            w1e_lo = sb("w1e_lo", [P, D], f32r, st)
            onehot = sb("onehot", [P, HOT1, T], f32r, st)
            gb_rows = sb("gb_rows", [4, 3 * D], f32r, st)
            gsel = sb("gsel", [4, 3, P], f32r, st)
            galpha = sb("galpha", [4, 1], f32, st)
            with ExitStack() as st2:
                ea = sb("ea", [P, 3, GRP * P], f32, st2)
                ea_hi = sb("ea_hi", [P, 2, GRP * P], f32r, st2)
                ea_lo = sb("ea_lo", [P, 2, GRP * P], f32r, st2)
                gath = sb("gath", [P, GATH, D], f32, st2)
                mp = sb("mp", [P, SUMS, D], f32, st2)
                m_hi = sb("m_hi", [P, MSG, D], f32r, st2)
                m_lo = sb("m_lo", [P, MSG, D], f32r, st2)
            with ExitStack() as st2:
                pad = sb("pad0", [P, 7, GRP * P], f32, st2)
                gb_raw = sb("gb_raw", [4, 3 * D], f32, st2)
                g1_it = sb("g1_it", [4, 3, P], f32, st2)
                g1_t = sb("g1_t", [4, 3, P], f32, st2)
            with ExitStack() as st2:
                S1 = sb("S1", [P, NT, D], f32, st2)
                agg = sb("agg", [P, NT, D], f32, st2)
                aT_hi = sb("aT_hi", [P, NT, KB, P], f32r, st2)
                aT_lo = sb("aT_lo", [P, NT, KB, P], f32r, st2)
                rz = sb("rz", [P, NT, 3, D], f32, st2)
            edge_space = sb("edge_space", [P, 40 * 256], f32, st)
            w1e = sb("w1e", [P, D], f32, st)
            g2s = sb("g2s", [P, D], f32, st)
            g2b = sb("g2b", [P, D], f32, st)
            g2m = sb("g2m", [P, D], f32, st)
            g2v = sb("g2v", [P, D], f32, st)
            b1 = sb("b1", [P, D], f32, st)
            b2 = sb("b2", [P, D], f32, st)

        B = [ctx.enter_context(nc.psum_tensor(f"bank{i}", [P, C], f32)) for i in range(8)]

        def quarters(bank):
            return bank[:, :].rearrange("p (k t) -> p k t", k=KB)

        def diffusion_bank(step, n):
            return 2 + NT * (step % 2) + n

        raw_in = [sem(f"raw_in{i}") for i in range(RAW)]
        hi_cut = sem("hi_cut")
        lo_cut = sem("lo_cut")
        chunk_used = sem("chunk_used")
        layer_done = sem("layer_done")
        x_in, idx_in, par0, par1, par2, par3 = (sem(n) for n in (
            "x_in", "idx_in", "par0", "par1", "par2", "par3"))
        PAR1 = (16 * 9, 16 * 12)
        iota_ok = sem("iota_ok")
        half_ok = sem("half_ok")
        var_ok = sem("var_ok")
        rstd_ok = sem("rstd_ok")
        consts_ok = sem("consts_ok")
        xn_ok = sem("xn_ok")
        xt_ps = sem("xt_ps")
        xt_sb = sem("xt_sb")
        dve_chain = sem("dve_chain")
        act_chain = sem("act_chain")

        class Chain:

            def __init__(self, eng, s):
                self.eng, self.s, self.n = eng, s, 0

            def __call__(self, ins):
                self.n += 1
                ins.then_inc(self.s, 1)
                self.eng.wait_ge(self.s, self.n)

        def both_tiles(eng, n, first_tile, value, chunk):
            if n == 0:
                eng.wait_ge(first_tile, value)
            else:
                eng.wait_ge(chunk_used, chunk + 1)

        class Run:
            def __init__(self, name, layer):
                self.layer = layer
                self.n_in, self.n_out = (FFN_IN, FFN_OUT) if layer == 0 else (LSTM_IN, LSTM_OUT)
                self.order = FFN_ORDER if layer == 0 else LSTM_ORDER
                self.at = {key: n for n, key in enumerate(self.order)}
                self.tag = "ffn" if layer == 0 else "lstm"
                self.g_built = sem(f"{name}_g_built")
                self.gather_ps = sem(f"{name}_gather_ps")
                self.turn_ps = sem(f"{name}_turn_ps")
                self.xe_cut = sem(f"{name}_xe_cut")
                self.gt_sb = sem(f"{name}_gt_sb")
                self.gates = sem(f"{name}_gates")
                self.h_ok = sem(f"{name}_h_ok")
                self.hT_ps = sem(f"{name}_hT_ps")
                self.hT_hi = sem(f"{name}_hT_hi")
                self.hT_lo = sem(f"{name}_hT_lo")
                self.y_cut = sem(f"{name}_y_cut")
                self.sum_ps = sem(f"{name}_sum_ps")
                self.banks_h = 2 if layer == 0 else 1
                self.base = CHUNK[self.order[0]]
                self.end = self.base + len(self.order)
                self.more_in = [sem(f"{name}_more_in{i}") for i in range(RAW)]
                self.more_hi, self.more_lo, self.more_used = (sem(f"{name}_{n}") for n in (
                    "more_hi", "more_lo", "more_used"))

            def chunk(self, kind, e, c):
                if e >= E:
                    return self.end + EC * (e - E) + (c if kind == "in" else self.n_in + c)
                return self.base + self.at[(self.tag, kind, e, c)]

            def used(self, q):
                return (chunk_used, q + 1) if q < self.end else (self.more_used, q - self.end + 1)

            def lo(self, q):
                return (lo_cut, q + 1) if q < self.end else (self.more_lo, q - self.end + 1)

            def last_in(self, e):
                return self.chunk("in", e, self.n_in - 1)

            def last_out(self, e):
                return self.chunk("out", e, self.n_out - 1)

        ffn, lstm = Run("ffn", 0), Run("lstm", 1)
        gate = {n: sem(f"gate_{n}") for n in (
            "hid_ps", "hid_sb", "lg_ps", "shift", "exp", "d", "dexp", "mask", "pos_ps", "route",
            "combT", "more", "xn_cut", "par")}

        g0 = {n: sem(f"g0_{n}") for n in ("hot", "used", "cnt", "turn_ps", "adj", "h_ps",
                                          "cur", "cut", "lo", "ps", "xT_hi", "wh")}
        more_chain = [sem("ffn_more_chain"), sem("lstm_more_chain")]
        g1 = {n: sem(f"g1_{n}") for n in (
            "a_ps", "a_sb", "a_out", "gh_ps", "gh_sb", "w1e_hi", "w1e_lo", "ea_hi", "ea_lo", "e_ps",
            "mp", "m_hi", "m_lo", "hot_even", "hot_odd", "sum_ps", "s1", "s1T_ps", "aT", "agg_ps", "agg", "aggT_ps",
            "gi_ps", "rz_in", "rz", "n_in", "n", "rows", "bn", "gsel")}
        ea_in = [sem(f"g1_ea_in{i}") for i in range(3)]
        gath_in = [sem(f"g1_gath_in{i}") for i in range(GATH)]
        out_done = sem("out_done")

        block = ctx.enter_context(nc.Block())

        weights = A["weights"]

        @block.sync
        def _(sp):
            sp.dma_start(x[:, :, :], A["x"].rearrange("(n p) d -> p n d", p=P)).then_inc(x_in, 16)
            sp.dma_start(src_i[:, :], A["src"]).then_inc(idx_in, 16)
            sp.dma_start(dst_i[:, :], A["dst"]).then_inc(idx_in, 16)

            def load(n, former_cut, arrived, source):
                if former_cut:
                    sp.wait_ge(*former_cut)
                sp.dma_start(raw[n % RAW][:, :, :], source).then_inc(arrived, 16)

            def main(keys):
                for key in keys:
                    n = CHUNK[key]
                    load(n, (lo_cut, n - RAW + 1) if n >= RAW else None, raw_in[n % RAW],
                         weights[PLACE[key], :, :, :])

            def more(run):
                sp.wait_ge(gate["more"], run.layer + 1)
                table = more_i[run.layer]
                number = sp.value_load(table[0:1, 0:1], min_val=0, max_val=MORE)
                for job in range(MORE):
                    with sp.If(number > job):
                        expert = sp.value_load(table[0:1, 1 + job:2 + job], min_val=0, max_val=E - 1)
                        for c in range(EC):
                            q = EC * job + c
                            first = PLACE[(run.tag, "in", 0, 0)] + c
                            load(run.end + q, run.lo(run.end + q - RAW), run.more_in[q % RAW],
                                 weights[bass.ds(expert * EC + first, 1), :, :, :]
                                 .rearrange("a p k c -> (a p) k c"))
                for job in range(MORE):
                    with sp.If(number > job):
                        sp.wait_ge(run.more_lo, EC * (job + 1))

            def edge_attr(g):
                if g >= 3:
                    sp.wait_ge(g1["ea_hi"], g - 2)
                    sp.wait_ge(g1["ea_lo"], g - 2)
                n = min(GRP, ET - g * GRP) * P
                sp.dma_start(ea[:, g % 3, 0:n], A["ea"][:, g * GRP * P:g * GRP * P + n]).then_inc(ea_in[g % 3], 16)

            main([("L0", "W")] + FFN_ORDER)
            more(ffn)
            main(GNN_ORDER[0:4])
            sp.wait_ge(layer_done, 2)
            for g in range(3):
                edge_attr(g)
            main(GNN_ORDER[4:8])
            for g in range(3, NG):
                edge_attr(g)
            main(LSTM_ORDER)
            more(lstm)
            sp.wait_ge(layer_done, 4)
            sp.dma_start(out.rearrange("(n p) d -> p n d", p=P), x[:, :, :]).then_inc(out_done, 16)
            sp.wait_ge(out_done, 16)

        @block.gpsimd
        def _(pool):
            pool.iota(iota_t[:, :], [[1, T]], base=0, channel_multiplier=0,
                      allow_small_or_imprecise_dtypes=True).then_inc(iota_ok, 1)
            pool.iota(node_id[:, :], [[P, NT]], base=0, channel_multiplier=1,
                      allow_small_or_imprecise_dtypes=True).then_inc(iota_ok, 1)
            pool.dma_start(g0_b[:, :], A["L0_gnn_b"].partition_broadcast(P)).then_inc(par0, 16)
            pool.dma_start(g0_w[:, :], A["L0_gnn_diffusion_weights"].partition_broadcast(P)).then_inc(par0, 16)

            pool.memset(minus_half[:, :], -0.5).then_inc(half_ok, 1)
            pool.wait_ge(half_ok, 1)

            def root(layer):
                pool.wait_ge(var_ok, layer + 1)
                pool.tensor_tensor(rstd[:, :], var_eps[:, :], minus_half[:, :], ALU.pow).then_inc(rstd_ok, 1)

            root(0)

            def moe_params(b_in, b_o):
                n = b_in.shape[1]
                pool.dma_start(b_raw[0:E, 0:n], b_in).then_inc(par1, 16)
                pool.dma_start(b_raw[E:2 * E, 0:n], b_in).then_inc(par1, 16)
                pool.dma_start(b_out[:, :], b_o).then_inc(par1, 16)

            for nth, name in enumerate(("L0_ffn_gb2", "L1_ffn_router_b")):
                pool.dma_start(gb[:, nth, :], A[name].partition_broadcast(P)).then_inc(par1, 16)
            pool.dma_start(rw[:, :, :], A["L1_ffn_router_w"].rearrange("(k p) n -> p k n", p=P)).then_inc(par1, 16)
            pool.dma_start(gw1[:, :, :], A["L0_ffn_gw1"].rearrange("(k p) n -> p k n", p=P)).then_inc(par1, 16)
            pool.dma_start(gb1[:, :], A["L0_ffn_gb1"]).then_inc(par1, 16)
            pool.dma_start(gw2[:, :, :], A["L0_ffn_gw2"].rearrange("(k p) n -> p k n", p=P)).then_inc(par1, 16)
            moe_params(A["L0_ffn_be1"], A["L0_ffn_be2"])
            root(1)
            pool.wait_ge(layer_done, 1)
            pool.iota(sel_v[:, :, :], [[-1, E], [0, P]], base=0, channel_multiplier=1,
                      allow_small_or_imprecise_dtypes=True).then_inc(gate["par"], 1)

            pool.dma_start(w1e[:, :], A["w1e"]).then_inc(par2, 16)
            for dst, name in ((b1, "b1"), (g2v, "run_var"), (b2, "b2"), (g2s, "gamma"),
                              (g2b, "beta"), (g2m, "run_mean")):
                pool.dma_start(dst[:, :], A["L1_gnn_" + name].partition_broadcast(P)).then_inc(par2, 16)
            root(2)
            for r in range(4):
                pool.dma_start(gb_raw[r:r + 1, :], A["L1_gnn_b_ih" if r % 2 == 0 else "L1_gnn_b_hh"]).then_inc(par3, 16)
            pool.iota(g1_it[:, :, :], [[0, 3], [0, P]], base=0, channel_multiplier=1,
                      allow_small_or_imprecise_dtypes=True).then_inc(gate["par"], 1)

            for n in range(NT):
                pool.wait_ge(g1["a_sb"], n + 1)
                pool.dma_start(node_rows[n * P:(n + 1) * P, :], A_sb[:, n, :]).then_inc(g1["a_out"], 16)

            def hot(t):
                if t >= HOT1:
                    pool.wait_ge(g1["sum_ps"], t - HOT1 + 1)
                pool.tensor_scalar(onehot[:, t % HOT1, :], iota_t[:, :], dst_f[:, t:t + 1], None,
                                   ALU.is_equal).then_inc(g1["hot_even"], 1)

            pool.wait_ge(g1["rows"], 2)
            pool.wait_ge(g1["a_out"], 16 * NT)
            for t in range(ET):
                if t >= GATH:
                    pool.wait_ge(g1["mp"], t - GATH + 1)
                pool.indirect_dma_start(
                    out=gath[:, t % GATH, :], out_offset=None, in_=node_rows[:, :],
                    in_offset=bass.IndirectOffsetOnAxis(ap=src_i[:, t:t + 1], axis=0)).then_inc(gath_in[t % GATH], 16)
                if t >= 1 and t % 2:
                    hot(t - 1)

            pool.wait_ge(layer_done, 3)
            moe_params(A["lstm_b"], A["L1_ffn_bo"])
            root(3)
            pool.iota(sel_v[:, :, :], [[-1, E], [0, P]], base=0, channel_multiplier=1,
                      allow_small_or_imprecise_dtypes=True).then_inc(gate["par"], 1)

        @block.scalar
        def _(act):
            def cut_hi(n):
                act.wait_ge(raw_in[n % RAW], 16 * (n // RAW + 1))
                if n >= SPL:
                    act.wait_ge(chunk_used, n - SPL + 1)
                act.activation(whi[n % SPL][:, :, :], raw[n % RAW][:, :, :], ACT.Copy).then_inc(hi_cut, 1)

            def more_hi(run, q):
                act.wait_ge(run.more_in[(q - run.end) % RAW], 16 * ((q - run.end) // RAW + 1))
                act.wait_ge(*run.used(q - SPL))
                act.activation(whi[q % SPL][:, :, :], raw[q % RAW][:, :, :], ACT.Copy)\
                   .then_inc(run.more_hi, 1)

            done = [0]

            def cut_to(n):
                while done[0] < n:
                    cut_hi(done[0])
                    done[0] += 1

            def xT_copy(layer, dst):
                for n in range(NT):
                    act.wait_ge(xt_ps, NT * layer + n + 1)
                    act.activation(dst[:, n, :, :], quarters(B[5 - n]), ACT.Copy).then_inc(xt_sb, 1)

            def experts(run):
                def cuts(upto):
                    cut_to(min(upto, run.base + len(run.order)))

                def xe(e):
                    act.wait_ge(run.gather_ps, e + 1)
                    act.activation(xe_hi[:, :, :], quarters(B[6]), ACT.Copy).then_inc(run.xe_cut, 1)

                def outputs(e):
                    act.wait_ge(*run.used(run.last_out(e)))
                    act.wait_ge(run.gt_sb, e + 1)
                    act.activation(y_hi[:, :], B[7][:, :], ACT.Copy,
                                   scale=wslot[:, e % 3:e % 3 + 1]).then_inc(run.y_cut, 1)

                def turned(e):
                    for b in range(run.banks_h):
                        act.wait_ge(run.hT_ps, run.banks_h * e + b + 1)
                        act.activation(hT_hi[:, KB * b:KB * b + KB, :], quarters(B[5 - b]),
                                       ACT.Copy).then_inc(run.hT_hi, 1)

                def results(e):
                    if run.layer == 0:
                        for c in range(2):
                            act.wait_ge(*run.used(run.chunk("in", e, c)))
                            act.activation(act3[:, c, :], B[2 + c][:, :], ACT.Gelu).then_inc(run.h_ok, 1)
                        return
                    for c, f in ((0, ACT.Sigmoid), (1, ACT.Tanh), (2, ACT.Sigmoid)):
                        act.wait_ge(*run.used(run.chunk("in", e, c)))
                        act.activation(act3[:, c, :], B[2 + c][:, :], f).then_inc(run.gates, 1)
                    act.wait_ge(run.h_ok, 2 * e + 1)
                    act.activation(act3[:, 1, :], act3[:, 0, :], ACT.Tanh).then_inc(run.gates, 1)

                def more_cuts(first, upto):
                    for q in range(max(first, run.end), upto):
                        more_hi(run, q)

                cuts(run.base + SPL)
                xe(0)
                for step in range(E):
                    if step >= 2:
                        outputs(step - 2)
                    if step >= 1:
                        turned(step - 1)
                    if step >= 2:
                        cuts(run.last_out(step - 2) + SPL + 1)
                    results(step)
                    if step + 1 < E:
                        xe(step + 1)
                    cuts(run.last_in(step) + SPL + 1)
                act.wait_ge(gate["more"], run.layer + 1)
                number = act.value_load(more_i[run.layer][0:1, 0:1], min_val=0, max_val=MORE)
                outputs(E - 2)
                turned(E - 1)
                with act.If(number > 0):
                    more_cuts(run.end, run.last_out(E - 2) + SPL + 1)
                    xe(E)
                outputs(E - 1)
                for e in range(E, E + MORE):
                    with act.If(number > e - E):
                        more_cuts(run.last_out(E - 2) + SPL + 1 if e == E else run.chunk("out", e, 0),
                                  run.last_out(e) + 1)
                        results(e)
                    if e + 1 < E + MORE:
                        with act.If(number > e + 1 - E):
                            xe(e + 1)
                    with act.If(number > e - E):
                        turned(e)
                    if e + 1 < E + MORE:
                        with act.If(number > e + 1 - E):
                            more_cuts(run.chunk("in", e + 1, 0), run.last_in(e + 1) + 1)
                    with act.If(number > e - E):
                        outputs(e)

            cut_to(1)
            for n in range(NT):
                act.wait_ge(xt_ps, n + 1)
                act.activation(g0_xT_hi[:, n, :, :], quarters(B[5 - n]), ACT.Copy).then_inc(g0["xT_hi"], 1)
            cut_to(2)
            for i in range(3):
                for n in range(NT):
                    act.wait_ge(g0["cur"], NT * i + n + 1)
                    act.activation(g0_hi[:, n, :], g0_cur[:, n, :], ACT.Copy).then_inc(g0["cut"], 1)
                if i == 0:
                    for n in range(NT):
                        for j in range(3):
                            act.activation(g0_wh[:, j, n, :], g0_h[:, n, :], ACT.Copy,
                                           scale=g0_w[:, 2 - j:3 - j]).then_inc(g0["wh"], 1)
                    cut_to(4)

            def gating(nth):
                act.wait_ge(xn_ok, NT * (2 * nth - 1) + NT)
                act.activation(xn_hi[:, :, :], xn[:, :, :], ACT.Copy).then_inc(gate["xn_cut"], 1)
                xT_copy(2 * nth - 1, xnT)
                act.wait_ge(par1, PAR1[nth - 1])
                n = 2 * C if nth == 1 else 3 * C
                act.activation(b_hi[:, 0:n], b_raw[:, 0:n], ACT.Copy).then_inc(gate["xn_cut"], 1)
                if nth == 1:
                    for b in range(2):
                        act.wait_ge(gate["hid_ps"], b + 1)
                        act.activation(hid[:, b, :], B[2 + b][:, 0:T],
                                       ACT.Relu, bias=gb1[:, b:b + 1]).then_inc(gate["hid_sb"], 1)
                    act.wait_ge(gate["shift"], NT)
                    act.activation(pr[:, :, :], lg[:, :, :], ACT.Exp).then_inc(gate["exp"], 1)
                act.wait_ge(gate["d"], nth)
                act.activation(tw[:, :, 1], tw[:, :, 0], ACT.Exp).then_inc(gate["dexp"], 1)

            gating(1)
            experts(ffn)

            first = CHUNK[("gnn", "W1")]
            cut_to(first + 2)
            for n in range(NT):
                act.wait_ge(xt_ps, 2 * NT + n + 1)
                act.activation(g1_xT_hi[:, n, :, :], quarters(B[5 - n]), ACT.Copy).then_inc(xt_sb, 1)
            act.wait_ge(par2, 16 * 7)
            act.activation(w1e_hi[:, :], w1e[:, :], ACT.Copy).then_inc(g1["w1e_hi"], 1)
            cut_to(first + 3)
            act.wait_ge(par3, 16 * 4)
            act.activation(gb_rows[:, :], gb_raw[:, :], ACT.Copy).then_inc(g1["rows"], 1)
            cut_to(first + SPL)

            def ea_cut(g):
                n = min(GRP, ET - g * GRP) * P
                act.wait_ge(ea_in[g % 3], 16 * (g // 3 + 1))
                if g >= 2:
                    act.wait_ge(g1["e_ps"], GRP * (g - 1))
                act.activation(ea_hi[:, g % 2, 0:n], ea[:, g % 3, 0:n], ACT.Copy).then_inc(g1["ea_hi"], 1)

            ea_cut(0)
            ea_cut(1)
            act.wait_ge(g1["bn"], 1)
            act.activation(g2v[:, :], g2v[:, :], ACT.Sqrt).then_inc(g1["bn"], 1)
            for n in range(SPL):
                cut_to(first + SPL + n + 1)
            for t in range(ET):
                act.wait_ge(g1["mp"], t + 1)
                if t >= MSG:
                    act.wait_ge(g1["sum_ps"], t - MSG + 1)
                act.activation(m_hi[:, t % MSG, :], mp[:, t % SUMS, :], ACT.Relu).then_inc(g1["m_hi"], 1)
                if t % GRP == 1 and t // GRP + 1 < NG and t >= GRP:
                    ea_cut(t // GRP + 1)
            for n in range(NT):
                act.wait_ge(g1["s1T_ps"], n + 1)
                act.activation(aT_hi[:, n, :, :], quarters(B[6 + n]), ACT.Copy).then_inc(g1["aT"], 1)
            for n in range(NT):
                act.wait_ge(g1["aggT_ps"], n + 1)
                act.activation(aT_hi[:, n, :, :], quarters(B[6 + n]), ACT.Copy).then_inc(g1["aT"], 1)
            for g in range(2):
                for n in range(NT):
                    act.wait_ge(g1["rz_in"], NT * g + n + 1)
                    act.activation(rz[:, n, g, :], rz[:, n, g, :], ACT.Sigmoid).then_inc(g1["rz"], 1)
            for n in range(NT):
                act.wait_ge(g1["n_in"], n + 1)
                act.activation(rz[:, n, 2, :], rz[:, n, 2, :], ACT.Tanh).then_inc(g1["n"], 1)

            cut_to(CHUNK[LSTM_ORDER[0]] + SPL)
            gating(2)
            experts(lstm)

        @block.vector
        def _(dve):
            link = Chain(dve, dve_chain)

            def cut_lo(n):
                dve.wait_ge(hi_cut, n + 1)
                dve.tensor_tensor(wlo[n % SPL][:, :, :], raw[n % RAW][:, :, :],
                                  whi[n % SPL][:, :, :].bitcast(f32), ALU.subtract).then_inc(lo_cut, 1)

            def more_lo(run, q):
                dve.wait_ge(run.more_hi, q - run.end + 1)
                dve.tensor_tensor(wlo[q % SPL][:, :, :], raw[q % RAW][:, :, :],
                                  whi[q % SPL][:, :, :].bitcast(f32), ALU.subtract).then_inc(run.more_lo, 1)

            done = [0]

            def cut_to(n):
                while done[0] < n:
                    cut_lo(done[0])
                    done[0] += 1

            def layernorm(layer):
                for n in range(NT):
                    link(dve.bn_stats(stats[:, n, :], x[:, n, :]))
                for n in range(NT):
                    link(dve.bn_aggr(mv[:, n, :], stats[:, n, :]))
                dve.tensor_scalar(var_eps[:, :], mv[:, :, 1], EPS, None, ALU.add).then_inc(var_ok, 1)
                dve.wait_ge(rstd_ok, layer + 1)
                for n in range(NT):
                    dve.tensor_scalar(xn[:, n, :], x[:, n, :], mv[:, n, 0:1], rstd[:, n:n + 1],
                                      ALU.subtract, ALU.mult).then_inc(xn_ok, 1)

            dve.wait_ge(iota_ok, 2)
            for n in range(NT):
                ins = dve.tensor_scalar(eye2[:, n, :], iota_t[:, :], node_id[:, n:n + 1], None, ALU.is_equal)
            link(ins)
            link(dve.tensor_copy(iota_b[:, :], iota_t[:, :]))
            dve.wait_ge(x_in, 16)
            layernorm(0)
            dve.wait_ge(idx_in, 32)
            dve.tensor_copy(g0_src_f[:, :], src_i[:, :]).then_inc(consts_ok, 1)
            dve.tensor_copy(dst_f[:, :], dst_i[:, :]).then_inc(consts_ok, 1)
            dve.wait_ge(consts_ok, 2)
            for n in range(NT):
                dve.wait_ge(g0["xT_hi"], n + 1)
                dve.tensor_tensor(g0_xT_lo[:, n, :, :], quarters(B[5 - n]),
                                  g0_xT_hi[:, n, :, :].bitcast(f32), ALU.subtract).then_inc(xt_sb, 1)
            cut_to(1)

            def edge_hots(first, last):
                for t in range(first, last):
                    if t >= HOT0:
                        dve.wait_ge(g0["used"], t - HOT0 + 1)
                    dve.tensor_scalar(g0_S[:, t % HOT0, :], iota_b[:, :], g0_src_f[:, t:t + 1], None,
                                      ALU.is_equal)
                    dve.tensor_scalar(g0_D[:, t % HOT0, :], iota_b[:, :], dst_f[:, t:t + 1], None,
                                      ALU.is_equal).then_inc(g0["hot"], 1)

            edge_hots(0, HOT0)
            dve.wait_ge(par0, 32)
            for n in range(NT):
                both_tiles(dve, n, g0["h_ps"], 1, 0)
                link(dve.tensor_tensor(g0_h[:, n, :], B[2 + n][:, :], g0_b[:, :], ALU.add))
                dve.tensor_scalar(g0_cur[:, n, :], g0_h[:, n, :], g0_w[:, 3:4], None,
                                  ALU.mult).then_inc(g0["cur"], 1)
            edge_hots(HOT0, ET)
            for n in range(NT):
                dve.wait_ge(g0["cut"], n + 1)
                dve.tensor_tensor(g0_lo[:, n, :], g0_cur[:, n, :], g0_hi[:, n, :].bitcast(f32),
                                  ALU.subtract).then_inc(g0["lo"], 1)
            dve.wait_ge(g0["used"], ET)
            for n in range(NT):
                dve.tensor_copy(g0_cnt[:, n, :], B[n][:, 0:T]).then_inc(g0["cnt"], 1)
            dve.wait_ge(g0["turn_ps"], 1)
            dve.wait_ge(g0["cnt"], NT)
            for n in range(NT):
                ins = dve.tensor_tensor(g0_sum[:, n, :], B[6][:, n * T:(n + 1) * T], g0_cnt[:, n, :], ALU.add)
            link(ins)
            for n in range(NT):
                dve.scalar_tensor_tensor(out=g0_adj[:, n, :], in0=g0_sum[:, n, :], scalar=1.0,
                                         in1=eye2[:, n, :], op0=ALU.min, op1=ALU.add).then_inc(g0["adj"], 1)
            dve.wait_ge(g0["adj"], NT)
            link(dve.tensor_reduce(g0_rs[:, :], g0_adj[:, :, :].bitcast(f32), AX, ALU.add))
            link(dve.tensor_scalar(g0_rs[:, :], g0_rs[:, :], 1.0, None, ALU.max))
            link(dve.reciprocal(g0_rinv[:, :], g0_rs[:, :]))
            dve.wait_ge(g0["wh"], 3 * NT)
            for i in range(3):
                for n in range(NT):
                    dve.wait_ge(g0["ps"], NT * i + n + 1)
                    dve.scalar_tensor_tensor(out=g0_cur[:, n, :], in0=B[diffusion_bank(i, n)][:, :],
                                             scalar=g0_rinv[:, n:n + 1], in1=g0_wh[:, i, n, :],
                                             op0=ALU.mult, op1=ALU.add).then_inc(g0["cur"], 1)
                    if i < 2:
                        dve.wait_ge(g0["cut"], NT * (i + 1) + n + 1)
                        dve.tensor_tensor(g0_lo[:, n, :], g0_cur[:, n, :], g0_hi[:, n, :].bitcast(f32),
                                          ALU.subtract).then_inc(g0["lo"], 1)
                    else:
                        dve.wait_ge(g0["cur"], NT * 3 + n + 1)
                        link(dve.scalar_tensor_tensor(out=x[:, n, :], in0=g0_cur[:, n, :], scalar=0.0,
                                                      in1=x[:, n, :], op0=ALU.max, op1=ALU.add))
                if i == 0:
                    dve.tensor_reduce(deg[:, :], B[6][:, :].rearrange("p (n t) -> p n t", n=NT), AX, ALU.add)
                if i < 2:
                    cut_to(2 + i)
            dve.drain().then_inc(layer_done, 1)

            def gating(nth):
                layernorm(2 * nth - 1)
                dve.tensor_scalar(tri[:, 0:P], iota_t[:, 0:P], node_id[:, 0:1], None, ALU.is_gt)
                dve.memset(tri[:, P:T], 1.0)
                dve.wait_ge(gate["par"], 1 if nth == 1 else 3)
                link(dve.tensor_scalar(sel_a[:, :, :], sel_v[:, :, :], 0.0, None, ALU.is_equal))
                link(dve.scalar_tensor_tensor(out=sel[:, :, :], in0=sel_v[:, :, :], scalar=float(E),
                                              in1=sel_a[:, :, :], op0=ALU.is_equal, op1=ALU.max))
                link(dve.tensor_scalar(alpha[:, :], node_id[0:2 * E, 0:1], float(E), -1.0, ALU.is_ge, ALU.mult))
                n = (2 if nth == 1 else 3) * C
                dve.wait_ge(gate["xn_cut"], 2 * nth)
                dve.tensor_tensor(xn_lo[:, :, :], xn[:, :, :], xn_hi[:, :, :].bitcast(f32), ALU.subtract)
                link(dve.scalar_tensor_tensor(out=b_rows[:, 0:n], in0=b_hi[:, 0:n].bitcast(f32),
                                              scalar=alpha[:, 0:1], in1=b_raw[:, 0:n],
                                              op0=ALU.mult, op1=ALU.add))
                cut_to(SPL if nth == 1 else CHUNK[LSTM_ORDER[0]] + 1)
                dve.wait_ge(par1, PAR1[0])
                dve.wait_ge(gate["lg_ps"], nth)
                ps = B[6][:, 0:NT * E].rearrange("p (n e) -> p n e", n=NT)
                dst = lg if nth == 1 else pr
                for m in range(NT):
                    link(dve.tensor_tensor(dst[:, m, :], ps[:, m, :], gb[:, nth - 1, :], ALU.add))
                if nth == 1:
                    link(dve.tensor_reduce(red[:, :], lg[:, :, :], AX, ALU.max))
                    for m in range(NT):
                        dve.tensor_scalar(lg[:, m, :], lg[:, m, :], red[:, m:m + 1], None, ALU.subtract)\
                           .then_inc(gate["shift"], 1)
                    dve.wait_ge(gate["exp"], 1)
                    link(dve.tensor_reduce(red2[:, :], pr[:, :, :], AX, ALU.add))
                    link(dve.reciprocal(red[:, :], red2[:, :]))
                    for m in range(NT):
                        link(dve.tensor_scalar(pr[:, m, :], pr[:, m, :], red[:, m:m + 1], None, ALU.mult))
                for m in range(NT):
                    link(dve.max(top[:, m, :], pr[:, m, :]))
                    link(dve.max_index(topi[:, m, :], top[:, m, :], pr[:, m, :]))
                link(dve.tensor_copy(topf[:, :, :], topi[:, :, :]))
                dve.tensor_tensor(tw[:, :, 0], top[:, :, 1], top[:, :, 0], ALU.subtract).then_inc(gate["d"], 1)
                for m in range(NT):
                    for k in range(2):
                        link(dve.tensor_scalar(oh[:, m, k, :], iota_t[:, 0:E], topf[:, m, k:k + 1], None,
                                               ALU.is_equal))
                dve.tensor_tensor(mask[:, :, :], oh[:, :, 0, :], oh[:, :, 1, :], ALU.add)\
                   .then_inc(gate["mask"], 1)
                dve.wait_ge(gate["mask"], nth)
                link(dve.tensor_scalar(penal[:, :, :], mask[:, :, :], -1000.0, 1000.0, ALU.mult, ALU.add))
                dve.wait_ge(gate["dexp"], nth)
                link(dve.tensor_scalar(tw[:, :, 2], tw[:, :, 1], 1.0, None, ALU.add))
                link(dve.reciprocal(tw[:, :, 3], tw[:, :, 2]))
                link(dve.tensor_tensor(tw[:, :, 2], tw[:, :, 1], tw[:, :, 3], ALU.mult))
                for m in range(NT):
                    link(dve.tensor_scalar(comb[:, m, :], oh[:, m, 0, :], tw[:, m, 3:4], None, ALU.mult))
                    link(dve.scalar_tensor_tensor(out=comb[:, m, :], in0=oh[:, m, 1, :],
                                                  scalar=tw[:, m, 2:3], in1=comb[:, m, :],
                                                  op0=ALU.mult, op1=ALU.add))
                dve.wait_ge(gate["pos_ps"], nth)
                ps = B[6][:, 32:32 + NT * E].rearrange("p (n e) -> p n e", n=NT)
                link(dve.tensor_tensor(posm[:, :, :], ps, penal[:, :, :], ALU.add))
                dve.tensor_scalar(over[:, :], B[6][:, 64:64 + E], float(P), None, ALU.is_gt).then_inc(gate["route"], 1)

            def more_experts(nth):
                dve.wait_ge(gate["route"], nth)
                link(dve.tensor_tensor_scan(rank[:, :], tri[:, P:P + E], over[:, :], 0.0, ALU.mult, ALU.add))
                for job in range(MORE):
                    link(dve.scalar_tensor_tensor(out=picked[:, job, :], in0=rank[:, :], scalar=job + 1.0,
                                                  in1=over[:, :], op0=ALU.is_equal, op1=ALU.mult))
                    link(dve.tensor_tensor(prod[:, 0, :], picked[:, job, :], iota_t[:, 0:E], ALU.mult))
                    link(dve.tensor_reduce(ids[:, 1 + job:2 + job], prod[:, 0, :], AX, ALU.add))
                link(dve.tensor_copy(ids[:, 0:1], rank[:, E - 1:E]))
                dve.tensor_copy(more_i[nth - 1][:, :], ids[:, :]).then_inc(gate["more"], 1)
                dve.wait_ge(gate["more"], nth)

            def experts(run):
                more_link = Chain(dve, more_chain[run.layer])

                def cuts(upto):
                    cut_to(min(upto, run.base + len(run.order)))

                def build_g(e):
                    if e >= 2:
                        dve.wait_ge(run.turn_ps, e - 1)
                    for n in range(NT):
                        slot = posm[:, n, e:e + 1] if e < E else more_pc[:, e - E, n:n + 1]
                        ins = dve.tensor_scalar(G[:, e % 2, n, :], iota_t[:, 0:P] if e < E else iota_t[:, P:T],
                                                slot, None, ALU.is_equal)
                    ins.then_inc(run.g_built, 1)

                def xe(e):
                    dve.wait_ge(run.xe_cut, 2 * e + 1)
                    dve.tensor_tensor(xe_lo[:, :, :], quarters(B[6]), xe_hi[:, :, :].bitcast(f32),
                                      ALU.subtract).then_inc(run.xe_cut, 1)
                    dve.wait_ge(run.turn_ps, e + 1)
                    dve.tensor_copy(GT[:, e % 3, :], B[5][:, 0:T])
                    dve.tensor_copy(wslot[:, e % 3:e % 3 + 1], B[5][:, T:T + 1]).then_inc(run.gt_sb, 1)

                def outputs(e):
                    dve.wait_ge(run.y_cut, 2 * e + 1)
                    dve.wait_ge(run.gt_sb, e + 1)
                    dve.scalar_tensor_tensor(out=y_lo[:, :], in0=B[7][:, :], scalar=wslot[:, e % 3:e % 3 + 1],
                                             in1=y_hi[:, :].bitcast(f32), op0=ALU.mult,
                                             op1=ALU.subtract).then_inc(run.y_cut, 1)

                def turned(e):
                    for b in range(run.banks_h):
                        dve.wait_ge(run.hT_hi, run.banks_h * e + b + 1)
                        dve.tensor_tensor(hT_lo[:, KB * b:KB * b + KB, :], quarters(B[5 - b]),
                                          hT_hi[:, KB * b:KB * b + KB, :].bitcast(f32),
                                          ALU.subtract).then_inc(run.hT_lo, 1)

                def results(e):
                    if run.layer == 1:
                        dve.wait_ge(run.gates, 4 * e + 2)
                        dve.tensor_tensor(act3[:, 0, :], act3[:, 0, :], act3[:, 1, :], ALU.mult)\
                           .then_inc(run.h_ok, 1)
                        dve.wait_ge(run.gates, 4 * e + 4)
                        dve.tensor_tensor(act3[:, 2, :], act3[:, 2, :], act3[:, 1, :], ALU.mult)\
                           .then_inc(run.h_ok, 1)

                def more_cuts(first, upto):
                    for q in range(max(first, run.end), upto):
                        more_lo(run, q)

                def prepare(e):
                    job = e - E
                    for n in range(NT):
                        for i, table in enumerate((posm, comb)):
                            ins = dve.tensor_tensor(prod[:, NT * i + n, :], table[:, n, :],
                                                    picked[:, job, :], ALU.mult)
                    more_link(ins)
                    more_link(dve.tensor_reduce(more_pc[:, job, :], prod[:, :, :], AX, ALU.add))
                    expert = ids[0:2 * E, 1 + job:2 + job]
                    dve.tensor_scalar(sel_m[:, 0, :], sel_v[:, 0, :], expert, None, ALU.is_equal)
                    more_link(dve.tensor_scalar(sel_m[:, 1, :], sel_v[:, 0, :], float(E), expert,
                                                ALU.subtract, ALU.is_equal))
                    more_link(dve.tensor_tensor(sel_more[:, job, :], sel_m[:, 0, :], sel_m[:, 1, :], ALU.max))
                    build_g(e)

                build_g(0)
                build_g(1)
                cuts(run.base + SPL)
                xe(0)
                more_experts(run.layer + 1)
                for step in range(E):
                    if step >= 2:
                        outputs(step - 2)
                    if step >= 1:
                        turned(step - 1)
                    if step >= 2:
                        cuts(run.last_out(step - 2) + SPL + 1)
                    results(step)
                    if step + 1 < E:
                        xe(step + 1)
                    if step + 2 < E:
                        build_g(step + 2)
                    if step == 0:
                        comb_turned(run.layer + 1)
                    cuts(run.last_in(step) + SPL + 1)
                number = dve.value_load(more_i[run.layer][0:1, 0:1], min_val=0, max_val=MORE)
                outputs(E - 2)
                turned(E - 1)
                with dve.If(number > 0):
                    prepare(E)
                    more_cuts(run.end, run.last_out(E - 2) + SPL + 1)
                    xe(E)
                outputs(E - 1)
                for e in range(E, E + MORE):
                    if e + 1 < E + MORE:
                        with dve.If(number > e + 1 - E):
                            prepare(e + 1)
                    with dve.If(number > e - E):
                        more_cuts(run.last_out(E - 2) + SPL + 1 if e == E else run.chunk("out", e, 0),
                                  run.last_out(e) + 1)
                        results(e)
                    if e + 1 < E + MORE:
                        with dve.If(number > e + 1 - E):
                            xe(e + 1)
                    with dve.If(number > e - E):
                        turned(e)
                    if e + 1 < E + MORE:
                        with dve.If(number > e + 1 - E):
                            more_cuts(run.chunk("in", e + 1, 0), run.last_in(e + 1) + 1)
                    with dve.If(number > e - E):
                        outputs(e)
                dve.wait_ge(run.sum_ps, E)
                for e in range(E, E + MORE):
                    with dve.If(number > e - E):
                        dve.wait_ge(run.sum_ps, e + 1)
                for n in range(NT):
                    link(dve.tensor_tensor(x[:, n, :], x[:, n, :], B[n][:, :], ALU.add))

            def comb_turned(nth):
                dve.wait_ge(gate["combT"], 2 * nth - 1)
                dve.tensor_copy(combT[:, :], B[7][0:E, 0:T]).then_inc(gate["combT"], 1)

            gating(1)
            experts(ffn)
            dve.drain().then_inc(layer_done, 1)

            layernorm(2)
            first = CHUNK[("gnn", "W1")]
            dve.wait_ge(xt_sb, 3 * NT)
            for n in range(NT):
                dve.tensor_tensor(g1_xT_lo[:, n, :, :], quarters(B[5 - n]),
                                  g1_xT_hi[:, n, :, :].bitcast(f32), ALU.subtract).then_inc(xt_sb, 1)
            cut_to(first + 2)
            dve.wait_ge(gate["par"], 2)
            link(dve.tensor_scalar(galpha[:, :], node_id[0:4, 0:1], 2.0, -1.0, ALU.is_ge, ALU.mult))
            for i, row in ((2, 0.0), (1, 1.0)):
                link(dve.tensor_scalar(g1_t[:, i, :], g1_it[:, i, :], row, None, ALU.is_equal))
                link(dve.scalar_tensor_tensor(out=gsel[:, i, :], in0=g1_it[:, i, :], scalar=row + 2.0,
                                              in1=g1_t[:, i, :], op0=ALU.is_equal, op1=ALU.max))
            dve.tensor_scalar(gsel[:, 0, :], g1_it[:, 0, :], 0.0, None, ALU.is_ge).then_inc(g1["gsel"], 1)
            dve.wait_ge(par2, 16 * 7)
            for n in range(NT):
                both_tiles(dve, n, g1["a_ps"], 1, CHUNK[("gnn", "W1")])
                dve.tensor_tensor(A_sb[:, n, :], B[2 + n][:, :], b1[:, :], ALU.add).then_inc(g1["a_sb"], 1)
            dve.wait_ge(g1["rows"], 1)
            dve.scalar_tensor_tensor(out=gb_rows[:, :], in0=gb_rows[:, :].bitcast(f32),
                                     scalar=galpha[:, 0:1], in1=gb_raw[:, :],
                                     op0=ALU.mult, op1=ALU.add).then_inc(g1["rows"], 1)
            cut_to(first + SPL)
            dve.tensor_scalar(g2v[:, :], g2v[:, :], EPS, None, ALU.add).then_inc(g1["bn"], 1)
            dve.wait_ge(g1["w1e_hi"], 1)
            dve.tensor_tensor(w1e_lo[:, :], w1e[:, :], w1e_hi[:, :].bitcast(f32), ALU.subtract)\
               .then_inc(g1["w1e_lo"], 1)

            def ea_cut(g):
                n = min(GRP, ET - g * GRP) * P
                dve.wait_ge(g1["ea_hi"], g + 1)
                dve.tensor_tensor(ea_lo[:, g % 2, 0:n], ea[:, g % 3, 0:n],
                                  ea_hi[:, g % 2, 0:n].bitcast(f32), ALU.subtract).then_inc(g1["ea_lo"], 1)

            ea_cut(0)
            ea_cut(1)
            for g in range(3):
                for n in range(NT):
                    both_tiles(dve, n, g1["gh_ps"], g + 1, CHUNK[("gnn", "Whh", g)])
                    dve.tensor_copy(gh[:, n, g, :], B[(6, 2, 6)[g] + n][:, :]).then_inc(g1["gh_sb"], 1)
                cut_to(first + SPL + 1 + g)
                if g == 0:
                    dve.wait_ge(g1["bn"], 2)
                    link(dve.reciprocal(g2v[:, :], g2v[:, :]))
                    link(dve.tensor_tensor(g2s[:, :], g2s[:, :], g2v[:, :], ALU.mult))
                    link(dve.tensor_tensor(g2m[:, :], g2m[:, :], g2s[:, :], ALU.mult))
                    link(dve.tensor_tensor(g2b[:, :], g2b[:, :], g2m[:, :], ALU.subtract))
                if g == 1:
                    for n in range(NT):
                        link(dve.tensor_tensor(x[:, n, :], x[:, n, :], g2b[:, :], ALU.add))
                        link(dve.tensor_tensor(x[:, n, :], x[:, n, :], xn[:, n, :], ALU.add))
            cut_to(first + 2 * SPL)

            def m_cut(t):
                dve.wait_ge(g1["m_hi"], t + 1)
                dve.scalar_tensor_tensor(out=m_lo[:, t % MSG, :], in0=mp[:, t % SUMS, :], scalar=0.0,
                                         in1=m_hi[:, t % MSG, :].bitcast(f32), op0=ALU.max,
                                         op1=ALU.subtract).then_inc(g1["m_lo"], 1)

            def hot(t):
                if t >= HOT1:
                    dve.wait_ge(g1["sum_ps"], t - HOT1 + 1)
                dve.tensor_scalar(onehot[:, t % HOT1, :], iota_t[:, :], dst_f[:, t:t + 1], None,
                                  ALU.is_equal).then_inc(g1["hot_odd"], 1)

            hot(1)
            for t in range(ET):
                if t % 2 == 0 and 2 <= t < ET - 1:
                    hot(t + 1)
                dve.wait_ge(g1["e_ps"], t + 1)
                dve.wait_ge(gath_in[t % GATH], 16 * (t // GATH + 1))
                if t >= SUMS:
                    dve.wait_ge(g1["m_lo"], t - SUMS + 1)
                dve.tensor_tensor(mp[:, t % SUMS, :], B[2 + t % EBANKS][:, :], gath[:, t % GATH, :], ALU.add)\
                   .then_inc(g1["mp"], 1)
                if t >= 1:
                    m_cut(t - 1)
                if t % GRP == 1 and t // GRP + 1 < NG and t >= GRP:
                    ea_cut(t // GRP + 1)
            m_cut(ET - 1)
            dve.wait_ge(g1["sum_ps"], ET)
            for n in range(NT):
                dve.tensor_copy(S1[:, n, :], B[n][:, :]).then_inc(g1["s1"], 1)
            for n in range(NT):
                dve.wait_ge(g1["aT"], NT)
                dve.tensor_tensor(aT_lo[:, n, :, :], quarters(B[6 + n]),
                                  aT_hi[:, n, :, :].bitcast(f32), ALU.subtract).then_inc(g1["aT"], 1)
            for n in range(NT):
                both_tiles(dve, n, g1["agg_ps"], 1, CHUNK[("gnn", "W2")])
                dve.scalar_tensor_tensor(out=agg[:, n, :], in0=b2[:, :], scalar=deg[:, n:n + 1],
                                         in1=B[2 + n][:, :], op0=ALU.mult, op1=ALU.add)\
                   .then_inc(g1["agg"], 1)
            for n in range(NT):
                dve.wait_ge(g1["aT"], 3 * NT)
                dve.tensor_tensor(aT_lo[:, n, :, :], quarters(B[6 + n]),
                                  aT_hi[:, n, :, :].bitcast(f32), ALU.subtract).then_inc(g1["aT"], 1)
            for g in range(2):
                for n in range(NT):
                    both_tiles(dve, n, g1["gi_ps"], g + 1, CHUNK[("gnn", "Wih", g)])
                    dve.tensor_tensor(rz[:, n, g, :], B[2 * g + n][:, :], gh[:, n, g, :], ALU.add)\
                       .then_inc(g1["rz_in"], 1)
            for n in range(NT):
                dve.wait_ge(g1["rz"], n + 1)
                link(dve.tensor_tensor(rz[:, n, 0, :], rz[:, n, 0, :], gh[:, n, 2, :], ALU.mult))
            for n in range(NT):
                dve.wait_ge(g1["rz"], NT + n + 1)
                link(dve.tensor_tensor(gh[:, n, 0, :], rz[:, n, 1, :], xn[:, n, :], ALU.mult))
                link(dve.tensor_tensor(gh[:, n, 0, :], gh[:, n, 0, :], g2s[:, :], ALU.mult))
                link(dve.tensor_tensor(x[:, n, :], x[:, n, :], gh[:, n, 0, :], ALU.add))
                link(dve.scalar_tensor_tensor(out=gh[:, n, 1, :], in0=rz[:, n, 1, :], scalar=1.0,
                                              in1=g2s[:, :], op0=ALU.subtract, op1=ALU.mult))
            for n in range(NT):
                both_tiles(dve, n, g1["gi_ps"], 3, CHUNK[("gnn", "Wih", 2)])
                dve.tensor_tensor(rz[:, n, 2, :], rz[:, n, 0, :], B[4 + n][:, :], ALU.add)\
                   .then_inc(g1["n_in"], 1)
            for n in range(NT):
                dve.wait_ge(g1["n"], n + 1)
                link(dve.tensor_tensor(rz[:, n, 2, :], rz[:, n, 2, :], gh[:, n, 1, :], ALU.mult))
                link(dve.tensor_tensor(x[:, n, :], x[:, n, :], rz[:, n, 2, :], ALU.subtract))
            dve.drain().then_inc(layer_done, 1)

            gating(2)
            experts(lstm)
            dve.drain().then_inc(layer_done, 1)

        @block.tensor
        def _(pe):
            def mm3(ps, xh, xl, wh, wl, first, last):
                pe.matmul(ps, xh, wh, start=first, stop=False)
                pe.matmul(ps, xh, wl, start=False, stop=False)
                return pe.matmul(ps, xl, wh, start=False, stop=last)

            def has_chunk(n):
                pe.wait_ge(lo_cut, n + 1)

            def turn_x(layer):
                for n in range(NT):
                    pe.wait_ge(xn_ok, NT * layer + n + 1)
                    for k in range(KB):
                        ins = pe.transpose(quarters(B[5 - n])[:, k, :], xn[:, n, k * P:(k + 1) * P], ident)
                    ins.then_inc(xt_ps, 1)

            pe.wait_ge(consts_ok, 1)
            turn_x(0)
            pe.wait_ge(xt_sb, NT)
            has_chunk(0)
            for n in range(NT):
                for k in range(KB):
                    ins = mm3(B[2 + n][:, :], g0_xT_hi[:, n, k, :], g0_xT_lo[:, n, k, :],
                              whi[0][:, k, :], wlo[0][:, k, :], k == 0, k == KB - 1)
                ins.then_inc(g0["h_ps"] if n == 0 else chunk_used, 1)
            for t in range(ET):
                pe.wait_ge(g0["hot"], t + 1)
                for n in range(NT):
                    ins = pe.matmul(B[n][:, 0:T], g0_S[:, t % HOT0, n * P:(n + 1) * P], g0_D[:, t % HOT0, :],
                                    start=t == 0, stop=t == ET - 1)
                ins.then_inc(g0["used"], 1)
            pe.wait_ge(g0["cnt"], NT)
            for a in range(NT):
                for b in range(NT):
                    ins = pe.transpose(B[6][:, b * T + a * P:b * T + (a + 1) * P],
                                       g0_cnt[:, a, b * P:(b + 1) * P], ident)
            ins.then_inc(g0["turn_ps"], 1)
            for i in range(3):
                for m in range(NT):
                    if i == 0:
                        pe.wait_ge(g0["adj"], m + 1)
                    pe.wait_ge(g0["lo"], NT * i + m + 1)
                    for n in range(NT):
                        lhs = g0_adj[:, m, n * P:(n + 1) * P]
                        ps = B[diffusion_bank(i, n)]
                        pe.matmul(ps[:, :], lhs, g0_hi[:, m, :], start=m == 0, stop=False)
                        ins = pe.matmul(ps[:, :], lhs, g0_lo[:, m, :], start=False, stop=m == NT - 1)
                        if m == NT - 1:
                            ins.then_inc(g0["ps"], 1)

            def gating(nth):
                turn_x(2 * nth - 1)
                pe.wait_ge(par1, PAR1[0])
                pe.wait_ge(xt_sb, NT * 2 if nth == 1 else 5 * NT)
                if nth == 1:
                    for b in range(2):
                        for k in range(KB):
                            ins = pe.matmul(B[2 + b][:, 0:T].rearrange("p (n t) -> p n t", n=NT),
                                            gw1[:, k, b * P:(b + 1) * P], xnT[:, :, k, :],
                                            start=k == 0, stop=k == KB - 1)
                        ins.then_inc(gate["hid_ps"], 1)
                    pe.wait_ge(gate["hid_sb"], 2)
                for n in range(NT):
                    for k in range(2 if nth == 1 else KB):
                        lhs = hid[:, k, n * P:(n + 1) * P] if nth == 1 else xnT[:, n, k, :]
                        rhs = gw2[:, k, :] if nth == 1 else rw[:, k, :]
                        ins = pe.matmul(B[6][:, n * E:(n + 1) * E], lhs, rhs, start=k == 0,
                                        stop=k == (2 if nth == 1 else KB) - 1)
                ins.then_inc(gate["lg_ps"], 1)
                pe.wait_ge(gate["mask"], nth)
                pe.matmul(B[6][:, 32:32 + E], tri[:, 0:P], mask[:, 0, :], start=True, stop=True)
                pe.matmul(B[6][:, 32 + E:32 + 2 * E], tri[:, P:T], mask[:, 0, :], start=True, stop=False)
                pe.matmul(B[6][:, 32 + E:32 + 2 * E], tri[:, 0:P], mask[:, 1, :], start=False, stop=True)
                pe.matmul(B[6][:, 64:64 + E], tri[:, P:T], mask[:, 0, :], start=True, stop=False)
                pe.matmul(B[6][:, 64:64 + E], tri[:, P:T], mask[:, 1, :], start=False, stop=True)\
                  .then_inc(gate["pos_ps"], 1)

            def biases(nth):
                pe.wait_ge(gate["route"], nth)
                for n in range(NT):
                    ins = pe.matmul(B[7][0:E, n * P:(n + 1) * P], comb[:, n, :], ident, start=True, stop=True)
                ins.then_inc(gate["combT"], 1)
                pe.wait_ge(gate["combT"], 2 * nth)
                for n in range(NT):
                    pe.matmul(B[n][:, :], combT[:, n * P:(n + 1) * P], b_out[:, :], start=True, stop=False,
                              skip_group_check=True)

            def experts(run):
                def gather(e):
                    pe.wait_ge(run.g_built, e + 1)
                    if e >= 1:
                        pe.wait_ge(run.xe_cut, 2 * e)
                        pe.wait_ge(run.gt_sb, e)
                        if e >= 2:
                            pe.wait_ge(run.hT_lo, run.banks_h * (e - 1))
                    for k in range(KB):
                        for n in range(NT):
                            pe.matmul(quarters(B[6])[:, k, :], xn_hi[:, n, k * P:(k + 1) * P],
                                      G[:, e % 2, n, :], start=n == 0, stop=False)
                            ins = pe.matmul(quarters(B[6])[:, k, :], xn_lo[:, n, k * P:(k + 1) * P],
                                            G[:, e % 2, n, :], start=False, stop=n == NT - 1)
                    ins.then_inc(run.gather_ps, 1)
                    for n in range(NT):
                        pe.transpose(B[5][:, n * P:(n + 1) * P], G[:, e % 2, n, :].bitcast(f32), ident)
                    for n in range(NT):
                        weight = comb[:, n, e:e + 1] if e < E else more_pc[:, e - E, NT + n:NT + n + 1]
                        ins = pe.matmul(B[5][:, T:T + 1], G[:, e % 2, n, :].bitcast(f32),
                                        weight, start=n == 0, stop=n == NT - 1)
                    ins.then_inc(run.turn_ps, 1)

                def first_product(e):
                    pe.wait_ge(run.xe_cut, 2 * e + 2)
                    for c in range(run.n_in):
                        if e >= 1 and c == 0:
                            pe.wait_ge(run.h_ok, 2 * e)
                        q = run.chunk("in", e, c)
                        pe.wait_ge(*run.lo(q))
                        rows = sel[:, e, :] if e < E else sel_more[:, e - E, :]
                        pe.matmul(B[2 + c][:, :], rows, b_rows[:, c * C:(c + 1) * C],
                                  start=True, stop=False)
                        for k in range(KB):
                            ins = mm3(B[2 + c][:, :], xe_hi[:, k, :], xe_lo[:, k, :],
                                      whi[q % SPL][:, k, :], wlo[q % SPL][:, k, :], False, k == KB - 1)
                        ins.then_inc(run.used(q)[0], 1)

                def weighted_sum(e):
                    pe.wait_ge(run.y_cut, 2 * e + 2)
                    pe.wait_ge(run.gt_sb, e + 1)
                    for n in range(NT):
                        lhs = GT[:, e % 3, n * P:(n + 1) * P]
                        pe.matmul(B[n][:, :], lhs, y_hi[:, :], start=False, stop=False,
                                  skip_group_check=True)
                        ins = pe.matmul(B[n][:, :], lhs, y_lo[:, :], start=False,
                                        stop=e >= E - 1, skip_group_check=True)
                    ins.then_inc(run.sum_ps, 1)

                def second_product(e):
                    pe.wait_ge(run.hT_lo, run.banks_h * (e + 1))
                    if e >= 1:
                        pe.wait_ge(run.y_cut, 2 * e)
                    for c in range(run.n_out):
                        q = run.chunk("out", e, c)
                        pe.wait_ge(*run.lo(q))
                        for k in range(KB):
                            ins = mm3(B[7][:, :], hT_hi[:, c * KB + k, :], hT_lo[:, c * KB + k, :],
                                      whi[q % SPL][:, k, :], wlo[q % SPL][:, k, :],
                                      c == 0 and k == 0, c == run.n_out - 1 and k == KB - 1)
                        ins.then_inc(run.used(q)[0], 1)

                def turn_h(e, gathered):
                    pe.wait_ge(run.h_ok, 2 * (e + 1))
                    pe.wait_ge(run.gt_sb, gathered)
                    for b in range(run.banks_h):
                        for k in range(KB):
                            h = act3[:, b if run.layer == 0 else 2, k * P:(k + 1) * P]
                            ins = pe.transpose(quarters(B[5 - b])[:, k, :], h, ident)
                        ins.then_inc(run.hT_ps, 1)

                gather(0)
                for step in range(E):
                    first_product(step)
                    if step >= 2:
                        weighted_sum(step - 2)
                    if step + 1 < E:
                        gather(step + 1)
                    if step >= 1:
                        second_product(step - 1)
                    turn_h(step, min(step + 2, E))
                    if step == 0:
                        biases(run.layer + 1)
                pe.wait_ge(gate["more"], run.layer + 1)
                number = pe.value_load(more_i[run.layer][0:1, 0:1], min_val=0, max_val=MORE)
                weighted_sum(E - 2)
                with pe.If(number > 0):
                    gather(E)
                second_product(E - 1)
                with pe.If(number > 0):
                    first_product(E)
                weighted_sum(E - 1)
                for e in range(E, E + MORE):
                    if e + 1 < E + MORE:
                        with pe.If(number > e + 1 - E):
                            gather(e + 1)
                            pe.wait_ge(run.gt_sb, e + 2)
                    with pe.If(number > e - E):
                        turn_h(e, e + 1)
                        second_product(e)
                    if e + 1 < E + MORE:
                        with pe.If(number > e + 1 - E):
                            first_product(e + 1)
                    with pe.If(number > e - E):
                        weighted_sum(e)

            pe.wait_ge(layer_done, 1)
            gating(1)
            experts(ffn)

            pe.wait_ge(layer_done, 2)
            turn_x(2)
            q = CHUNK[("gnn", "W1")]
            pe.wait_ge(xt_sb, 4 * NT)
            has_chunk(q)
            for n in range(NT):
                for k in range(KB):
                    ins = mm3(B[2 + n][:, :], g1_xT_hi[:, n, k, :], g1_xT_lo[:, n, k, :],
                              whi[q % SPL][:, k, :], wlo[q % SPL][:, k, :], k == 0, k == KB - 1)
                ins.then_inc(g1["a_ps"] if n == 0 else chunk_used, 1)
            pe.wait_ge(g1["gsel"], 1)
            for g in range(3):
                q = CHUNK[("gnn", "Whh", g)]
                has_chunk(q)
                for n in range(NT):
                    ps = B[(6, 2, 6)[g] + n]
                    if g == 1:
                        pe.wait_ge(g1["a_sb"], n + 1)
                    if g == 2:
                        pe.wait_ge(g1["gh_sb"], n + 1)
                    for k in range(KB):
                        mm3(ps[:, :], g1_xT_hi[:, n, k, :], g1_xT_lo[:, n, k, :],
                            whi[q % SPL][:, k, :], wlo[q % SPL][:, k, :], k == 0, False)
                    pe.wait_ge(g1["rows"], 2)
                    ins = pe.matmul(ps[:, :], gsel[:, 0 if g < 2 else 1, :], gb_rows[:, g * D:(g + 1) * D],
                                    start=False, stop=True)
                    ins.then_inc(g1["gh_ps"] if n == 0 else chunk_used, 1)

            pe.wait_ge(g1["w1e_lo"], 1)

            def edge_product(t):
                g, j = t // GRP, t % GRP
                if j == 0:
                    pe.wait_ge(g1["ea_lo"], g + 1)
                if t >= EBANKS:
                    pe.wait_ge(g1["mp"], t - EBANKS + 1)
                elif t in (0, 4):
                    pe.wait_ge(g1["gh_sb"], 2 * NT if t == 0 else 3 * NT)
                mm3(B[2 + t % EBANKS][:, :], ea_hi[:, g % 2, j * P:(j + 1) * P],
                    ea_lo[:, g % 2, j * P:(j + 1) * P], w1e_hi[:, :], w1e_lo[:, :], True, True)\
                    .then_inc(g1["e_ps"], 1)

            def edge_sum(t):
                pe.wait_ge(g1["m_lo"], t + 1)
                pe.wait_ge(g1["hot_odd"] if t % 2 else g1["hot_even"], t // 2 + 1)
                for n in range(NT):
                    lhs = onehot[:, t % HOT1, n * P:(n + 1) * P]
                    pe.matmul(B[n][:, :], lhs, m_hi[:, t % MSG, :], start=t == 0, stop=False)
                    ins = pe.matmul(B[n][:, :], lhs, m_lo[:, t % MSG, :], start=False, stop=t == ET - 1)
                ins.then_inc(g1["sum_ps"], 1)

            for t in range(ET + EAHEAD):
                if t < ET:
                    edge_product(t)
                if t >= EAHEAD:
                    edge_sum(t - EAHEAD)
            for n in range(NT):
                pe.wait_ge(g1["s1"], n + 1)
                for k in range(KB):
                    ins = pe.transpose(quarters(B[6 + n])[:, k, :], S1[:, n, k * P:(k + 1) * P], ident)
                ins.then_inc(g1["s1T_ps"], 1)
            pe.wait_ge(g1["aT"], 2 * NT)
            q = CHUNK[("gnn", "W2")]
            has_chunk(q)
            for n in range(NT):
                for k in range(KB):
                    ins = mm3(B[2 + n][:, :], aT_hi[:, n, k, :], aT_lo[:, n, k, :],
                              whi[q % SPL][:, k, :], wlo[q % SPL][:, k, :], k == 0, k == KB - 1)
                ins.then_inc(g1["agg_ps"] if n == 0 else chunk_used, 1)
            for n in range(NT):
                pe.wait_ge(g1["agg"], n + 1)
                for k in range(KB):
                    ins = pe.transpose(quarters(B[6 + n])[:, k, :], agg[:, n, k * P:(k + 1) * P], ident)
                ins.then_inc(g1["aggT_ps"], 1)
            pe.wait_ge(g1["aT"], 4 * NT)
            for g in range(3):
                q = CHUNK[("gnn", "Wih", g)]
                has_chunk(q)
                for n in range(NT):
                    ps = B[2 * g + n]
                    if g == 2:
                        pe.matmul(ps[:, :], gsel[:, 2, :], gb_rows[:, g * D:(g + 1) * D], start=True, stop=False)
                    for k in range(KB):
                        ins = mm3(ps[:, :], aT_hi[:, n, k, :], aT_lo[:, n, k, :],
                                  whi[q % SPL][:, k, :], wlo[q % SPL][:, k, :], g < 2 and k == 0, k == KB - 1)
                    ins.then_inc(g1["gi_ps"] if n == 0 else chunk_used, 1)

            pe.wait_ge(layer_done, 3)
            gating(2)
            experts(lstm)


def kernel(**inputs):
    import numpy as _np
    import concourse.bacc as _bacc
    from concourse import mybir as _mybir
    from concourse.bass_utils import run_bass_kernel_spmd as _run

    a = {k: _np.asarray(v) for k, v in inputs.items()}

    W1T, W2T, WihT, WhhT = (a["L1_gnn_" + n].T for n in ("W1", "W2", "W_ih", "W_hh"))

    def block(w, r, c):
        return w[r * C:(r + 1) * C, c * C:(c + 1) * C]

    def matrix(key):
        kind = key[0]
        if kind == "L0":
            return a["L0_gnn_W"]
        if kind == "ffn":
            return block(a["L0_ffn_we1"][key[2]], 0, key[3]) if key[1] == "in" else \
                block(a["L0_ffn_we2"][key[2]], key[3], 0)
        if kind == "lstm":
            return block(a["L1_ffn_Wi"][key[2]], 0, (0, 2, 3)[key[3]]) if key[1] == "in" else \
                a["L1_ffn_Wo"][key[2]]
        if key[1] == "W1":
            return W1T[0:D, :]
        if key[1] == "W2":
            return W2T
        return block(WhhT if key[1] == "Whh" else WihT, 0, key[2])

    b = a["L1_ffn_b"]
    arrays = {
        "x": a["x"],
        "src": a["src"].reshape(ET, P).T,
        "dst": a["dst"].reshape(ET, P).T,
        "ea": a["edge_attr_128"].T,
        "w1e": W1T[D:, :],
        "weights": _np.stack([matrix(k).reshape(KB, P, C).transpose(1, 0, 2) for k in STORE]),
        "L0_ffn_gb1": a["L0_ffn_gb1"].reshape(2, P).T,
        "lstm_b": _np.concatenate([b[:, 0:D], b[:, 2 * D:3 * D], b[:, 3 * D:4 * D]], axis=1),
        "L1_gnn_b_ih": a["L1_gnn_b_ih"].reshape(1, 3 * D),
        "L1_gnn_b_hh": a["L1_gnn_b_hh"].reshape(1, 3 * D),
    }
    for n in ("L0_gnn_b", "L0_gnn_diffusion_weights", "L0_ffn_gw1", "L0_ffn_gw2", "L0_ffn_gb2",
              "L0_ffn_be1", "L0_ffn_be2", "L1_gnn_b1", "L1_gnn_b2", "L1_gnn_gamma", "L1_gnn_beta",
              "L1_gnn_run_mean", "L1_gnn_run_var", "L1_ffn_router_w", "L1_ffn_router_b", "L1_ffn_bo"):
        arrays[n] = a[n]
    arrays = {f"in_{n}_dram": _np.ascontiguousarray(v) for n, v in arrays.items()}

    nc = _bacc.Bacc("TRN2", target_bir_lowering=False, num_devices=1)
    aps = {n[3:-5]: nc.dram_tensor(n, v.shape, _mybir.dt.from_np(v.dtype), kind="ExternalInput").ap()
           for n, v in arrays.items()}
    out = nc.dram_tensor("out_0_dram", (T, D), _mybir.dt.float32, kind="ExternalOutput").ap()
    node_rows = nc.dram_tensor("node_rows", (T, D), _mybir.dt.float32).ap()
    build(nc, aps, out, node_rows)
    r = _run(nc, [arrays], core_ids=[0])
    return r.results[0]["out_0_dram"]
```

```python
import numpy as np
import concourse.bass as bass
from concourse import mybir
from contextlib import ExitStack

P = 128
T = 256
NT = T // P
D = 512
KB = D // P
E = 8
MORE = 2 * T // (P + 1)
EDGES = 4352
ET = EDGES // P
C = 512
EPS = 1e-5
RAW = 4
SPL = 4
WJ = E + MORE
TURN = P + 2 * WJ
HOT0 = 16
GRP = 4
NG = -(-ET // GRP)
HOT1 = 5
GATH = 5
SUMS = 2
MSG = 3
EAHEAD = 3
EBANKS = 4

FFN_IN, FFN_OUT = 2, 2
LSTM_IN, LSTM_OUT = 3, 1


def moe_order(layer, n_in, n_out):
    order = []
    for step in range(E + 1):
        if step < E:
            order += [(layer, "in", step, c) for c in range(n_in)]
        if step >= 1:
            order += [(layer, "out", step - 1, c) for c in range(n_out)]
    return order


FFN_ORDER = moe_order("ffn", FFN_IN, FFN_OUT)
LSTM_ORDER = moe_order("lstm", LSTM_IN, LSTM_OUT)
EC = FFN_IN + FFN_OUT
GNN_ORDER = [("gnn", "W1")] + [("gnn", "Whh", g) for g in range(3)] + [("gnn", "W2")] \
    + [("gnn", "Wih", g) for g in range(3)]
ORDER = [("L0", "W")] + FFN_ORDER + GNN_ORDER + LSTM_ORDER
CHUNK = {key: n for n, key in enumerate(ORDER)}


def moe_store(layer, n_in):
    return [(layer, "in", e, c) if c < n_in else (layer, "out", e, c - n_in)
            for e in range(E) for c in range(EC)]


STORE = [("L0", "W")] + moe_store("ffn", FFN_IN) + GNN_ORDER + moe_store("lstm", LSTM_IN)
PLACE = {key: n for n, key in enumerate(STORE)}


def build(nc, A, out, node_rows):
    f32, f32r, bf16, i32, u32 = (mybir.dt.float32, mybir.dt.float32r, mybir.dt.bfloat16,
                                 mybir.dt.int32, mybir.dt.uint32)
    ALU = mybir.AluOpType
    ACT = mybir.ActivationFunctionType
    AX = mybir.AxisListType.X

    ctx = ExitStack()
    with ctx:
        def sb(name, shape, dt=f32, stack=ctx):
            return stack.enter_context(nc.sbuf_tensor(name, shape, dt))

        def sem(name):
            return ctx.enter_context(nc.semaphore(name))

        raw = [sb(f"raw{i}", [P, KB, C]) for i in range(RAW)]
        whi = [sb(f"whi{i}", [P, KB, C], f32r) for i in range(SPL)]
        wlo = [sb(f"wlo{i}", [P, KB, C], f32r) for i in range(SPL)]
        x = sb("x", [P, NT, D])
        xn = sb("xn", [P, NT, D])
        xnT = sb("xnT", [P, NT, KB, P])
        iota_t = sb("iota_t", [P, T])
        node_id = sb("node_id", [P, NT])
        eye2 = sb("eye2", [P, NT, T])
        ident = eye2[:, 0, 0:P]
        src_i = sb("src_i", [P, ET], i32)
        dst_i = sb("dst_i", [P, ET], i32)
        dst_f = sb("dst_f", [P, ET])
        deg = sb("deg", [P, NT])
        stats = sb("stats", [P, NT, 6])
        mv = sb("mv", [P, NT, 2])
        rstd = sb("rstd", [P, NT])
        var_eps = sb("var_eps", [P, NT])
        minus_half = sb("minus_half", [P, NT])
        iota_b = sb("iota_b", [P, T], bf16)
        more_i = [sb(f"more_i{i}", [P, 1 + MORE], i32) for i in range(2)]
        rw = sb("rw", [P, KB, E])
        gb = sb("gb", [P, 2, E])

        with ExitStack() as st:
            g0_src_f = sb("g0_src_f", [P, ET], f32, st)
            g0_S = sb("g0_S", [P, HOT0, T], bf16, st)
            g0_D = sb("g0_D", [P, HOT0, T], bf16, st)
            g0_cnt = sb("g0_cnt", [P, NT, T], f32, st)
            g0_sum = sb("g0_sum", [P, NT, T], f32, st)
            g0_adj = sb("g0_adj", [P, NT, T], f32r, st)
            g0_rs = sb("g0_rs", [P, NT], f32, st)
            g0_rinv = sb("g0_rinv", [P, NT], f32, st)
            g0_xT_hi = sb("g0_xT_hi", [P, NT, KB, P], f32r, st)
            g0_xT_lo = sb("g0_xT_lo", [P, NT, KB, P], f32r, st)
            g0_h = sb("g0_h", [P, NT, D], f32, st)
            g0_cur = sb("g0_cur", [P, NT, D], f32, st)
            g0_wh = sb("g0_wh", [P, 3, NT, D], f32, st)
            g0_hi = sb("g0_hi", [P, NT, D], f32r, st)
            g0_lo = sb("g0_lo", [P, NT, D], f32r, st)
            g0_b = sb("g0_b", [P, D], f32, st)
            g0_w = sb("g0_w", [P, 4], f32, st)
        with ExitStack() as st:
            xn_hi = sb("xn_hi", [P, NT, D], f32r, st)
            xn_lo = sb("xn_lo", [P, NT, D], f32r, st)
            xe_hi = sb("xe_hi", [P, KB, P], f32r, st)
            xe_lo = sb("xe_lo", [P, KB, P], f32r, st)
            act3 = sb("act3", [P, 3, C], f32, st)
            hT_hi = sb("hT_hi", [P, 2 * KB, P], f32r, st)
            hT_lo = sb("hT_lo", [P, 2 * KB, P], f32r, st)
            y_hi = sb("y_hi", [P, D], f32r, st)
            y_lo = sb("y_lo", [P, D], f32r, st)
            G = sb("G", [P, 2, NT, P], f32r, st)
            GT = sb("GT", [P, 3, T], f32r, st)
            wslot = sb("wslot", [P, 3], f32, st)
            turner = sb("turner", [P, NT, TURN], f32r, st)
            sel_v = sb("sel_v", [2 * E, E, P], f32, st)
            sel_a = sb("sel_a", [2 * E, E, P], f32, st)
            sel = sb("sel", [2 * E, E, P], f32r, st)
            b_hi = sb("b_hi", [2 * E, 3 * C], f32r, st)
            b_rows = sb("b_rows", [2 * E, 3 * C], f32r, st)
            alpha = sb("alpha", [2 * E, 1], f32, st)
            hid = sb("hid", [P, 2, T], f32, st)
            lg = sb("lg", [P, NT, E], f32, st)
            pr = sb("pr", [P, NT, E], f32, st)
            red = sb("red", [P, NT], f32, st)
            red2 = sb("red2", [P, NT], f32, st)
            top = sb("top", [P, NT, 8], f32, st)
            topi = sb("topi", [P, NT, 8], u32, st)
            topf = sb("topf", [P, NT, 8], f32, st)
            tw = sb("tw", [P, NT, 4], f32, st)
            oh = sb("oh", [P, NT, 2, E], f32, st)
            mask = sb("mask", [P, NT, E], f32, st)
            comb = sb("comb", [P, NT, E], f32, st)
            combT = sb("combT", [E, T], f32, st)
            posm = sb("posm", [P, NT, E], f32, st)
            penal = sb("penal", [P, NT, E], f32, st)
            tri = sb("tri", [P, T], f32, st)
            over = sb("over", [P, E], f32, st)
            rank = sb("rank", [P, E], f32, st)
            picked = sb("picked", [P, MORE, E], f32, st)
            prod = sb("prod", [P, 2 * NT, E], f32, st)
            ids = sb("ids", [P, 1 + MORE], f32, st)
            more_pc = sb("more_pc", [P, MORE, 2 * NT], f32, st)
            sel_m = sb("sel_m", [2 * E, 2, P], f32, st)
            sel_more = sb("sel_more", [2 * E, MORE, P], f32r, st)
            b_raw = sb("b_raw", [2 * E, 3 * C], f32, st)
            b_out = sb("b_out", [E, D], f32, st)
            gw1 = sb("gw1", [P, KB, 256], f32, st)
            gb1 = sb("gb1", [P, 2], f32, st)
            gw2 = sb("gw2", [P, 2, E], f32, st)
        with ExitStack() as st:
            g1_xT_hi = sb("g1_xT_hi", [P, NT, KB, P], f32r, st)
            g1_xT_lo = sb("g1_xT_lo", [P, NT, KB, P], f32r, st)
            A_sb = sb("A_sb", [P, NT, D], f32, st)
            gh = sb("gh", [P, NT, 3, D], f32, st)
            w1e_hi = sb("w1e_hi", [P, D], f32r, st)
            w1e_lo = sb("w1e_lo", [P, D], f32r, st)
            onehot = sb("onehot", [P, HOT1, T], f32r, st)
            gb_rows = sb("gb_rows", [4, 3 * D], f32r, st)
            gsel = sb("gsel", [4, 3, P], f32r, st)
            galpha = sb("galpha", [4, 1], f32, st)
            with ExitStack() as st2:
                ea = sb("ea", [P, 3, GRP * P], f32, st2)
                ea_hi = sb("ea_hi", [P, 2, GRP * P], f32r, st2)
                ea_lo = sb("ea_lo", [P, 2, GRP * P], f32r, st2)
                gath = sb("gath", [P, GATH, D], f32, st2)
                mp = sb("mp", [P, SUMS, D], f32, st2)
                m_hi = sb("m_hi", [P, MSG, D], f32r, st2)
                m_lo = sb("m_lo", [P, MSG, D], f32r, st2)
            with ExitStack() as st2:
                pad = sb("pad0", [P, 7, GRP * P], f32, st2)
                gb_raw = sb("gb_raw", [4, 3 * D], f32, st2)
                g1_it = sb("g1_it", [4, 3, P], f32, st2)
                g1_t = sb("g1_t", [4, 3, P], f32, st2)
            with ExitStack() as st2:
                S1 = sb("S1", [P, NT, D], f32, st2)
                agg = sb("agg", [P, NT, D], f32, st2)
                aT_hi = sb("aT_hi", [P, NT, KB, P], f32r, st2)
                aT_lo = sb("aT_lo", [P, NT, KB, P], f32r, st2)
                rz = sb("rz", [P, NT, 3, D], f32, st2)
            edge_space = sb("edge_space", [P, 40 * 256], f32, st)
            w1e = sb("w1e", [P, D], f32, st)
            g2s = sb("g2s", [P, D], f32, st)
            g2b = sb("g2b", [P, D], f32, st)
            g2m = sb("g2m", [P, D], f32, st)
            g2v = sb("g2v", [P, D], f32, st)
            b1 = sb("b1", [P, D], f32, st)
            b2 = sb("b2", [P, D], f32, st)

        B = [ctx.enter_context(nc.psum_tensor(f"bank{i}", [P, C], f32)) for i in range(8)]

        def quarters(bank):
            return bank[:, :].rearrange("p (k t) -> p k t", k=KB)

        def diffusion_bank(step, n):
            return 2 + NT * (step % 2) + n

        raw_in = [sem(f"raw_in{i}") for i in range(RAW)]
        hi_cut = sem("hi_cut")
        lo_cut = sem("lo_cut")
        chunk_used = sem("chunk_used")
        layer_done = sem("layer_done")
        x_in, idx_in, par0, par1, par2, par3 = (sem(n) for n in (
            "x_in", "idx_in", "par0", "par1", "par2", "par3"))
        PAR1 = (16 * 9, 16 * 12)
        iota_ok = sem("iota_ok")
        half_ok = sem("half_ok")
        var_ok = sem("var_ok")
        rstd_ok = sem("rstd_ok")
        consts_ok = sem("consts_ok")
        xn_ok = sem("xn_ok")
        xt_ps = sem("xt_ps")
        xt_sb = sem("xt_sb")
        dve_chain = sem("dve_chain")
        pool_chain = sem("pool_chain")

        class Chain:

            def __init__(self, eng, s):
                self.eng, self.s, self.n = eng, s, 0

            def __call__(self, ins):
                self.n += 1
                ins.then_inc(self.s, 1)
                self.eng.wait_ge(self.s, self.n)

        def further_jobs(eng, number, before, job):
            def run_from(e):
                if e + 1 == E + MORE:
                    job(e, False)
                    return
                with eng.If(number > e + 1 - E):
                    job(e, True)
                    run_from(e + 1)
                with eng.If(number < e + 2 - E):
                    job(e, False)

            with eng.If(number > 0):
                before(True)
                run_from(E)
            with eng.If(number < 1):
                before(False)

        def both_tiles(eng, n, first_tile, value, chunk):
            if n == 0:
                eng.wait_ge(first_tile, value)
            else:
                eng.wait_ge(chunk_used, chunk + 1)

        class Run:
            def __init__(self, name, layer):
                self.layer = layer
                self.n_in, self.n_out = (FFN_IN, FFN_OUT) if layer == 0 else (LSTM_IN, LSTM_OUT)
                self.order = FFN_ORDER if layer == 0 else LSTM_ORDER
                self.at = {key: n for n, key in enumerate(self.order)}
                self.tag = "ffn" if layer == 0 else "lstm"
                self.g_built = sem(f"{name}_g_built")
                self.gather_ps = sem(f"{name}_gather_ps")
                self.turn_ps = sem(f"{name}_turn_ps")
                self.xe_cut = sem(f"{name}_xe_cut")
                self.gt_sb = sem(f"{name}_gt_sb")
                self.gates = sem(f"{name}_gates")
                self.h_ok = sem(f"{name}_h_ok")
                self.hT_ps = sem(f"{name}_hT_ps")
                self.hT_hi = sem(f"{name}_hT_hi")
                self.hT_lo = sem(f"{name}_hT_lo")
                self.y_cut = sem(f"{name}_y_cut")
                self.sum_ps = sem(f"{name}_sum_ps")
                self.banks_h = 2 if layer == 0 else 1
                self.base = CHUNK[self.order[0]]
                self.end = self.base + len(self.order)
                self.more_in = [sem(f"{name}_more_in{i}") for i in range(RAW)]
                self.more_hi, self.more_lo, self.more_used = (sem(f"{name}_{n}") for n in (
                    "more_hi", "more_lo", "more_used"))

            def chunk(self, kind, e, c):
                if e >= E:
                    return self.end + EC * (e - E) + (c if kind == "in" else self.n_in + c)
                return self.base + self.at[(self.tag, kind, e, c)]

            def used(self, q):
                return (chunk_used, q + 1) if q < self.end else (self.more_used, q - self.end + 1)

            def lo(self, q):
                return (lo_cut, q + 1) if q < self.end else (self.more_lo, q - self.end + 1)

            def last_in(self, e):
                return self.chunk("in", e, self.n_in - 1)

            def last_out(self, e):
                return self.chunk("out", e, self.n_out - 1)

        ffn, lstm = Run("ffn", 0), Run("lstm", 1)
        gate = {n: sem(f"gate_{n}") for n in (
            "hid_ps", "hid_sb", "lg_ps", "shift", "exp", "d", "dexp", "mask", "pos_ps", "route",
            "combT", "more", "xn_cut", "par", "rows")}

        g0 = {n: sem(f"g0_{n}") for n in ("hot", "used", "cnt", "turn_ps", "adj", "h_ps",
                                          "cur", "cut", "lo", "ps", "xT_hi", "wh")}
        more_chain = [sem("ffn_more_chain"), sem("lstm_more_chain")]
        g1 = {n: sem(f"g1_{n}") for n in (
            "a_ps", "a_sb", "a_out", "gh_ps", "gh_sb", "w1e_hi", "w1e_lo", "ea_hi", "ea_lo", "e_ps",
            "mp", "m_hi", "m_lo", "hot_even", "hot_odd", "sum_ps", "s1", "s1T_ps", "aT", "agg_ps", "agg", "aggT_ps",
            "gi_ps", "rz_in", "rz", "n_in", "n", "rows", "bn", "gsel", "x_base")}
        ea_in = [sem(f"g1_ea_in{i}") for i in range(3)]
        gath_in = [sem(f"g1_gath_in{i}") for i in range(GATH)]
        out_done = sem("out_done")

        block = ctx.enter_context(nc.Block())

        weights = A["weights"]

        @block.sync
        def _(sp):
            sp.dma_start(x[:, :, :], A["x"].rearrange("(n p) d -> p n d", p=P)).then_inc(x_in, 16)
            sp.dma_start(src_i[:, :], A["src"]).then_inc(idx_in, 16)
            sp.dma_start(dst_i[:, :], A["dst"]).then_inc(idx_in, 16)

            def load(n, former_cut, arrived, source):
                if former_cut:
                    sp.wait_ge(*former_cut)
                sp.dma_start(raw[n % RAW][:, :, :], source).then_inc(arrived, 16)

            def main(keys):
                for key in keys:
                    n = CHUNK[key]
                    load(n, (lo_cut, n - RAW + 1) if n >= RAW else None, raw_in[n % RAW],
                         weights[PLACE[key], :, :, :])

            def more(run):
                sp.wait_ge(gate["more"], run.layer + 1)
                table = more_i[run.layer]
                number = sp.value_load(table[0:1, 0:1], min_val=0, max_val=MORE)
                for job in range(MORE):
                    with sp.If(number > job):
                        expert = sp.value_load(table[0:1, 1 + job:2 + job], min_val=0, max_val=E - 1)
                        for c in range(EC):
                            q = EC * job + c
                            first = PLACE[(run.tag, "in", 0, 0)] + c
                            load(run.end + q, run.lo(run.end + q - RAW), run.more_in[q % RAW],
                                 weights[bass.ds(expert * EC + first, 1), :, :, :]
                                 .rearrange("a p k c -> (a p) k c"))
                for job in range(MORE):
                    with sp.If(number > job):
                        sp.wait_ge(run.more_lo, EC * (job + 1))

            def edge_attr(g):
                if g >= 3:
                    sp.wait_ge(g1["ea_hi"], g - 2)
                    sp.wait_ge(g1["ea_lo"], g - 2)
                n = min(GRP, ET - g * GRP) * P
                sp.dma_start(ea[:, g % 3, 0:n], A["ea"][:, g * GRP * P:g * GRP * P + n]).then_inc(ea_in[g % 3], 16)

            main([("L0", "W")] + FFN_ORDER)
            more(ffn)
            main(GNN_ORDER[0:4])
            sp.wait_ge(layer_done, 2)
            for g in range(3):
                edge_attr(g)
            main(GNN_ORDER[4:8])
            for g in range(3, NG):
                edge_attr(g)
            main(LSTM_ORDER)
            more(lstm)
            sp.wait_ge(layer_done, 4)
            sp.dma_start(out.rearrange("(n p) d -> p n d", p=P), x[:, :, :]).then_inc(out_done, 16)
            sp.wait_ge(out_done, 16)

        @block.gpsimd
        def _(pool):
            pool.iota(iota_t[:, :], [[1, T]], base=0, channel_multiplier=0,
                      allow_small_or_imprecise_dtypes=True).then_inc(iota_ok, 1)
            pool.iota(node_id[:, :], [[P, NT]], base=0, channel_multiplier=1,
                      allow_small_or_imprecise_dtypes=True).then_inc(iota_ok, 1)
            pool.dma_start(g0_b[:, :], A["L0_gnn_b"].partition_broadcast(P)).then_inc(par0, 16)
            pool.dma_start(g0_w[:, :], A["L0_gnn_diffusion_weights"].partition_broadcast(P)).then_inc(par0, 16)

            pool.memset(minus_half[:, :], -0.5).then_inc(half_ok, 1)
            pool.wait_ge(half_ok, 1)

            def root(layer):
                pool.wait_ge(var_ok, layer + 1)
                pool.tensor_tensor(rstd[:, :], var_eps[:, :], minus_half[:, :], ALU.pow).then_inc(rstd_ok, 1)

            root(0)
            bn_link = Chain(pool, pool_chain)

            def moe_params(b_in, b_o):
                n = b_in.shape[1]
                pool.dma_start(b_raw[0:E, 0:n], b_in).then_inc(par1, 16)
                pool.dma_start(b_raw[E:2 * E, 0:n], b_in).then_inc(par1, 16)
                pool.dma_start(b_out[:, :], b_o).then_inc(par1, 16)

            for nth, name in enumerate(("L0_ffn_gb2", "L1_ffn_router_b")):
                pool.dma_start(gb[:, nth, :], A[name].partition_broadcast(P)).then_inc(par1, 16)
            pool.dma_start(rw[:, :, :], A["L1_ffn_router_w"].rearrange("(k p) n -> p k n", p=P)).then_inc(par1, 16)
            pool.dma_start(gw1[:, :, :], A["L0_ffn_gw1"].rearrange("(k p) n -> p k n", p=P)).then_inc(par1, 16)
            pool.dma_start(gb1[:, :], A["L0_ffn_gb1"]).then_inc(par1, 16)
            pool.dma_start(gw2[:, :, :], A["L0_ffn_gw2"].rearrange("(k p) n -> p k n", p=P)).then_inc(par1, 16)
            moe_params(A["L0_ffn_be1"], A["L0_ffn_be2"])
            for dst, name in ((g2v, "run_var"), (b1, "b1"), (b2, "b2"), (g2s, "gamma"),
                              (g2b, "beta"), (g2m, "run_mean")):
                pool.dma_start(dst[:, :], A["L1_gnn_" + name].partition_broadcast(P)).then_inc(par2, 16)
            pool.dma_start(w1e[:, :], A["w1e"]).then_inc(par2, 16)
            pool.wait_ge(par2, 16 * 7)
            pool.tensor_scalar(g2v[:, :], g2v[:, :], EPS, None, ALU.add).then_inc(g1["bn"], 1)
            root(1)
            pool.wait_ge(layer_done, 1)
            pool.iota(sel_v[:, :, :], [[-1, E], [0, P]], base=0, channel_multiplier=1,
                      allow_small_or_imprecise_dtypes=True).then_inc(gate["par"], 1)

            pool.wait_ge(g1["bn"], 3)
            bn_link(pool.tensor_tensor(g2s[:, :], g2s[:, :], g2v[:, :], ALU.mult))
            bn_link(pool.tensor_tensor(g2m[:, :], g2m[:, :], g2s[:, :], ALU.mult))
            bn_link(pool.tensor_tensor(g2b[:, :], g2b[:, :], g2m[:, :], ALU.subtract))
            root(2)
            for r in range(4):
                pool.dma_start(gb_raw[r:r + 1, :], A["L1_gnn_b_ih" if r % 2 == 0 else "L1_gnn_b_hh"]).then_inc(par3, 16)
            pool.iota(g1_it[:, :, :], [[0, 3], [0, P]], base=0, channel_multiplier=1,
                      allow_small_or_imprecise_dtypes=True).then_inc(gate["par"], 1)

            for n in range(NT):
                pool.wait_ge(g1["a_sb"], n + 1)
                pool.dma_start(node_rows[n * P:(n + 1) * P, :], A_sb[:, n, :]).then_inc(g1["a_out"], 16)

            def hot(t):
                if t >= HOT1:
                    pool.wait_ge(g1["sum_ps"], t - HOT1 + 1)
                pool.tensor_scalar(onehot[:, t % HOT1, :], iota_t[:, :], dst_f[:, t:t + 1], None,
                                   ALU.is_equal).then_inc(g1["hot_even"], 1)

            pool.wait_ge(g1["rows"], 2)
            pool.wait_ge(g1["a_out"], 16 * NT)
            for t in range(ET):
                if t >= GATH:
                    pool.wait_ge(g1["mp"], t - GATH + 1)
                pool.indirect_dma_start(
                    out=gath[:, t % GATH, :], out_offset=None, in_=node_rows[:, :],
                    in_offset=bass.IndirectOffsetOnAxis(ap=src_i[:, t:t + 1], axis=0)).then_inc(gath_in[t % GATH], 16)
                if t >= 1 and t % 2:
                    hot(t - 1)

            for n in range(NT):
                bn_link(pool.tensor_tensor(x[:, n, :], x[:, n, :], g2b[:, :], ALU.add))
                pool.tensor_tensor(x[:, n, :], x[:, n, :], xn[:, n, :], ALU.add).then_inc(g1["x_base"], 1)

            root(3)
            pool.iota(sel_v[:, :, :], [[-1, E], [0, P]], base=0, channel_multiplier=1,
                      allow_small_or_imprecise_dtypes=True).then_inc(gate["par"], 1)
            moe_params(A["lstm_b"], A["L1_ffn_bo"])

        @block.scalar
        def _(act):
            def cut_hi(n):
                act.wait_ge(raw_in[n % RAW], 16 * (n // RAW + 1))
                if n >= SPL:
                    act.wait_ge(chunk_used, n - SPL + 1)
                act.activation(whi[n % SPL][:, :, :], raw[n % RAW][:, :, :], ACT.Copy).then_inc(hi_cut, 1)

            def more_hi(run, q):
                act.wait_ge(run.more_in[(q - run.end) % RAW], 16 * ((q - run.end) // RAW + 1))
                act.wait_ge(*run.used(q - SPL))
                act.activation(whi[q % SPL][:, :, :], raw[q % RAW][:, :, :], ACT.Copy)\
                   .then_inc(run.more_hi, 1)

            done = [0]

            def cut_to(n):
                while done[0] < n:
                    cut_hi(done[0])
                    done[0] += 1

            def xT_copy(layer, dst):
                for n in range(NT):
                    act.wait_ge(xt_ps, NT * layer + n + 1)
                    act.activation(dst[:, n, :, :], quarters(B[5 - n]), ACT.Copy).then_inc(xt_sb, 1)

            def experts(run):
                def cuts(upto):
                    cut_to(min(upto, run.base + len(run.order)))

                def xe(e):
                    act.wait_ge(run.gather_ps, e + 1)
                    act.activation(xe_hi[:, :, :], quarters(B[6]), ACT.Copy).then_inc(run.xe_cut, 1)

                def outputs(e):
                    act.wait_ge(*run.used(run.last_out(e)))
                    act.wait_ge(run.gt_sb, e + 1)
                    act.activation(y_hi[:, :], B[7][:, :], ACT.Copy,
                                   scale=wslot[:, e % 3:e % 3 + 1]).then_inc(run.y_cut, 1)

                def turned(e):
                    for b in range(run.banks_h):
                        act.wait_ge(run.hT_ps, run.banks_h * e + b + 1)
                        act.activation(hT_hi[:, KB * b:KB * b + KB, :], quarters(B[5 - b]),
                                       ACT.Copy).then_inc(run.hT_hi, 1)

                def results(e):
                    if run.layer == 0:
                        for c in range(2):
                            act.wait_ge(*run.used(run.chunk("in", e, c)))
                            act.activation(act3[:, c, :], B[2 + c][:, :], ACT.Gelu).then_inc(run.h_ok, 1)
                        return
                    for c, f in ((0, ACT.Sigmoid), (1, ACT.Tanh), (2, ACT.Sigmoid)):
                        act.wait_ge(*run.used(run.chunk("in", e, c)))
                        act.activation(act3[:, c, :], B[2 + c][:, :], f).then_inc(run.gates, 1)
                        if e + 1 < E and c < 2:
                            cuts(run.chunk("in", e, c) + SPL + 1)
                    act.wait_ge(run.h_ok, 2 * e + 1)
                    act.activation(act3[:, 1, :], act3[:, 0, :], ACT.Tanh).then_inc(run.gates, 1)

                def more_cuts(first, upto):
                    for q in range(max(first, run.end), upto):
                        more_hi(run, q)

                cuts(run.base + SPL)
                xe(0)
                for step in range(E):
                    if step >= 2:
                        outputs(step - 2)
                    if step >= 1:
                        turned(step - 1)
                    if step >= 2:
                        cuts(run.last_out(step - 2) + SPL + 1)
                    results(step)
                    if step + 1 < E:
                        xe(step + 1)
                    else:
                        act.wait_ge(gate["more"], run.layer + 1)
                        number = act.value_load(more_i[run.layer][0:1, 0:1], min_val=0, max_val=MORE)
                        with act.If(number > 0):
                            xe(E)
                    cuts(run.last_in(step) + SPL + 1)
                outputs(E - 2)
                turned(E - 1)

                def before(followed):
                    if followed:
                        more_cuts(run.end, run.last_out(E - 2) + SPL + 1)
                    outputs(E - 1)

                def job(e, followed):
                    more_cuts(run.last_out(E - 2) + SPL + 1 if e == E else run.chunk("out", e, 0),
                              run.last_out(e) + 1)
                    results(e)
                    if followed:
                        xe(e + 1)
                    turned(e)
                    if followed:
                        more_cuts(run.chunk("in", e + 1, 0), run.last_in(e + 1) + 1)
                    outputs(e)

                further_jobs(act, number, before, job)

            cut_to(1)
            for n in range(NT):
                act.wait_ge(xt_ps, n + 1)
                act.activation(g0_xT_hi[:, n, :, :], quarters(B[5 - n]), ACT.Copy).then_inc(g0["xT_hi"], 1)
            cut_to(2)
            for i in range(3):
                for n in range(NT):
                    act.wait_ge(g0["cur"], NT * i + n + 1)
                    act.activation(g0_hi[:, n, :], g0_cur[:, n, :], ACT.Copy).then_inc(g0["cut"], 1)
                if i == 0:
                    for n in range(NT):
                        for j in range(3):
                            act.activation(g0_wh[:, j, n, :], g0_h[:, n, :], ACT.Copy,
                                           scale=g0_w[:, 2 - j:3 - j]).then_inc(g0["wh"], 1)
                    cut_to(4)
            act.wait_ge(g1["bn"], 1)
            act.activation(g2v[:, :], g2v[:, :], ACT.Sqrt).then_inc(g1["bn"], 1)

            def gating(nth):
                act.wait_ge(xn_ok, NT * (2 * nth - 1) + NT)
                xT_copy(2 * nth - 1, xnT)
                cut_to(SPL if nth == 1 else CHUNK[LSTM_ORDER[0]] + SPL)
                act.activation(xn_hi[:, :, :], xn[:, :, :], ACT.Copy).then_inc(gate["xn_cut"], 1)
                act.wait_ge(par1, PAR1[nth - 1])
                n = 2 * C if nth == 1 else 3 * C
                act.activation(b_hi[:, 0:n], b_raw[:, 0:n], ACT.Copy).then_inc(gate["xn_cut"], 1)
                if nth == 1:
                    for b in range(2):
                        act.wait_ge(gate["hid_ps"], b + 1)
                        act.activation(hid[:, b, :], B[2 + b][:, 0:T],
                                       ACT.Relu, bias=gb1[:, b:b + 1]).then_inc(gate["hid_sb"], 1)
                    act.wait_ge(gate["shift"], 1)
                    act.activation(pr[:, :, :], lg[:, :, :], ACT.Exp).then_inc(gate["exp"], 1)
                act.wait_ge(gate["d"], nth)
                act.activation(tw[:, :, 1], tw[:, :, 0], ACT.Exp).then_inc(gate["dexp"], 1)

            gating(1)
            experts(ffn)

            first = CHUNK[("gnn", "W1")]
            cut_to(first + 2)
            for n in range(NT):
                act.wait_ge(xt_ps, 2 * NT + n + 1)
                act.activation(g1_xT_hi[:, n, :, :], quarters(B[5 - n]), ACT.Copy).then_inc(xt_sb, 1)
            act.wait_ge(par2, 16 * 7)
            act.activation(w1e_hi[:, :], w1e[:, :], ACT.Copy).then_inc(g1["w1e_hi"], 1)
            cut_to(first + 3)
            act.wait_ge(par3, 16 * 4)
            act.activation(gb_rows[:, :], gb_raw[:, :], ACT.Copy).then_inc(g1["rows"], 1)
            cut_to(first + SPL)

            def ea_cut(g):
                n = min(GRP, ET - g * GRP) * P
                act.wait_ge(ea_in[g % 3], 16 * (g // 3 + 1))
                if g >= 2:
                    act.wait_ge(g1["e_ps"], GRP * (g - 1))
                act.activation(ea_hi[:, g % 2, 0:n], ea[:, g % 3, 0:n], ACT.Copy).then_inc(g1["ea_hi"], 1)

            ea_cut(0)
            ea_cut(1)

            def gh_copy(g, n):
                both_tiles(act, n, g1["gh_ps"], g + 1, CHUNK[("gnn", "Whh", g)])
                act.activation(gh[:, n, g, :], B[(6, 2, 4)[g] + n][:, :], ACT.Copy).then_inc(g1["gh_sb"], 1)

            for g in range(2):
                for n in range(NT):
                    gh_copy(g, n)
                if g == 0:
                    cut_to(first + SPL + 1)
            for t in range(ET):
                act.wait_ge(g1["mp"], t + 1)
                if t >= MSG:
                    act.wait_ge(g1["sum_ps"], t - MSG + 1)
                act.activation(m_hi[:, t % MSG, :], mp[:, t % SUMS, :], ACT.Relu).then_inc(g1["m_hi"], 1)
                if t % GRP == 1 and t // GRP + 1 < NG and t >= GRP:
                    ea_cut(t // GRP + 1)
            for n in range(NT):
                act.wait_ge(g1["s1T_ps"], n + 1)
                act.activation(aT_hi[:, n, :, :], quarters(B[6 + n]), ACT.Copy).then_inc(g1["aT"], 1)
            cut_to(first + 2 * SPL - 1)
            for n in range(NT):
                gh_copy(2, n)
            cut_to(first + 2 * SPL)
            for n in range(NT):
                act.wait_ge(g1["aggT_ps"], n + 1)
                act.activation(aT_hi[:, n, :, :], quarters(B[6 + n]), ACT.Copy).then_inc(g1["aT"], 1)
            cut_to(first + 2 * SPL + 1)
            for n in range(NT):
                for g in range(2):
                    act.wait_ge(g1["rz_in"], 2 * n + g + 1)
                    act.activation(rz[:, n, g, :], rz[:, n, g, :], ACT.Sigmoid).then_inc(g1["rz"], 1)
                act.wait_ge(g1["n_in"], n + 1)
                act.activation(rz[:, n, 2, :], rz[:, n, 2, :], ACT.Tanh).then_inc(g1["n"], 1)
            cut_to(first + 2 * SPL + 3)

            gating(2)
            experts(lstm)

        @block.vector
        def _(dve):
            link = Chain(dve, dve_chain)

            def cut_lo(n):
                dve.wait_ge(hi_cut, n + 1)
                dve.tensor_tensor(wlo[n % SPL][:, :, :], raw[n % RAW][:, :, :],
                                  whi[n % SPL][:, :, :].bitcast(f32), ALU.subtract).then_inc(lo_cut, 1)

            def more_lo(run, q):
                dve.wait_ge(run.more_hi, q - run.end + 1)
                dve.tensor_tensor(wlo[q % SPL][:, :, :], raw[q % RAW][:, :, :],
                                  whi[q % SPL][:, :, :].bitcast(f32), ALU.subtract).then_inc(run.more_lo, 1)

            done = [0]

            def cut_to(n):
                while done[0] < n:
                    cut_lo(done[0])
                    done[0] += 1

            def layernorm(layer):
                for n in range(1 if layer == 3 else 0, NT):
                    ins = dve.bn_stats(stats[:, n, :], x[:, n, :])
                link(ins)
                for n in range(NT):
                    ins = dve.bn_aggr(mv[:, n, :], stats[:, n, :])
                link(ins)
                dve.tensor_scalar(var_eps[:, :], mv[:, :, 1], EPS, None, ALU.add).then_inc(var_ok, 1)
                dve.wait_ge(rstd_ok, layer + 1)
                for n in range(NT):
                    dve.tensor_scalar(xn[:, n, :], x[:, n, :], mv[:, n, 0:1], rstd[:, n:n + 1],
                                      ALU.subtract, ALU.mult).then_inc(xn_ok, 1)

            dve.wait_ge(iota_ok, 2)
            for n in range(NT):
                ins = dve.tensor_scalar(eye2[:, n, :], iota_t[:, :], node_id[:, n:n + 1], None, ALU.is_equal)
            link(ins)
            link(dve.tensor_copy(iota_b[:, :], iota_t[:, :]))
            dve.wait_ge(x_in, 16)
            layernorm(0)
            dve.wait_ge(idx_in, 32)
            dve.tensor_copy(g0_src_f[:, :], src_i[:, :]).then_inc(consts_ok, 1)
            dve.tensor_copy(dst_f[:, :], dst_i[:, :]).then_inc(consts_ok, 1)
            dve.wait_ge(consts_ok, 2)
            cut_to(1)
            for n in range(NT):
                dve.wait_ge(g0["xT_hi"], n + 1)
                dve.tensor_tensor(g0_xT_lo[:, n, :, :], quarters(B[5 - n]),
                                  g0_xT_hi[:, n, :, :].bitcast(f32), ALU.subtract).then_inc(xt_sb, 1)

            def edge_hots(first, last):
                for t in range(first, last):
                    if t >= HOT0:
                        dve.wait_ge(g0["used"], t - HOT0 + 1)
                    dve.tensor_scalar(g0_S[:, t % HOT0, :], iota_b[:, :], g0_src_f[:, t:t + 1], None,
                                      ALU.is_equal)
                    dve.tensor_scalar(g0_D[:, t % HOT0, :], iota_b[:, :], dst_f[:, t:t + 1], None,
                                      ALU.is_equal).then_inc(g0["hot"], 1)

            edge_hots(0, HOT0)
            dve.wait_ge(par0, 32)
            for n in range(NT):
                both_tiles(dve, n, g0["h_ps"], 1, 0)
                link(dve.tensor_tensor(g0_h[:, n, :], B[2 + n][:, :], g0_b[:, :], ALU.add))
                dve.tensor_scalar(g0_cur[:, n, :], g0_h[:, n, :], g0_w[:, 3:4], None,
                                  ALU.mult).then_inc(g0["cur"], 1)
            edge_hots(HOT0, ET)
            for n in range(NT):
                dve.wait_ge(g0["cut"], n + 1)
                dve.tensor_tensor(g0_lo[:, n, :], g0_cur[:, n, :], g0_hi[:, n, :].bitcast(f32),
                                  ALU.subtract).then_inc(g0["lo"], 1)
            dve.wait_ge(g0["used"], ET)
            for n in range(NT):
                dve.tensor_copy(g0_cnt[:, n, :], B[n][:, 0:T]).then_inc(g0["cnt"], 1)
            dve.wait_ge(g0["turn_ps"], 1)
            dve.wait_ge(g0["cnt"], NT)
            for n in range(NT):
                ins = dve.tensor_tensor(g0_sum[:, n, :], B[6][:, n * T:(n + 1) * T], g0_cnt[:, n, :], ALU.add)
            link(ins)
            for n in range(NT):
                dve.scalar_tensor_tensor(out=g0_adj[:, n, :], in0=g0_sum[:, n, :], scalar=1.0,
                                         in1=eye2[:, n, :], op0=ALU.min, op1=ALU.add).then_inc(g0["adj"], 1)
            dve.wait_ge(g0["adj"], NT)
            link(dve.tensor_reduce(g0_rs[:, :], g0_adj[:, :, :].bitcast(f32), AX, ALU.add))
            link(dve.tensor_scalar(g0_rs[:, :], g0_rs[:, :], 1.0, None, ALU.max))
            link(dve.reciprocal(g0_rinv[:, :], g0_rs[:, :]))
            dve.wait_ge(g0["wh"], 3 * NT)
            for i in range(3):
                for n in range(NT):
                    dve.wait_ge(g0["ps"], NT * i + n + 1)
                    dve.scalar_tensor_tensor(out=g0_cur[:, n, :], in0=B[diffusion_bank(i, n)][:, :],
                                             scalar=g0_rinv[:, n:n + 1], in1=g0_wh[:, i, n, :],
                                             op0=ALU.mult, op1=ALU.add).then_inc(g0["cur"], 1)
                    if i < 2:
                        dve.wait_ge(g0["cut"], NT * (i + 1) + n + 1)
                        dve.tensor_tensor(g0_lo[:, n, :], g0_cur[:, n, :], g0_hi[:, n, :].bitcast(f32),
                                          ALU.subtract).then_inc(g0["lo"], 1)
                    else:
                        dve.wait_ge(g0["cur"], NT * 3 + n + 1)
                        link(dve.scalar_tensor_tensor(out=x[:, n, :], in0=g0_cur[:, n, :], scalar=0.0,
                                                      in1=x[:, n, :], op0=ALU.max, op1=ALU.add))
                if i == 0:
                    dve.tensor_reduce(deg[:, :], B[6][:, :].rearrange("p (n t) -> p n t", n=NT), AX, ALU.add)
                if i == 0:
                    cut_to(2)
            dve.drain().then_inc(layer_done, 1)

            def gating(nth):
                layernorm(2 * nth - 1)
                dve.tensor_scalar(tri[:, 0:P], iota_t[:, 0:P], node_id[:, 0:1], None, ALU.is_gt)
                dve.memset(tri[:, P:T], 1.0)
                for n in range(NT):
                    dve.tensor_copy(turner[:, n, 0:P], ident)
                dve.tensor_scalar(turner[:, :, P:TURN], iota_t[:, 0:2 * WJ].unsqueeze(1).to_broadcast([P, NT, 2 * WJ]),
                                  0.0, None, ALU.mult)
                cut_to(SPL if nth == 1 else CHUNK[LSTM_ORDER[0]] + 3)
                dve.wait_ge(gate["xn_cut"], 2 * nth - 1)
                dve.tensor_tensor(xn_lo[:, :, :], xn[:, :, :], xn_hi[:, :, :].bitcast(f32), ALU.subtract)
                dve.wait_ge(par1, PAR1[0])
                dve.wait_ge(gate["lg_ps"], nth)
                ps = B[6][:, 0:NT * E].rearrange("p (n e) -> p n e", n=NT)
                dst = lg if nth == 1 else pr
                link(dve.tensor_tensor(dst[:, :, :], ps, gb[:, nth - 1:nth, :].to_broadcast([P, NT, E]), ALU.add))
                if nth == 1:
                    link(dve.tensor_reduce(red[:, :], lg[:, :, :], AX, ALU.max))
                    dve.tensor_tensor(lg[:, :, :], lg[:, :, :],
                                      red[:, :].unsqueeze(2).to_broadcast([P, NT, E]), ALU.subtract)\
                       .then_inc(gate["shift"], 1)
                    dve.wait_ge(gate["exp"], 1)
                    link(dve.tensor_reduce(red2[:, :], pr[:, :, :], AX, ALU.add))
                    link(dve.reciprocal(red[:, :], red2[:, :]))
                    link(dve.tensor_tensor(pr[:, :, :], pr[:, :, :],
                                           red[:, :].unsqueeze(2).to_broadcast([P, NT, E]), ALU.mult))
                for m in range(NT):
                    ins = dve.max(top[:, m, :], pr[:, m, :])
                link(ins)
                for m in range(NT):
                    ins = dve.max_index(topi[:, m, :], top[:, m, :], pr[:, m, :])
                link(ins)
                dve.tensor_tensor(tw[:, :, 0], top[:, :, 1], top[:, :, 0], ALU.subtract).then_inc(gate["d"], 1)
                link(dve.tensor_copy(topf[:, :, :], topi[:, :, :]))
                link(dve.tensor_tensor(oh[:, :, :, :],
                                       iota_t[:, 0:E].unsqueeze(1).unsqueeze(1).to_broadcast([P, NT, 2, E]),
                                       topf[:, :, 0:2].unsqueeze(3).to_broadcast([P, NT, 2, E]), ALU.is_equal))
                dve.tensor_tensor(mask[:, :, :], oh[:, :, 0, :], oh[:, :, 1, :], ALU.add)\
                   .then_inc(gate["mask"], 1)
                dve.wait_ge(gate["mask"], nth)
                dve.tensor_scalar(penal[:, :, :], mask[:, :, :], -1000.0, 1000.0, ALU.mult, ALU.add)
                dve.wait_ge(gate["dexp"], nth)
                link(dve.tensor_scalar(tw[:, :, 2], tw[:, :, 1], 1.0, None, ALU.add))
                link(dve.reciprocal(tw[:, :, 2], tw[:, :, 2]))
                link(dve.tensor_tensor(tw[:, :, 3], tw[:, :, 1], tw[:, :, 2], ALU.mult))
                link(dve.tensor_tensor(oh[:, :, :, :], oh[:, :, :, :],
                                       tw[:, :, 2:4].unsqueeze(3).to_broadcast([P, NT, 2, E]), ALU.mult))
                link(dve.tensor_tensor(comb[:, :, :], oh[:, :, 0, :], oh[:, :, 1, :], ALU.add))
                link(dve.tensor_copy(turner[:, :, P:P + E], comb[:, :, :]))
                dve.tensor_tensor(turner[:, :, P + WJ:P + WJ + E], comb[:, :, :],
                                  turner[:, :, P:P + E].bitcast(f32), ALU.subtract)
                dve.wait_ge(gate["pos_ps"], nth)
                ps = B[6][:, 32:32 + NT * E].rearrange("p (n e) -> p n e", n=NT)
                link(dve.tensor_tensor(posm[:, :, :], ps, penal[:, :, :], ALU.add))
                dve.tensor_scalar(over[:, :], B[6][:, 64:64 + E], float(P), None, ALU.is_gt).then_inc(gate["route"], 1)

            def bias_rows(nth):
                dve.wait_ge(gate["par"], 1 if nth == 1 else 3)
                link(dve.tensor_scalar(sel_a[:, :, :], sel_v[:, :, :], 0.0, None, ALU.is_equal))
                dve.scalar_tensor_tensor(out=sel[:, :, :], in0=sel_v[:, :, :], scalar=float(E),
                                         in1=sel_a[:, :, :], op0=ALU.is_equal, op1=ALU.max)
                link(dve.tensor_scalar(alpha[:, :], node_id[0:2 * E, 0:1], float(E), -1.0, ALU.is_ge, ALU.mult))
                n = (2 if nth == 1 else 3) * C
                dve.wait_ge(gate["xn_cut"], 2 * nth)
                dve.scalar_tensor_tensor(out=b_rows[:, 0:n], in0=b_hi[:, 0:n].bitcast(f32),
                                         scalar=alpha[:, 0:1], in1=b_raw[:, 0:n],
                                         op0=ALU.mult, op1=ALU.add).then_inc(gate["rows"], 1)

            def more_experts(nth):
                dve.wait_ge(gate["route"], nth)
                link(dve.tensor_tensor_scan(rank[:, :], tri[:, P:P + E], over[:, :], 0.0, ALU.mult, ALU.add))
                for job in range(MORE):
                    link(dve.scalar_tensor_tensor(out=picked[:, job, :], in0=rank[:, :], scalar=job + 1.0,
                                                  in1=over[:, :], op0=ALU.is_equal, op1=ALU.mult))
                    link(dve.tensor_tensor(prod[:, 0, :], picked[:, job, :], iota_t[:, 0:E], ALU.mult))
                    link(dve.tensor_reduce(ids[:, 1 + job:2 + job], prod[:, 0, :], AX, ALU.add))
                link(dve.tensor_copy(ids[:, 0:1], rank[:, E - 1:E]))
                dve.tensor_copy(more_i[nth - 1][:, :], ids[:, :]).then_inc(gate["more"], 1)
                dve.wait_ge(gate["more"], nth)

            def experts(run):
                more_link = Chain(dve, more_chain[run.layer])

                def cuts(upto):
                    cut_to(min(upto, run.base + len(run.order)))

                def build_g(e):
                    if e >= 2:
                        dve.wait_ge(run.turn_ps, e - 1)
                    for n in range(NT):
                        slot = posm[:, n, e:e + 1] if e < E else more_pc[:, e - E, n:n + 1]
                        ins = dve.tensor_scalar(G[:, e % 2, n, :], iota_t[:, 0:P] if e < E else iota_t[:, P:T],
                                                slot, None, ALU.is_equal)
                    ins.then_inc(run.g_built, 1)

                def xe(e):
                    dve.wait_ge(run.xe_cut, 2 * e + 1)
                    dve.tensor_tensor(xe_lo[:, :, :], quarters(B[6]), xe_hi[:, :, :].bitcast(f32),
                                      ALU.subtract).then_inc(run.xe_cut, 1)
                    dve.wait_ge(run.turn_ps, e + 1)
                    turned_g = B[5][:, 0:NT * TURN].rearrange("p (n c) -> p n c", n=NT)
                    dve.tensor_copy(GT[:, e % 3, :].rearrange("p (n t) -> p n t", n=NT), turned_g[:, :, 0:P])
                    dve.tensor_reduce(wslot[:, e % 3:e % 3 + 1], turned_g[:, :, P + e:TURN:WJ],
                                      mybir.AxisListType.XY, ALU.add).then_inc(run.gt_sb, 1)

                def outputs(e):
                    dve.wait_ge(run.y_cut, 2 * e + 1)
                    dve.wait_ge(run.gt_sb, e + 1)
                    dve.scalar_tensor_tensor(out=y_lo[:, :], in0=B[7][:, :], scalar=wslot[:, e % 3:e % 3 + 1],
                                             in1=y_hi[:, :].bitcast(f32), op0=ALU.mult,
                                             op1=ALU.subtract).then_inc(run.y_cut, 1)

                def turned(e):
                    for b in range(run.banks_h):
                        dve.wait_ge(run.hT_hi, run.banks_h * e + b + 1)
                        dve.tensor_tensor(hT_lo[:, KB * b:KB * b + KB, :], quarters(B[5 - b]),
                                          hT_hi[:, KB * b:KB * b + KB, :].bitcast(f32),
                                          ALU.subtract).then_inc(run.hT_lo, 1)

                def results(e):
                    if run.layer == 1:
                        if e + 1 < E:
                            cuts(run.chunk("in", e, 0) + SPL + 1)
                        dve.wait_ge(run.gates, 4 * e + 2)
                        dve.tensor_tensor(act3[:, 0, :], act3[:, 0, :], act3[:, 1, :], ALU.mult)\
                           .then_inc(run.h_ok, 1)
                        if e + 1 < E:
                            cuts(run.chunk("in", e, 1) + SPL + 1)
                        dve.wait_ge(run.gates, 4 * e + 4)
                        dve.tensor_tensor(act3[:, 2, :], act3[:, 2, :], act3[:, 1, :], ALU.mult)\
                           .then_inc(run.h_ok, 1)

                def more_cuts(first, upto):
                    for q in range(max(first, run.end), upto):
                        more_lo(run, q)

                def prepare(e):
                    job = e - E
                    for n in range(NT):
                        for i, table in enumerate((posm, comb)):
                            ins = dve.tensor_tensor(prod[:, NT * i + n, :], table[:, n, :],
                                                    picked[:, job, :], ALU.mult)
                    more_link(ins)
                    more_link(dve.tensor_reduce(more_pc[:, job, :], prod[:, :, :], AX, ALU.add))
                    weight = more_pc[:, job, NT:2 * NT]
                    more_link(dve.tensor_copy(turner[:, :, P + e], weight))
                    dve.tensor_tensor(turner[:, :, P + WJ + e], weight, turner[:, :, P + e].bitcast(f32),
                                      ALU.subtract)
                    expert = ids[0:2 * E, 1 + job:2 + job]
                    dve.tensor_scalar(sel_m[:, 0, :], sel_v[:, 0, :], expert, None, ALU.is_equal)
                    more_link(dve.tensor_scalar(sel_m[:, 1, :], sel_v[:, 0, :], float(E), expert,
                                                ALU.subtract, ALU.is_equal))
                    more_link(dve.tensor_tensor(sel_more[:, job, :], sel_m[:, 0, :], sel_m[:, 1, :], ALU.max))
                    build_g(e)

                build_g(0)
                build_g(1)
                bias_rows(run.layer + 1)
                xe(0)
                cuts(run.base + SPL)
                comb_turned(run.layer + 1)
                more_experts(run.layer + 1)
                number = dve.value_load(more_i[run.layer][0:1, 0:1], min_val=0, max_val=MORE)
                for step in range(E):
                    if step >= 2:
                        outputs(step - 2)
                    if step >= 1:
                        turned(step - 1)
                    if step >= 2:
                        cuts(run.last_out(step - 2) + SPL + 1)
                    results(step)
                    if step + 1 < E:
                        xe(step + 1)
                    else:
                        with dve.If(number > 0):
                            xe(E)
                    if step + 2 < E:
                        build_g(step + 2)
                    elif step + 2 == E:
                        with dve.If(number > 0):
                            prepare(E)
                    cuts(run.last_in(step) + SPL + 1)
                    if run.layer == 0 and step == 3:
                        dve.wait_ge(g1["bn"], 2)
                        dve.reciprocal(g2v[:, :], g2v[:, :]).then_inc(g1["bn"], 1)
                outputs(E - 2)
                turned(E - 1)

                def before(followed):
                    if followed:
                        more_cuts(run.end, run.last_out(E - 2) + SPL + 1)
                    outputs(E - 1)
                    if not followed:
                        dve.wait_ge(run.sum_ps, E)

                def job(e, followed):
                    if followed:
                        prepare(e + 1)
                    more_cuts(run.last_out(E - 2) + SPL + 1 if e == E else run.chunk("out", e, 0),
                              run.last_out(e) + 1)
                    results(e)
                    if followed:
                        xe(e + 1)
                    turned(e)
                    if followed:
                        more_cuts(run.chunk("in", e + 1, 0), run.last_in(e + 1) + 1)
                    outputs(e)
                    if not followed:
                        dve.wait_ge(run.sum_ps, e + 1)

                further_jobs(dve, number, before, job)
                for n in range(NT):
                    ins = dve.tensor_tensor(x[:, n, :], x[:, n, :], B[n][:, :], ALU.add)
                link(ins)

            def comb_turned(nth):
                dve.wait_ge(gate["combT"], 2 * nth - 1)
                dve.tensor_copy(combT[:, :], B[7][0:E, 0:T]).then_inc(gate["combT"], 1)

            gating(1)
            experts(ffn)
            dve.drain().then_inc(layer_done, 1)

            layernorm(2)
            first = CHUNK[("gnn", "W1")]
            cut_to(first + 1)
            dve.wait_ge(xt_sb, 3 * NT)
            for n in range(NT):
                dve.tensor_tensor(g1_xT_lo[:, n, :, :], quarters(B[5 - n]),
                                  g1_xT_hi[:, n, :, :].bitcast(f32), ALU.subtract).then_inc(xt_sb, 1)
            cut_to(first + 2)
            dve.wait_ge(gate["par"], 2)
            link(dve.tensor_scalar(galpha[:, :], node_id[0:4, 0:1], 2.0, -1.0, ALU.is_ge, ALU.mult))
            for i, row in ((2, 0.0), (1, 1.0)):
                link(dve.tensor_scalar(g1_t[:, i, :], g1_it[:, i, :], row, None, ALU.is_equal))
                link(dve.scalar_tensor_tensor(out=gsel[:, i, :], in0=g1_it[:, i, :], scalar=row + 2.0,
                                              in1=g1_t[:, i, :], op0=ALU.is_equal, op1=ALU.max))
            dve.tensor_scalar(gsel[:, 0, :], g1_it[:, 0, :], 0.0, None, ALU.is_ge).then_inc(g1["gsel"], 1)
            dve.wait_ge(par2, 16 * 7)
            for n in range(NT):
                both_tiles(dve, n, g1["a_ps"], 1, CHUNK[("gnn", "W1")])
                dve.tensor_tensor(A_sb[:, n, :], B[2 + n][:, :], b1[:, :], ALU.add).then_inc(g1["a_sb"], 1)
            dve.wait_ge(g1["rows"], 1)
            dve.scalar_tensor_tensor(out=gb_rows[:, :], in0=gb_rows[:, :].bitcast(f32),
                                     scalar=galpha[:, 0:1], in1=gb_raw[:, :],
                                     op0=ALU.mult, op1=ALU.add).then_inc(g1["rows"], 1)
            cut_to(first + SPL)
            dve.wait_ge(g1["w1e_hi"], 1)
            dve.tensor_tensor(w1e_lo[:, :], w1e[:, :], w1e_hi[:, :].bitcast(f32), ALU.subtract)\
               .then_inc(g1["w1e_lo"], 1)

            def ea_cut(g):
                n = min(GRP, ET - g * GRP) * P
                dve.wait_ge(g1["ea_hi"], g + 1)
                dve.tensor_tensor(ea_lo[:, g % 2, 0:n], ea[:, g % 3, 0:n],
                                  ea_hi[:, g % 2, 0:n].bitcast(f32), ALU.subtract).then_inc(g1["ea_lo"], 1)

            ea_cut(0)
            ea_cut(1)
            cut_to(first + SPL + 1)

            def m_cut(t):
                dve.wait_ge(g1["m_hi"], t + 1)
                dve.scalar_tensor_tensor(out=m_lo[:, t % MSG, :], in0=mp[:, t % SUMS, :], scalar=0.0,
                                         in1=m_hi[:, t % MSG, :].bitcast(f32), op0=ALU.max,
                                         op1=ALU.subtract).then_inc(g1["m_lo"], 1)

            def hot(t):
                if t >= HOT1:
                    dve.wait_ge(g1["sum_ps"], t - HOT1 + 1)
                dve.tensor_scalar(onehot[:, t % HOT1, :], iota_t[:, :], dst_f[:, t:t + 1], None,
                                  ALU.is_equal).then_inc(g1["hot_odd"], 1)

            hot(1)
            for t in range(ET):
                if t % 2 == 0 and 2 <= t < ET - 1:
                    hot(t + 1)
                dve.wait_ge(g1["e_ps"], t + 1)
                dve.wait_ge(gath_in[t % GATH], 16 * (t // GATH + 1))
                if t >= SUMS:
                    dve.wait_ge(g1["m_lo"], t - SUMS + 1)
                dve.tensor_tensor(mp[:, t % SUMS, :], B[2 + t % EBANKS][:, :], gath[:, t % GATH, :], ALU.add)\
                   .then_inc(g1["mp"], 1)
                if t >= 1:
                    m_cut(t - 1)
                if t % GRP == 1 and t // GRP + 1 < NG and t >= GRP:
                    ea_cut(t // GRP + 1)
            m_cut(ET - 1)
            dve.wait_ge(g1["sum_ps"], ET)
            for n in range(NT):
                dve.tensor_copy(S1[:, n, :], B[n][:, :]).then_inc(g1["s1"], 1)
            for n in range(NT):
                dve.wait_ge(g1["aT"], NT)
                dve.tensor_tensor(aT_lo[:, n, :, :], quarters(B[6 + n]),
                                  aT_hi[:, n, :, :].bitcast(f32), ALU.subtract).then_inc(g1["aT"], 1)
            cut_to(first + 2 * SPL - 1)
            for n in range(NT):
                both_tiles(dve, n, g1["agg_ps"], 1, CHUNK[("gnn", "W2")])
                dve.scalar_tensor_tensor(out=agg[:, n, :], in0=b2[:, :], scalar=deg[:, n:n + 1],
                                         in1=B[2 + n][:, :], op0=ALU.mult, op1=ALU.add)\
                   .then_inc(g1["agg"], 1)
            for n in range(NT):
                dve.wait_ge(g1["aT"], 3 * NT)
                dve.tensor_tensor(aT_lo[:, n, :, :], quarters(B[6 + n]),
                                  aT_hi[:, n, :, :].bitcast(f32), ALU.subtract).then_inc(g1["aT"], 1)
            cut_to(first + 2 * SPL)
            for n in range(NT):
                for g in range(2):
                    both_tiles(dve, n, g1["gi_ps"], g + 1, CHUNK[("gnn", "Wih", g)])
                    dve.tensor_tensor(rz[:, n, g, :], B[2 * g + n][:, :], gh[:, n, g, :], ALU.add)\
                       .then_inc(g1["rz_in"], 1)
                    if n == 0 and g == 0:
                        cut_to(first + 2 * SPL + 1)
                dve.wait_ge(g1["rz"], 2 * n + 1)
                dve.wait_ge(g1["gh_sb"], 2 * NT + n + 1)
                link(dve.tensor_tensor(rz[:, n, 0, :], rz[:, n, 0, :], gh[:, n, 2, :], ALU.mult))
                dve.wait_ge(g1["rz"], 2 * n + 2)
                dve.wait_ge(g1["x_base"], n + 1)
                link(dve.tensor_tensor(gh[:, n, 0, :], rz[:, n, 1, :], xn[:, n, :], ALU.mult))
                link(dve.tensor_tensor(gh[:, n, 0, :], gh[:, n, 0, :], g2s[:, :], ALU.mult))
                link(dve.tensor_tensor(x[:, n, :], x[:, n, :], gh[:, n, 0, :], ALU.add))
                link(dve.scalar_tensor_tensor(out=gh[:, n, 1, :], in0=rz[:, n, 1, :], scalar=1.0,
                                              in1=g2s[:, :], op0=ALU.subtract, op1=ALU.mult))
                both_tiles(dve, n, g1["gi_ps"], 3, CHUNK[("gnn", "Wih", 2)])
                dve.tensor_tensor(rz[:, n, 2, :], rz[:, n, 0, :], B[4 + n][:, :], ALU.add)\
                   .then_inc(g1["n_in"], 1)
                dve.wait_ge(g1["n"], n + 1)
                link(dve.tensor_tensor(rz[:, n, 2, :], rz[:, n, 2, :], gh[:, n, 1, :], ALU.mult))
                link(dve.tensor_tensor(x[:, n, :], x[:, n, :], rz[:, n, 2, :], ALU.subtract))
                if n == 0:
                    dve.bn_stats(stats[:, n, :], x[:, n, :])
            dve.drain().then_inc(layer_done, 1)

            gating(2)
            experts(lstm)
            dve.drain().then_inc(layer_done, 1)

        @block.tensor
        def _(pe):
            def mm3(ps, xh, xl, wh, wl, first, last):
                pe.matmul(ps, xh, wh, start=first, stop=False)
                pe.matmul(ps, xh, wl, start=False, stop=False)
                return pe.matmul(ps, xl, wh, start=False, stop=last)

            def product(ps, xh, xl, w, blocks, lo_ready, first, last):
                for k in range(KB):
                    pe.matmul(ps, xh[:, blocks + k, :], whi[w % SPL][:, k, :], start=first and k == 0, stop=False)
                    pe.matmul(ps, xh[:, blocks + k, :], wlo[w % SPL][:, k, :], start=False, stop=False)
                if lo_ready:
                    pe.wait_ge(*lo_ready)
                for k in range(KB):
                    ins = pe.matmul(ps, xl[:, blocks + k, :], whi[w % SPL][:, k, :], start=False,
                                    stop=last and k == KB - 1)
                return ins

            def has_chunk(n):
                pe.wait_ge(lo_cut, n + 1)

            def turn_x(layer):
                for n in range(NT):
                    pe.wait_ge(xn_ok, NT * layer + n + 1)
                    for k in range(KB):
                        ins = pe.transpose(quarters(B[5 - n])[:, k, :], xn[:, n, k * P:(k + 1) * P], ident)
                    ins.then_inc(xt_ps, 1)

            pe.wait_ge(consts_ok, 1)
            turn_x(0)
            pe.wait_ge(hi_cut, 1)
            for n in range(NT):
                pe.wait_ge(g0["xT_hi"], n + 1)
                for k in range(KB):
                    pe.matmul(B[2 + n][:, :], g0_xT_hi[:, n, k, :], whi[0][:, k, :], start=k == 0, stop=False)
            has_chunk(0)
            for n in range(NT):
                pe.wait_ge(xt_sb, n + 1)
                for k in range(KB):
                    pe.matmul(B[2 + n][:, :], g0_xT_hi[:, n, k, :], wlo[0][:, k, :], start=False, stop=False)
                    ins = pe.matmul(B[2 + n][:, :], g0_xT_lo[:, n, k, :], whi[0][:, k, :], start=False,
                                    stop=k == KB - 1)
                ins.then_inc(g0["h_ps"] if n == 0 else chunk_used, 1)
            for t in range(ET):
                pe.wait_ge(g0["hot"], t + 1)
                for n in range(NT):
                    ins = pe.matmul(B[n][:, 0:T], g0_S[:, t % HOT0, n * P:(n + 1) * P], g0_D[:, t % HOT0, :],
                                    start=t == 0, stop=t == ET - 1)
                ins.then_inc(g0["used"], 1)
            pe.wait_ge(g0["cnt"], NT)
            for a in range(NT):
                for b in range(NT):
                    ins = pe.transpose(B[6][:, b * T + a * P:b * T + (a + 1) * P],
                                       g0_cnt[:, a, b * P:(b + 1) * P], ident)
            ins.then_inc(g0["turn_ps"], 1)
            for i in range(3):
                for a, b in ((0, 0), (0, 1), (1, 0), (1, 1)):
                    m, n = (a, b) if i < 2 else (b, a)
                    if i == 0:
                        pe.wait_ge(g0["adj"], m + 1)
                    pe.wait_ge(g0["lo"], NT * i + m + 1)
                    lhs = g0_adj[:, m, n * P:(n + 1) * P]
                    ps = B[diffusion_bank(i, n)]
                    pe.matmul(ps[:, :], lhs, g0_hi[:, m, :], start=m == 0, stop=False)
                    ins = pe.matmul(ps[:, :], lhs, g0_lo[:, m, :], start=False, stop=m == NT - 1)
                    if m == NT - 1:
                        ins.then_inc(g0["ps"], 1)

            def gating(nth):
                turn_x(2 * nth - 1)
                pe.wait_ge(par1, PAR1[0])
                pe.wait_ge(xt_sb, NT * 2 if nth == 1 else 5 * NT)
                if nth == 1:
                    for b in range(2):
                        for k in range(KB):
                            ins = pe.matmul(B[2 + b][:, 0:T].rearrange("p (n t) -> p n t", n=NT),
                                            gw1[:, k, b * P:(b + 1) * P], xnT[:, :, k, :],
                                            start=k == 0, stop=k == KB - 1)
                        ins.then_inc(gate["hid_ps"], 1)
                    pe.wait_ge(gate["hid_sb"], 2)
                for n in range(NT):
                    for k in range(2 if nth == 1 else KB):
                        lhs = hid[:, k, n * P:(n + 1) * P] if nth == 1 else xnT[:, n, k, :]
                        rhs = gw2[:, k, :] if nth == 1 else rw[:, k, :]
                        ins = pe.matmul(B[6][:, n * E:(n + 1) * E], lhs, rhs, start=k == 0,
                                        stop=k == (2 if nth == 1 else KB) - 1)
                ins.then_inc(gate["lg_ps"], 1)
                pe.wait_ge(gate["mask"], nth)
                pe.matmul(B[6][:, 32:32 + E], tri[:, 0:P], mask[:, 0, :], start=True, stop=True)
                pe.matmul(B[6][:, 32 + E:32 + 2 * E], tri[:, P:T], mask[:, 0, :], start=True, stop=False)
                pe.matmul(B[6][:, 32 + E:32 + 2 * E], tri[:, 0:P], mask[:, 1, :], start=False, stop=True)
                pe.matmul(B[6][:, 64:64 + E], tri[:, P:T], mask[:, 0, :], start=True, stop=False)
                pe.matmul(B[6][:, 64:64 + E], tri[:, P:T], mask[:, 1, :], start=False, stop=True)\
                  .then_inc(gate["pos_ps"], 1)

            def turn_comb(nth):
                pe.wait_ge(gate["route"], nth)
                for n in range(NT):
                    ins = pe.matmul(B[7][0:E, n * P:(n + 1) * P], comb[:, n, :], ident, start=True, stop=True)
                ins.then_inc(gate["combT"], 1)

            def biases(nth):
                pe.wait_ge(gate["combT"], 2 * nth)
                for n in range(NT):
                    pe.matmul(B[n][:, :], combT[:, n * P:(n + 1) * P], b_out[:, :], start=True, stop=False,
                              skip_group_check=True)

            def experts(run):
                def gather(e):
                    pe.wait_ge(run.g_built, e + 1)
                    if e >= 1:
                        pe.wait_ge(run.xe_cut, 2 * e)
                        pe.wait_ge(run.gt_sb, e)
                        if e >= 2:
                            pe.wait_ge(run.hT_lo, run.banks_h * (e - 1))
                    for k in range(KB):
                        for n in range(NT):
                            pe.matmul(quarters(B[6])[:, k, :], xn_hi[:, n, k * P:(k + 1) * P],
                                      G[:, e % 2, n, :], start=n == 0, stop=False)
                            ins = pe.matmul(quarters(B[6])[:, k, :], xn_lo[:, n, k * P:(k + 1) * P],
                                            G[:, e % 2, n, :], start=False, stop=n == NT - 1)
                    ins.then_inc(run.gather_ps, 1)
                    for n in range(NT):
                        ins = pe.matmul(B[5][:, n * TURN:(n + 1) * TURN], G[:, e % 2, n, :],
                                        turner[:, n, :], start=True, stop=True)
                    ins.then_inc(run.turn_ps, 1)

                def first_product(e):
                    pe.wait_ge(run.xe_cut, 2 * e + 1)
                    for c in range(run.n_in):
                        if e >= 1 and c == 0:
                            pe.wait_ge(run.h_ok, 2 * e)
                        q = run.chunk("in", e, c)
                        pe.wait_ge(*run.lo(q))
                        rows = sel[:, e, :] if e < E else sel_more[:, e - E, :]
                        product(B[2 + c][:, :], xe_hi, xe_lo, q, 0, (run.xe_cut, 2 * e + 2), True, False)
                        if e == 0 and c == 0:
                            pe.wait_ge(gate["rows"], run.layer + 1)
                        ins = pe.matmul(B[2 + c][:, :], rows, b_rows[:, c * C:(c + 1) * C],
                                        start=False, stop=True)
                        ins.then_inc(run.used(q)[0], 1)

                def weighted_sum(e):
                    pe.wait_ge(run.y_cut, 2 * e + 2)
                    pe.wait_ge(run.gt_sb, e + 1)
                    for n in range(NT):
                        lhs = GT[:, e % 3, n * P:(n + 1) * P]
                        pe.matmul(B[n][:, :], lhs, y_hi[:, :], start=False, stop=False,
                                  skip_group_check=True)
                        ins = pe.matmul(B[n][:, :], lhs, y_lo[:, :], start=False,
                                        stop=e >= E - 1, skip_group_check=True)
                    ins.then_inc(run.sum_ps, 1)

                def second_product(e):
                    pe.wait_ge(run.hT_hi, run.banks_h * (e + 1))
                    if e >= 1:
                        pe.wait_ge(run.y_cut, 2 * e)
                    for c in range(run.n_out):
                        q = run.chunk("out", e, c)
                        pe.wait_ge(*run.lo(q))
                        ins = product(B[7][:, :], hT_hi, hT_lo, q, c * KB, (run.hT_lo, run.banks_h * e + c + 1),
                                      c == 0, c == run.n_out - 1)
                        ins.then_inc(run.used(q)[0], 1)

                def turn_h(e, gathered):
                    pe.wait_ge(run.h_ok, 2 * (e + 1))
                    pe.wait_ge(run.gt_sb, gathered)
                    for b in range(run.banks_h):
                        for k in range(KB):
                            h = act3[:, b if run.layer == 0 else 2, k * P:(k + 1) * P]
                            ins = pe.transpose(quarters(B[5 - b])[:, k, :], h, ident)
                        ins.then_inc(run.hT_ps, 1)

                gather(0)
                turn_comb(run.layer + 1)
                for step in range(E):
                    first_product(step)
                    if step >= 2:
                        weighted_sum(step - 2)
                    if step + 1 < E:
                        gather(step + 1)
                        if step == 0:
                            biases(run.layer + 1)
                    else:
                        pe.wait_ge(gate["more"], run.layer + 1)
                        number = pe.value_load(more_i[run.layer][0:1, 0:1], min_val=0, max_val=MORE)
                        with pe.If(number > 0):
                            gather(E)
                    if step >= 1:
                        second_product(step - 1)
                    if step == E - 1:
                        with pe.If(number > 0):
                            pe.wait_ge(run.gt_sb, E + 1)
                    turn_h(step, min(step + 2, E))
                weighted_sum(E - 2)
                second_product(E - 1)

                def before(followed):
                    if followed:
                        first_product(E)
                    weighted_sum(E - 1)

                def job(e, followed):
                    if followed:
                        gather(e + 1)
                        pe.wait_ge(run.gt_sb, e + 2)
                    turn_h(e, e + 1)
                    second_product(e)
                    if followed:
                        first_product(e + 1)
                    weighted_sum(e)

                further_jobs(pe, number, before, job)

            pe.wait_ge(layer_done, 1)
            gating(1)
            experts(ffn)

            pe.wait_ge(layer_done, 2)
            turn_x(2)
            q = CHUNK[("gnn", "W1")]
            has_chunk(q)
            for n in range(NT):
                pe.wait_ge(xt_sb, 2 * NT + n + 1)
                ins = product(B[2 + n][:, :], g1_xT_hi[:, n, :, :], g1_xT_lo[:, n, :, :], q, 0,
                              (xt_sb, 3 * NT + n + 1), True, True)
                ins.then_inc(g1["a_ps"] if n == 0 else chunk_used, 1)
            pe.wait_ge(g1["gsel"], 1)

            def whh(g, n):
                q = CHUNK[("gnn", "Whh", g)]
                has_chunk(q)
                ps = B[(6, 2, 4)[g] + n]
                if g == 1:
                    pe.wait_ge(g1["a_sb"], n + 1)
                for k in range(KB):
                    mm3(ps[:, :], g1_xT_hi[:, n, k, :], g1_xT_lo[:, n, k, :],
                        whi[q % SPL][:, k, :], wlo[q % SPL][:, k, :], k == 0, False)
                pe.wait_ge(g1["rows"], 2)
                ins = pe.matmul(ps[:, :], gsel[:, 0 if g < 2 else 1, :], gb_rows[:, g * D:(g + 1) * D],
                                start=False, stop=True)
                ins.then_inc(g1["gh_ps"] if n == 0 else chunk_used, 1)

            for g in range(2):
                for n in range(NT):
                    whh(g, n)

            pe.wait_ge(g1["w1e_lo"], 1)

            def edge_product(t):
                g, j = t // GRP, t % GRP
                if j == 0:
                    pe.wait_ge(g1["ea_lo"], g + 1)
                if t >= EBANKS:
                    pe.wait_ge(g1["mp"], t - EBANKS + 1)
                elif t == 0:
                    pe.wait_ge(g1["gh_sb"], 2 * NT)
                mm3(B[2 + t % EBANKS][:, :], ea_hi[:, g % 2, j * P:(j + 1) * P],
                    ea_lo[:, g % 2, j * P:(j + 1) * P], w1e_hi[:, :], w1e_lo[:, :], True, True)\
                    .then_inc(g1["e_ps"], 1)

            def edge_sum(t):
                pe.wait_ge(g1["m_lo"], t + 1)
                pe.wait_ge(g1["hot_odd"] if t % 2 else g1["hot_even"], t // 2 + 1)
                for n in range(NT):
                    lhs = onehot[:, t % HOT1, n * P:(n + 1) * P]
                    pe.matmul(B[n][:, :], lhs, m_hi[:, t % MSG, :], start=t == 0, stop=False)
                    ins = pe.matmul(B[n][:, :], lhs, m_lo[:, t % MSG, :], start=False, stop=t == ET - 1)
                ins.then_inc(g1["sum_ps"], 1)

            for t in range(ET + EAHEAD):
                if t < ET:
                    edge_product(t)
                if t >= EAHEAD:
                    edge_sum(t - EAHEAD)
            pe.wait_ge(g1["mp"], ET)
            whh(2, 0)
            for n in range(NT):
                pe.wait_ge(g1["s1"], n + 1)
                for k in range(KB):
                    ins = pe.transpose(quarters(B[6 + n])[:, k, :], S1[:, n, k * P:(k + 1) * P], ident)
                ins.then_inc(g1["s1T_ps"], 1)
            whh(2, 1)
            q = CHUNK[("gnn", "W2")]
            has_chunk(q)
            for n in range(NT):
                pe.wait_ge(g1["aT"], NT)
                ins = product(B[2 + n][:, :], aT_hi[:, n, :, :], aT_lo[:, n, :, :], q, 0,
                              (g1["aT"], NT + n + 1), True, True)
                ins.then_inc(g1["agg_ps"] if n == 0 else chunk_used, 1)
            for n in range(NT):
                pe.wait_ge(g1["agg"], n + 1)
                for k in range(KB):
                    ins = pe.transpose(quarters(B[6 + n])[:, k, :], agg[:, n, k * P:(k + 1) * P], ident)
                ins.then_inc(g1["aggT_ps"], 1)
            pe.wait_ge(g1["aT"], 4 * NT)
            for n in range(NT):
                for g in range(3):
                    q = CHUNK[("gnn", "Wih", g)]
                    has_chunk(q)
                    ps = B[2 * g + n]
                    if g == 2:
                        pe.wait_ge(g1["gh_sb"], 2 * NT + n + 1)
                        pe.matmul(ps[:, :], gsel[:, 2, :], gb_rows[:, g * D:(g + 1) * D], start=True, stop=False)
                    for k in range(KB):
                        ins = mm3(ps[:, :], aT_hi[:, n, k, :], aT_lo[:, n, k, :],
                                  whi[q % SPL][:, k, :], wlo[q % SPL][:, k, :], g < 2 and k == 0, k == KB - 1)
                    ins.then_inc(g1["gi_ps"] if n == 0 else chunk_used, 1)

            pe.wait_ge(layer_done, 3)
            gating(2)
            experts(lstm)


def kernel(**inputs):
    import numpy as _np
    import concourse.bacc as _bacc
    from concourse import mybir as _mybir
    from concourse.bass_utils import run_bass_kernel_spmd as _run

    a = {k: _np.asarray(v) for k, v in inputs.items()}

    W1T, W2T, WihT, WhhT = (a["L1_gnn_" + n].T for n in ("W1", "W2", "W_ih", "W_hh"))

    def block(w, r, c):
        return w[r * C:(r + 1) * C, c * C:(c + 1) * C]

    def matrix(key):
        kind = key[0]
        if kind == "L0":
            return a["L0_gnn_W"]
        if kind == "ffn":
            return block(a["L0_ffn_we1"][key[2]], 0, key[3]) if key[1] == "in" else \
                block(a["L0_ffn_we2"][key[2]], key[3], 0)
        if kind == "lstm":
            return block(a["L1_ffn_Wi"][key[2]], 0, (0, 2, 3)[key[3]]) if key[1] == "in" else \
                a["L1_ffn_Wo"][key[2]]
        if key[1] == "W1":
            return W1T[0:D, :]
        if key[1] == "W2":
            return W2T
        return block(WhhT if key[1] == "Whh" else WihT, 0, key[2])

    b = a["L1_ffn_b"]
    arrays = {
        "x": a["x"],
        "src": a["src"].reshape(ET, P).T,
        "dst": a["dst"].reshape(ET, P).T,
        "ea": a["edge_attr_128"].T,
        "w1e": W1T[D:, :],
        "weights": _np.stack([matrix(k).reshape(KB, P, C).transpose(1, 0, 2) for k in STORE]),
        "L0_ffn_gb1": a["L0_ffn_gb1"].reshape(2, P).T,
        "lstm_b": _np.concatenate([b[:, 0:D], b[:, 2 * D:3 * D], b[:, 3 * D:4 * D]], axis=1),
        "L1_gnn_b_ih": a["L1_gnn_b_ih"].reshape(1, 3 * D),
        "L1_gnn_b_hh": a["L1_gnn_b_hh"].reshape(1, 3 * D),
    }
    for n in ("L0_gnn_b", "L0_gnn_diffusion_weights", "L0_ffn_gw1", "L0_ffn_gw2", "L0_ffn_gb2",
              "L0_ffn_be1", "L0_ffn_be2", "L1_gnn_b1", "L1_gnn_b2", "L1_gnn_gamma", "L1_gnn_beta",
              "L1_gnn_run_mean", "L1_gnn_run_var", "L1_ffn_router_w", "L1_ffn_router_b", "L1_ffn_bo"):
        arrays[n] = a[n]
    arrays = {f"in_{n}_dram": _np.ascontiguousarray(v) for n, v in arrays.items()}

    nc = _bacc.Bacc("TRN2", target_bir_lowering=False, num_devices=1)
    aps = {n[3:-5]: nc.dram_tensor(n, v.shape, _mybir.dt.from_np(v.dtype), kind="ExternalInput").ap()
           for n, v in arrays.items()}
    out = nc.dram_tensor("out_0_dram", (T, D), _mybir.dt.float32, kind="ExternalOutput").ap()
    node_rows = nc.dram_tensor("node_rows", (T, D), _mybir.dt.float32).ap()
    build(nc, aps, out, node_rows)
    r = _run(nc, [arrays], core_ids=[0])
    return r.results[0]["out_0_dram"]
```
